# Optimizing a Trainium2 kernel written in Bass

```python
import numpy as np
import jax
import jax.numpy as jnp

def _softmax(x, axis=-1):
    return jax.nn.softmax(x, axis=axis)

def _gelu(x):
    return jax.nn.gelu(x, approximate=True)

def _silu(x):
    return jax.nn.silu(x)

def _sigmoid(x):
    return jax.nn.sigmoid(x)

def _layernorm(x, axis=-1, eps=1e-05):
    m = jnp.mean(x, axis=axis, keepdims=True)
    v = jnp.var(x, axis=axis, keepdims=True)
    return (x - m) / jnp.sqrt(v + eps)

def _scatter_add(tgt, idx, src, axis=0):
    return tgt.at[idx].add(src)

def _segment_sum(src, seg, n):
    return jax.ops.segment_sum(src, seg, n)
kernel_name = 'mk_adj_resnorm_d4_adj_r2_34f323'

def setup_inputs(seed: int=0):
    np.random.seed(seed)
    _w = jnp.asarray

    def _rec_inputs():
        import jax
        import jax.numpy as jnp
        _gk = jax.random.key(seed)
        x = -0.003407 + 1.001 * jax.random.normal(jax.random.fold_in(_gk, 1), (2048, 128), jnp.float32)
        _w = (1.0 + jnp.arange(2048, dtype=jnp.float32)) ** (-0.5)
        _w = _w / _w.mean()
        _pij = jnp.clip(0.00195312 * _w[:, None] * _w[None, :], 0.0, 1.0)
        _a = jax.random.uniform(jax.random.fold_in(_gk, 2), (2048, 2048)) < _pij
        _a = jnp.logical_or(_a, jnp.swapaxes(_a, -1, -2))
        _a = jnp.logical_or(_a, jnp.eye(2048, dtype=bool))
        _af = _a.astype(jnp.float32)
        _af = _af * jax.random.uniform(jax.random.fold_in(_gk, 3), (2048, 2048), jnp.float32, 0.05, 1)
        adj = _af
        return (x, adj)
    x, adj = _rec_inputs()

    def _L0_gnn_setup():
        import jax, jax.numpy as jnp
        import numpy as np
        LN_EPS = 1e-05
        key = jax.random.key(seed)
        ks = jax.random.split(key, 6)
        N, D = (512, 128)
        return {'node_feats': jax.random.normal(ks[0], (N, D), dtype=jnp.float32), 'adj': jax.random.uniform(ks[1], (N, N), dtype=jnp.float32), 'msg_w': jax.random.normal(ks[2], (D, 2 * D), dtype=jnp.float32) * 0.05, 'msg_b': jax.random.normal(ks[3], (D,), dtype=jnp.float32) * 0.05, 'upd_w': jax.random.normal(ks[4], (D, 2 * D), dtype=jnp.float32) * 0.05, 'upd_b': jax.random.normal(ks[5], (D,), dtype=jnp.float32) * 0.05, 'ln_w': jnp.ones((D,), dtype=jnp.float32), 'ln_b': jnp.zeros((D,), dtype=jnp.float32)}
    _L0_gnn_all = _L0_gnn_setup()
    _L0_gnn_in = {k: v for k, v in _L0_gnn_all.items() if k in ('msg_w', 'msg_b', 'upd_w', 'upd_b', 'ln_w', 'ln_b')}
    del _L0_gnn_all

    def _L1_gnn_setup():
        import jax, jax.numpy as jnp
        import numpy as np
        K = 5
        TAU = 0.5
        N = 4096
        IN_DIM = 128
        OUT_DIM = 128

        def _cheb_coeff(k_order: int, tau: float) -> jnp.ndarray:
            ks = jnp.arange(k_order, dtype=jnp.float32)
            x_k = jnp.cos(jnp.pi * (ks + 0.5) / k_order)
            return 2.0 / k_order * jnp.exp(-tau * x_k)
        key = jax.random.key(seed)
        k1, k2, k3 = jax.random.split(key, 3)
        x = jax.random.normal(k1, (N, IN_DIM), dtype=jnp.float32)
        laplacian = jax.random.normal(k2, (N, N), dtype=jnp.float32) / np.sqrt(N)
        limit = np.sqrt(6.0 / (IN_DIM + OUT_DIM))
        theta = jax.random.uniform(k3, (K, IN_DIM, OUT_DIM), dtype=jnp.float32, minval=-limit, maxval=limit)
        return {'x': x, 'laplacian': laplacian, 'theta': theta}
    _L1_gnn_all = _L1_gnn_setup()
    _L1_gnn_in = {k: v for k, v in _L1_gnn_all.items() if k in ('theta',)}
    del _L1_gnn_all

    def _L2_gnn_setup():
        import jax, jax.numpy as jnp
        import numpy as np
        N, DIM = (8192, 128)

        def _gru_cell(x, h, W_ih, W_hh, b_ih, b_hh):
            gi = x @ W_ih.T + b_ih
            gh = h @ W_hh.T + b_hh
            i_r, i_z, i_n = jnp.split(gi, 3, axis=-1)
            h_r, h_z, h_n = jnp.split(gh, 3, axis=-1)
            r = jax.nn.sigmoid(i_r + h_r)
            z = jax.nn.sigmoid(i_z + h_z)
            n = jnp.tanh(i_n + r * h_n)
            return (1.0 - z) * n + z * h
        key = jax.random.key(seed)
        ks = jax.random.split(key, 8)
        states = jax.random.normal(ks[0], (N, DIM), dtype=jnp.float32)
        adj = jax.random.uniform(ks[1], (N, N), dtype=jnp.float32)
        s = 1.0 / np.sqrt(DIM)
        W_msg = jax.random.uniform(ks[2], (DIM, DIM), minval=-s, maxval=s, dtype=jnp.float32)
        b_msg = jax.random.uniform(ks[3], (DIM,), minval=-s, maxval=s, dtype=jnp.float32)
        W_ih = jax.random.uniform(ks[4], (3 * DIM, DIM), minval=-s, maxval=s, dtype=jnp.float32)
        W_hh = jax.random.uniform(ks[5], (3 * DIM, DIM), minval=-s, maxval=s, dtype=jnp.float32)
        b_ih = jax.random.uniform(ks[6], (3 * DIM,), minval=-s, maxval=s, dtype=jnp.float32)
        b_hh = jax.random.uniform(ks[7], (3 * DIM,), minval=-s, maxval=s, dtype=jnp.float32)
        return {'states': states, 'adj': adj, 'W_msg': W_msg, 'b_msg': b_msg, 'W_ih': W_ih, 'W_hh': W_hh, 'b_ih': b_ih, 'b_hh': b_hh}
    _L2_gnn_all = _L2_gnn_setup()
    _L2_gnn_in = {k: v for k, v in _L2_gnn_all.items() if k in ('W_msg', 'b_msg', 'W_ih', 'W_hh', 'b_ih', 'b_hh')}
    del _L2_gnn_all

    def _L3_gnn_setup():
        import jax, jax.numpy as jnp
        import numpy as np
        N, IN, H, C = (2048, 128, 4, 32)
        HC = H * C
        EDGE_P = 0.008

        def _linear_params(key, fan_in, fan_out, bias=True):
            k1, k2 = jax.random.split(key)
            lim = 1.0 / np.sqrt(fan_in)
            W = jax.random.uniform(k1, (fan_in, fan_out), jnp.float32, -lim, lim)
            if not bias:
                return W
            b = jax.random.uniform(k2, (fan_out,), jnp.float32, -lim, lim)
            return (W, b)

        def _transformer_conv(x, adj, Wq, bq, Wk, bk, Wv, bv, Ws, bs, Wb):
            n = x.shape[0]
            q = (x @ Wq + bq).reshape(n, H, C)
            k = (x @ Wk + bk).reshape(n, H, C)
            v = (x @ Wv + bv).reshape(n, H, C)
            attn = jnp.einsum('nhc,mhc->hnm', q, k) / np.float32(np.sqrt(C))
            mask = adj == 0.0
            neg = jnp.where(mask[None], -jnp.inf, attn)
            m = jnp.max(neg, axis=-1, keepdims=True)
            all_inf = jnp.isneginf(m)
            e = jnp.where(mask[None], 0.0, jnp.exp(neg - jnp.where(all_inf, 0.0, m)))
            denom = jnp.sum(e, axis=-1, keepdims=True)
            alpha = e / jnp.where(denom == 0.0, 1.0, denom)
            out = jnp.einsum('hnm,mhc->hnc', alpha, v)
            out = jnp.transpose(out, (1, 2, 0)).reshape(n, C * H)
            x_r = x @ Ws + bs
            beta = jax.nn.sigmoid(jnp.concatenate([out, x_r, out - x_r], axis=-1) @ Wb)
            return beta * x_r + (1.0 - beta) * out
        key = jax.random.key(seed)
        ks = jax.random.split(key, 7)
        x = jax.random.normal(ks[0], (N, IN), jnp.float32)
        adj = (jax.random.uniform(ks[1], (N, N)) < EDGE_P).astype(jnp.float32)
        Wq, bq = _linear_params(ks[2], IN, HC)
        Wk, bk = _linear_params(ks[3], IN, HC)
        Wv, bv = _linear_params(ks[4], IN, HC)
        Ws, bs = _linear_params(ks[5], IN, HC)
        Wb = _linear_params(ks[6], 3 * HC, 1, bias=False)
        return dict(x=x, adj=adj, Wq=Wq, bq=bq, Wk=Wk, bk=bk, Wv=Wv, bv=bv, Ws=Ws, bs=bs, Wb=Wb)
    _L3_gnn_all = _L3_gnn_setup()
    _L3_gnn_in = {k: v for k, v in _L3_gnn_all.items() if k in ('Wq', 'bq', 'Wk', 'bk', 'Wv', 'bv', 'Ws', 'bs', 'Wb')}
    del _L3_gnn_all
    return {'x': x, 'adj': adj, 'L0_gnn_msg_w': _L0_gnn_in['msg_w'], 'L0_gnn_msg_b': _L0_gnn_in['msg_b'], 'L0_gnn_upd_w': _L0_gnn_in['upd_w'], 'L0_gnn_upd_b': _L0_gnn_in['upd_b'], 'L0_gnn_ln_w': _L0_gnn_in['ln_w'], 'L0_gnn_ln_b': _L0_gnn_in['ln_b'], 'L1_gnn_theta': _L1_gnn_in['theta'], 'L2_gnn_W_msg': _L2_gnn_in['W_msg'], 'L2_gnn_b_msg': _L2_gnn_in['b_msg'], 'L2_gnn_W_ih': _L2_gnn_in['W_ih'], 'L2_gnn_W_hh': _L2_gnn_in['W_hh'], 'L2_gnn_b_ih': _L2_gnn_in['b_ih'], 'L2_gnn_b_hh': _L2_gnn_in['b_hh'], 'L3_gnn_Wq': _L3_gnn_in['Wq'], 'L3_gnn_bq': _L3_gnn_in['bq'], 'L3_gnn_Wk': _L3_gnn_in['Wk'], 'L3_gnn_bk': _L3_gnn_in['bk'], 'L3_gnn_Wv': _L3_gnn_in['Wv'], 'L3_gnn_bv': _L3_gnn_in['bv'], 'L3_gnn_Ws': _L3_gnn_in['Ws'], 'L3_gnn_bs': _L3_gnn_in['bs'], 'L3_gnn_Wb': _L3_gnn_in['Wb']}

def reference(x, adj, L0_gnn_msg_w, L0_gnn_msg_b, L0_gnn_upd_w, L0_gnn_upd_b, L0_gnn_ln_w, L0_gnn_ln_b, L1_gnn_theta, L2_gnn_W_msg, L2_gnn_b_msg, L2_gnn_W_ih, L2_gnn_W_hh, L2_gnn_b_ih, L2_gnn_b_hh, L3_gnn_Wq, L3_gnn_bq, L3_gnn_Wk, L3_gnn_bk, L3_gnn_Wv, L3_gnn_bv, L3_gnn_Ws, L3_gnn_bs, L3_gnn_Wb):
    import jax
    import jax.numpy as jnp

    def _L0_gnn_ref(node_feats, adj, msg_w, msg_b, upd_w, upd_b, ln_w, ln_b):
        import jax, jax.numpy as jnp
        import numpy as np
        LN_EPS = 1e-05
        D = node_feats.shape[-1]
        s = node_feats @ msg_w[:, :D].T
        d = node_feats @ msg_w[:, D:].T
        messages = jax.nn.gelu(s[:, None, :] + d[None, :, :] + msg_b, approximate=False)
        aggregated = jnp.einsum('ijd,ij->id', messages, adj)
        combined = jnp.concatenate([node_feats, aggregated], axis=-1)
        new_feats = combined @ upd_w.T + upd_b
        h = jax.nn.gelu(new_feats, approximate=False) + node_feats
        mu = jnp.mean(h, axis=-1, keepdims=True)
        var = jnp.var(h, axis=-1, keepdims=True)
        return (h - mu) / jnp.sqrt(var + LN_EPS) * ln_w + ln_b

    def _L1_gnn_ref(x, laplacian, theta):
        import jax, jax.numpy as jnp
        import numpy as np
        K = 5
        TAU = 0.5
        N = 4096
        IN_DIM = 128
        OUT_DIM = 128

        def _cheb_coeff(k_order: int, tau: float) -> jnp.ndarray:
            ks = jnp.arange(k_order, dtype=jnp.float32)
            x_k = jnp.cos(jnp.pi * (ks + 0.5) / k_order)
            return 2.0 / k_order * jnp.exp(-tau * x_k)
        coeff = _cheb_coeff(K, TAU)
        tx_prev, tx_curr = (x, laplacian @ x)
        tx_list = [tx_prev, tx_curr]
        for _ in range(2, K):
            tx_next = 2.0 * (laplacian @ tx_curr) - tx_prev
            tx_list.append(tx_next)
            tx_prev, tx_curr = (tx_curr, tx_next)
        tx_stack = jnp.stack(tx_list, axis=0)
        return jnp.einsum('kni,kio,k->no', tx_stack, theta, coeff)

    def _L2_gnn_ref(states, adj, W_msg, b_msg, W_ih, W_hh, b_ih, b_hh):
        import jax, jax.numpy as jnp
        import numpy as np
        N, DIM = (8192, 128)

        def _gru_cell(x, h, W_ih, W_hh, b_ih, b_hh):
            gi = x @ W_ih.T + b_ih
            gh = h @ W_hh.T + b_hh
            i_r, i_z, i_n = jnp.split(gi, 3, axis=-1)
            h_r, h_z, h_n = jnp.split(gh, 3, axis=-1)
            r = jax.nn.sigmoid(i_r + h_r)
            z = jax.nn.sigmoid(i_z + h_z)
            n = jnp.tanh(i_n + r * h_n)
            return (1.0 - z) * n + z * h
        agg = adj @ states
        msg = jax.nn.relu(agg @ W_msg.T + b_msg)
        return _gru_cell(msg, states, W_ih, W_hh, b_ih, b_hh)

    def _L3_gnn_ref(x, adj, Wq, bq, Wk, bk, Wv, bv, Ws, bs, Wb):
        import jax, jax.numpy as jnp
        import numpy as np
        N, IN, H, C = (2048, 128, 4, 32)
        HC = H * C
        EDGE_P = 0.008

        def _linear_params(key, fan_in, fan_out, bias=True):
            k1, k2 = jax.random.split(key)
            lim = 1.0 / np.sqrt(fan_in)
            W = jax.random.uniform(k1, (fan_in, fan_out), jnp.float32, -lim, lim)
            if not bias:
                return W
            b = jax.random.uniform(k2, (fan_out,), jnp.float32, -lim, lim)
            return (W, b)

        def _transformer_conv(x, adj, Wq, bq, Wk, bk, Wv, bv, Ws, bs, Wb):
            n = x.shape[0]
            q = (x @ Wq + bq).reshape(n, H, C)
            k = (x @ Wk + bk).reshape(n, H, C)
            v = (x @ Wv + bv).reshape(n, H, C)
            attn = jnp.einsum('nhc,mhc->hnm', q, k) / np.float32(np.sqrt(C))
            mask = adj == 0.0
            neg = jnp.where(mask[None], -jnp.inf, attn)
            m = jnp.max(neg, axis=-1, keepdims=True)
            all_inf = jnp.isneginf(m)
            e = jnp.where(mask[None], 0.0, jnp.exp(neg - jnp.where(all_inf, 0.0, m)))
            denom = jnp.sum(e, axis=-1, keepdims=True)
            alpha = e / jnp.where(denom == 0.0, 1.0, denom)
            out = jnp.einsum('hnm,mhc->hnc', alpha, v)
            out = jnp.transpose(out, (1, 2, 0)).reshape(n, C * H)
            x_r = x @ Ws + bs
            beta = jax.nn.sigmoid(jnp.concatenate([out, x_r, out - x_r], axis=-1) @ Wb)
            return beta * x_r + (1.0 - beta) * out
        return _transformer_conv(x, adj, Wq, bq, Wk, bk, Wv, bv, Ws, bs, Wb)
    x = _layernorm(x + _L0_gnn_ref(x, adj, L0_gnn_msg_w, L0_gnn_msg_b, L0_gnn_upd_w, L0_gnn_upd_b, L0_gnn_ln_w, L0_gnn_ln_b), axis=-1)
    x = _layernorm(x + _L1_gnn_ref(x, adj, L1_gnn_theta), axis=-1)
    x = _layernorm(x + _L2_gnn_ref(x, adj, L2_gnn_W_msg, L2_gnn_b_msg, L2_gnn_W_ih, L2_gnn_W_hh, L2_gnn_b_ih, L2_gnn_b_hh), axis=-1)
    x = _layernorm(x + _L3_gnn_ref(x, adj, L3_gnn_Wq, L3_gnn_bq, L3_gnn_Wk, L3_gnn_bk, L3_gnn_Wv, L3_gnn_bv, L3_gnn_Ws, L3_gnn_bs, L3_gnn_Wb), axis=-1)
    return x

_drawn_inputs = setup_inputs


def setup_inputs(seed=0):
    import zlib

    import numpy as np

    out = dict(_drawn_inputs(seed))
    spreads = {'L0_gnn_ln_w': (1.0, 0.2), 'L0_gnn_ln_b': (0.0, 0.1)}
    factors = {'L2_gnn_b_msg': 8.0,
     'L2_gnn_b_ih': 3.796,
     'L2_gnn_b_hh': 5.645,
     'L3_gnn_Wq': 8.0,
     'L3_gnn_bq': 8.0,
     'L3_gnn_Wk': 8.0,
     'L3_gnn_bk': 8.0,
     'L3_gnn_bv': 3.824}
    for name, (base, spread) in spreads.items():
        noise = np.random.default_rng([zlib.crc32(name.encode()), seed]).standard_normal(out[name].shape)
        drawn = base * np.exp(spread * noise) if base else spread * noise
        out[name] = jnp.asarray(drawn.astype(out[name].dtype))
    for name, factor in factors.items():
        out[name] = (out[name] * factor).astype(out[name].dtype)
    return out
```

```python
import math
import concourse.bass as bass
from concourse import mybir
from contextlib import ExitStack

N, D, PT, BANK = 2048, 128, 128, 512
NT = N // PT
NQ = N // BANK
TPQ = BANK // PT
H, C = 4, 32
CHEB = 5
TAU = 0.5
LN_EPS = 1e-5
SCALE = 1.0 / math.sqrt(C)
ORDER = [1, 0] + list(range(2, NT))
UNIT = 4
SLOTS = {0: 32, 1: 20, 2: 20, 3: 16, 4: 16, 5: 16}
UNITS = [SLOTS.get(t, 12) // UNIT for t in ORDER]
ALL_UNITS = sum(UNITS)
SEG = 256
NSEG = N // SEG
CAND = 8 * NSEG
RING = 4
MASKED = -1.0e30
FLOOR = -1.0e20


def cheb_coeff(k):
    return 2.0 / CHEB * math.exp(-TAU * math.cos(math.pi * (k + 0.5) / CHEB))


class Tally:

    def __init__(self, semaphore):
        self.semaphore, self.count = semaphore, 0

    def step(self, instruction):
        instruction.then_inc(self.semaphore, 1)
        self.count += 1
        return self.count


def graph_network(nc, x, adj, msg_w, msg_b, upd_w, upd_b, ln_w, ln_b, theta, w_msg, b_msg, w_ih, w_hh, b_ih, b_hh,
                  wq, bq, wk, bk, wv, bv, ws, bs, wb, out, d_rows):
    fp32 = mybir.dt.float32
    fp32r = mybir.dt.float32r
    bf16 = mybir.dt.bfloat16
    i32 = mybir.dt.int32
    u32 = mybir.dt.uint32
    ALU = mybir.AluOpType
    ACT = mybir.ActivationFunctionType
    ds = bass.ds

    ctx = ExitStack()
    with ctx:
        def sb(name, shape, dt=fp32):
            return ctx.enter_context(nc.sbuf_tensor(name, shape, dt))

        def sem(name):
            return ctx.enter_context(nc.semaphore(name))

        ident = sb("ident", [PT, PT + 4])
        eye = ident[:, 0:PT]
        psum = ctx.enter_context(nc.psum_tensor("psum", [PT, 8, BANK], fp32))
        cols = sb("cols", [PT, 12])
        msgb_col, updb_col, bmsg_col = cols[:, 0:1], cols[:, 1:2], cols[:, 2:3]
        bih_cols, bhh_cols, brz_cols = cols[:, 3:6], cols[:, 6:9], cols[:, 9:11]
        iota_r = sb("iota_r", [PT, PT])
        rowid = sb("rowid", [PT, NT])
        flags = sb("flags", [PT, NT])
        seg_base = sb("seg_base", [PT, NSEG, 8])
        cand_val = sb("cand_val", [PT, CAND])
        cand_pos = sb("cand_pos", [PT, CAND], u32)
        cand_key = sb("cand_key", [PT, CAND])
        cand_left = sb("cand_left", [PT, CAND])
        picked = sb("picked", [PT, 32])
        scrap = sb("scrap", [PT, 32])
        edge_count = sb("edge_count", [PT, 2])
        keep = sb("keep", [PT, 1])
        weight = sb("weight", [PT, 3, 32])
        column = sb("column", [PT, 3, 32], i32)
        pos = sb("pos", [PT, NT])
        loop_counts = sb("loop_counts", [PT, NT + 1], i32)
        rows_i = sb("rows_i", [PT, 1], i32)
        diag = sb("diag", [PT, 2, UNIT, PT])
        stats = diag[:, 0, 0, 0:6 * NT].rearrange("p (t c) -> p t c", c=6)
        moments = diag[:, 0, 1, 0:2 * NT].rearrange("p (t c) -> p t c", c=2)
        rstd = diag[:, 0, 2, 0:NT]
        pool = sb("pool", [PT, 9, N])
        pool_end = ctx.enter_context(ExitStack())
        adjT = pool_end.enter_context(nc.sbuf_tensor("adjT", [PT, NT, N], fp32))
        pool_end.close()
        qs = sb("q_stack", [PT, H, N], fp32r)
        ks = sb("k_stack", [PT, H, N], fp32r)
        masked = sb("masked_scores", [PT, 2, N])
        adj_again = sb("adj_again", [PT, 2, N])
        turned_sb = sb("turned_probs", [PT, H, N])

        def as_rows(ap):
            return ap.rearrange("p (t d) -> p t d", t=NT)

        def slot(k):
            return pool[:, k, :]

        xT, dT, s_rows, aggT, aggD = slot(0), slot(1), as_rows(slot(2)), slot(3), slot(4)
        x_rows, d_stage = as_rows(slot(3)), as_rows(slot(4))
        adj_in = pool[:, 5:7, :]
        adj_sel, sel_hot, pick_hot = slot(5), as_rows(slot(5)), as_rows(slot(6))
        msgs = slot(7)
        total, loop_f = slot(7)[:, 0:2 * NT], slot(7)[:, 2 * NT:5 * NT]
        msgw_in, wT, msgb_rows = slot(7)[:, 0:256], slot(7)[:, 256:512], slot(7)[:, 512:640]
        prefix_tri, ones_sq = slot(4)[:, 0:128], slot(4)[:, 128:256]
        gath = slot(8).rearrange("p (r k d) -> p r k d", r=RING, k=UNIT)
        agg_sel, half_sum = slot(8)[:, 0:PT], slot(8)[:, PT:PT + 4].rearrange("p (k h) -> p k h", k=2)
        sT_sel, agg_selr = slot(8)[:, 256:384], slot(8)[:, 384:512]
        updw_in, uT = slot(7)[:, 0:256], slot(7)[:, 256:512]
        lnw_rows, lnb_rows = slot(7)[:, 512:640], slot(7)[:, 640:768]
        newT, h_rows, x_again, x1_rows = slot(1), as_rows(slot(2)), as_rows(slot(5)), as_rows(slot(6))
        termT = [slot(0), slot(1), slot(2), slot(0), slot(1)]
        term_rows = [x1_rows, as_rows(slot(3)), as_rows(slot(4)), as_rows(slot(3))]
        theta_in = slot(7)[:, 768:768 + CHEB * PT].rearrange("p (k o) -> p k o", k=CHEB)
        y_rows, x2_rows = as_rows(slot(5)), as_rows(slot(3))
        x2T = slot(0)
        gw_in = slot(8)[:, 0:7 * PT].rearrange("p (g f) -> p g f", g=7)
        gwT = slot(8)[:, 7 * PT:14 * PT].rearrange("p (g f) -> p g f", g=7)
        agg_c, msg_c, r_c, z_c = [slot(1)[:, BANK * i:BANK * i + BANK] for i in range(4)]
        n_c, t_c, u_c, _ = [slot(2)[:, BANK * i:BANK * i + BANK] for i in range(4)]
        u_rows, x3_rows = as_rows(slot(4)), as_rows(slot(5))
        x3T, v_rows, xr_rows, o_rows = slot(0), as_rows(slot(1)), as_rows(slot(2)), as_rows(slot(3))
        w_rep = slot(6)[:, 0:1024].rearrange("p (i h m) -> p i h m", i=2, h=H)
        attw = slot(8)[:, 0:512]
        bvs_rows, wb_rows = slot(8)[:, 512:768], slot(8)[:, 768:1152]
        wb_out, wb_skip = slot(8)[:, 1152:1280], slot(8)[:, 1280:1408]
        turned = [as_rows(turned_sb[:, h, :]) for h in range(H)] + [as_rows(slot(k)) for k in (4, 6, 7, 0)]
        avT, gate_scrap = slot(8)[:, 1408:1536], slot(8)[:, 1536:1664]
        qk_cols = slot(8)[:, 1664:1672]
        row_max = slot(8)[:, 1672:1688].rearrange("p (a b) -> p a b", b=4)
        den = slot(8)[:, 1688:1752].rearrange("p (t h) -> p t h", h=H)
        rden = slot(8)[:, 1752:1760].rearrange("p (a h) -> p a h", h=H)
        skip_dot = slot(8)[:, 1760:1776]
        gate = slot(8)[:, 1776:1792].rearrange("p (a b) -> p a b", b=8)

        s_w, s_x, s_const, s_const2 = sem("message_weights"), sem("x_loaded"), sem("constants"), sem("prefix_consts")
        s_adj = [sem(f"adj_loaded{i}") for i in range(2)]
        s_dve, s_act, s_pool = sem("vector_step"), sem("scalar_step"), sem("gpsimd_step")
        s_xtp, s_xt = sem("x_turned"), sem("x_turned_copied")
        s_sdp, s_sdA, s_sdV, s_dstore = sem("sd_product"), sem("s_copied"), sem("d_copied"), sem("d_rows_stored")
        s_dtp, s_dt = sem("dT_product"), sem("dT_copied")
        s_tp, s_tpc = sem("adj_turned"), sem("adj_turned_copied")
        s_ext = sem("neighbours_extracted")
        s_gath = [sem(f"gathered{i}") for i in range(RING)]
        s_add, s_gelu, s_diag, s_unit, s_aggc = sem("s_added"), sem("unit_gelu"), sem("diag_made"), sem("unit_summed"), sem("agg_tile_copied")
        s_flagp, s_counts = sem("flag_prefix"), sem("loop_counts_ready")
        s_hot, s_pickp, s_picki, s_asel = sem("pick_hot"), sem("picked_product"), sem("picked_ready"), sem("adj_rows_gathered")
        s_sel, s_bc, s_mg, s_half = sem("selector"), sem("adj_half_broadcast"), sem("dense_half_gelu"), sem("dense_half_reduced")
        s_dsum, s_dtr, s_dcp, s_dout, s_dacc = sem("dense_sum"), sem("dense_turned"), sem("dense_turned_copied"), sem("dense_scattered"), sem("dense_accumulated")
        s_dense, s_zero, s_iota, s_stsel, s_hc, s_held = sem("dense_done"), sem("sums_cleared"), sem("iota_moved"), sem("picked_s"), sem("h_copied"), sem("waits_held")
        s_w2, s_utp, s_ut = sem("update_weights"), sem("upd_w_turned"), sem("upd_w_copied")
        s_newp, s_newg, s_newx = sem("new_feats_product"), sem("new_feats_gelu"), sem("new_feats_plus_x")
        s_rowp = sem("h_turned")
        s_ln, s_ln2 = sem("layernorm_variance"), sem("layernorm_sqrt")
        s_x1, s_x2, s_x3 = sem("x1_ready"), sem("x2_ready"), sem("x3_ready")
        s_tnp, s_tnc = sem("turned_psum"), sem("turned_copied")
        s_th, s_ths = sem("theta_loaded"), sem("theta_scaled")
        s_hopp, s_hopc, s_chp = sem("hop_product"), sem("hop_copied"), sem("cheb_sum")
        s_gwl, s_gwp, s_gwc, s_gb = sem("gru_weights"), sem("gru_weights_turned"), sem("gru_weights_copied"), sem("gru_bias")
        s_agg2p, s_agg2, s_msgp, s_msg = sem("agg2_product"), sem("agg2_copied"), sem("msg_product"), sem("msg_ready")
        s_gate, s_gact, s_pre, s_tanh, s_cell = sem("gates_product"), sem("gates_ready"), sem("candidate_sum"), sem("candidate_ready"), sem("cell_ready")
        s_utn, s_utc = sem("u_turned"), sem("u_turned_copied")
        s_rep, s_aw, s_prp, s_hi, s_lo = sem("weights_repeated"), sem("att_weights"), sem("projection"), sem("stack_high"), sem("stack_low")
        s_vp, s_vc, s_wbs = sem("value_product"), sem("value_copied"), sem("gate_weights")
        s_adj2 = [sem(f"adj_again{i}") for i in range(2)]
        s_pen, s_scp, s_mask, s_bias, s_exp = sem("penalty"), sem("scores"), sem("masked_half"), sem("exp_bias"), sem("exp_done")
        s_etp, s_etA, s_etV = sem("probs_turned"), sem("turned_by_scalar"), sem("turned_by_vector")
        s_avp, s_avc, s_avt, s_o = sem("av_product"), sem("av_copied"), sem("av_turned"), sem("out_rows")
        s_gz, s_ge, s_gd = sem("gate_dot"), sem("gate_exp"), sem("gated")
        s_fin, s_out = sem("result_ready"), sem("output_written")
        block = ctx.enter_context(nc.Block())

        def hold(engine, semaphore, value):
            engine.wait_ge(semaphore, value)
            engine.sem_inc(s_held, 1)

        def all_rows(dram):
            return dram.rearrange("(t p) d -> p t d", p=PT)

        def column_of(dram):
            return dram.rearrange("(p o) -> p o", o=1)

        @block.sync
        def _(sp):
            sp.dma_start(msgw_in, msg_w).then_inc(s_w, 16)
            sp.dma_start(msgb_rows, msg_b.partition_broadcast(PT)).then_inc(s_w, 16)
            sp.dma_start(msgb_col, column_of(msg_b)).then_inc(s_w, 16)
            sp.dma_start(x_rows, all_rows(x)).then_inc(s_x, 16)
            for s in range(NT):
                t = ORDER[s]
                if s >= 2:
                    sp.wait_ge(s_tp, NQ * (s - 1))
                    sp.wait_ge(s_ext, s - 1)
                sp.dma_start(adj_in[:, s % 2, :], adj[t * PT:(t + 1) * PT, :]).then_inc(s_adj[s % 2], 16)
                if s == 1:
                    sp.wait_ge(s_sdV, NT // 2)
                    sp.dma_start(all_rows(d_rows), d_stage).then_inc(s_dstore, 16)
            sp.wait_ge(s_dense, 1)
            sp.dma_start(updw_in, upd_w).then_inc(s_w2, 16)
            sp.dma_start(updb_col, column_of(upd_b)).then_inc(s_w2, 16)
            sp.dma_start(lnw_rows, ln_w.partition_broadcast(PT)).then_inc(s_w2, 16)
            sp.dma_start(lnb_rows, ln_b.partition_broadcast(PT)).then_inc(s_w2, 16)
            sp.dma_start(x_again, all_rows(x)).then_inc(s_w2, 16)
            sp.dma_start(theta_in, theta.rearrange("k i o -> i k o")).then_inc(s_th, 16)
            sp.dma_start(gw_in[:, 0, :], w_msg).then_inc(s_gwl, 16)
            sp.dma_start(gw_in[:, 1:4, :], w_ih.rearrange("(g p) f -> p g f", p=PT)).then_inc(s_gwl, 16)
            sp.dma_start(gw_in[:, 4:7, :], w_hh.rearrange("(g p) f -> p g f", p=PT)).then_inc(s_gwl, 16)
            sp.dma_start(bmsg_col, column_of(b_msg)).then_inc(s_gwl, 16)
            sp.dma_start(bih_cols, b_ih.rearrange("(g p) -> p g", p=PT), allow_slow_non_contiguous=True).then_inc(s_gwl, 16)
            sp.dma_start(bhh_cols, b_hh.rearrange("(g p) -> p g", p=PT), allow_slow_non_contiguous=True).then_inc(s_gwl, 16)
            sp.wait_ge(s_x3, 1)
            for i, w in enumerate((wq, wk, wv, ws)):
                sp.dma_start(attw[:, PT * i:PT * i + PT], w).then_inc(s_aw, 16)
            sp.dma_start(bvs_rows[:, 0:PT], bv.partition_broadcast(PT)).then_inc(s_aw, 16)
            sp.dma_start(bvs_rows[:, PT:2 * PT], bs.partition_broadcast(PT)).then_inc(s_aw, 16)
            sp.dma_start(wb_rows, wb.rearrange("k o -> (k o)").partition_broadcast(PT)).then_inc(s_aw, 16)
            for r in range(4):
                for i, b in enumerate((bq, bk)):
                    sp.dma_start(qk_cols[C * r:C * r + C, H * i:H * i + H], b.rearrange("(h c) -> c h", c=C),
                                 allow_slow_non_contiguous=True).then_inc(s_aw, 16)
            for t in range(NT):
                if t >= 2:
                    sp.wait_ge(s_mask, 2 * H * (t - 1))
                sp.dma_start(adj_again[:, t % 2, :], adj[t * PT:(t + 1) * PT, :]).then_inc(s_adj2[t % 2], 16)
            sp.wait_ge(s_fin, 1)
            sp.dma_start(all_rows(out), o_rows).then_inc(s_out, 16)
            sp.wait_ge(s_out, 16)

        @block.gpsimd
        def _(gp):
            gp.memset(ident[:, :], 0.0).then_inc(s_pool, 1)
            gp.wait_ge(s_pool, 1)
            gp.affine_select(out=ident[:, :], in_=ident[:, :], compare_op=ALU.not_equal, fill=1.0,
                             base=0, pattern=[[-1, PT + 4]], channel_multiplier=1).then_inc(s_const, 1)
            gp.iota(iota_r[:, :], pattern=[[1, PT]], base=0, channel_multiplier=0,
                    allow_small_or_imprecise_dtypes=True).then_inc(s_const, 1)
            gp.iota(rowid[:, :], pattern=[[PT, NT]], base=0, channel_multiplier=1,
                    allow_small_or_imprecise_dtypes=True).then_inc(s_const, 1)
            gp.iota(seg_base[:, :, :], pattern=[[SEG, NSEG], [0, 8]], base=1, channel_multiplier=0,
                    allow_small_or_imprecise_dtypes=True).then_inc(s_const, 1)
            gp.wait_ge(s_dstore, 16)
            gp.memset(ones_sq, 1.0).then_inc(s_const2, 1)
            gp.memset(prefix_tri, 1.0).then_inc(s_const2, 1)
            gp.wait_ge(s_const2, 2)
            gp.affine_select(out=prefix_tri, in_=prefix_tri, compare_op=ALU.is_gt, fill=0.0,
                             base=0, pattern=[[1, PT]], channel_multiplier=-1).then_inc(s_const2, 1)
            u = 0
            for s in range(NT):
                gp.wait_ge(s_ext, s + 1)
                for v in range(UNITS[s]):
                    if u >= RING:
                        gp.wait_ge(s_unit, u - RING + 1)
                    for j in range(UNIT):
                        k = UNIT * v + j
                        gp.indirect_dma_start(
                            out=gath[:, u % RING, j, :], out_offset=None, in_=d_rows,
                            in_offset=bass.IndirectOffsetOnAxis(ap=column[:, s % 3, k:k + 1], axis=0)
                        ).then_inc(s_gath[u % RING], 16)
                    u += 1
            gp.wait_ge(s_counts, 1)
            batches = gp.value_load(loop_counts[0:1, NT:NT + 1], min_val=1, max_val=NT)
            with gp.Fori(0, batches) as b:
                hold(gp, s_picki, b + 1)
                gp.indirect_dma_start(out=adj_sel, out_offset=None, in_=adj,
                                      in_offset=bass.IndirectOffsetOnAxis(ap=rows_i[:, 0:1], axis=0)).then_inc(s_asel, 16)
            gp.wait_ge(s_aw, 16 * 15)
            for i in range(2):
                source = attw[:, PT * i:PT * i + PT].rearrange("p (h o c) -> p h o c", h=H, o=1)
                gp.tensor_copy(w_rep[:, i].rearrange("p h (r c) -> p h r c", r=4),
                               source.to_broadcast([PT, H, 4, C])).then_inc(s_rep, 1)
            for t in range(NT):
                gp.wait_ge(s_adj2[t % 2], 16 * (t // 2 + 1))
                gp.tensor_scalar(adj_again[:, t % 2, :], adj_again[:, t % 2, :], 0.0, MASKED,
                                 ALU.is_equal, ALU.mult).then_inc(s_pen, 1)

        @block.tensor
        def _(pe):
            pe.wait_ge(s_const, 1)
            pe.wait_ge(s_w, 48)
            pe.transpose(psum[:, 0, 0:PT], msgw_in[:, 0:PT], eye)
            pe.transpose(psum[:, 0, PT:2 * PT], msgw_in[:, PT:2 * PT], eye).then_inc(s_xtp, 1)
            pe.wait_ge(s_x, 16)
            for q in range(NQ):
                for j in range(TPQ):
                    ins = pe.transpose(psum[:, 1 + q, PT * j:PT * j + PT], x_rows[:, TPQ * q + j, :], eye)
                ins.then_inc(s_xtp, 1)
            for g in range(NT // 2):
                pe.wait_ge(s_xt, 2 + g // 2)
                if g >= 2:
                    pe.wait_ge(s_sdA, g - 1)
                    pe.wait_ge(s_sdV, g - 1)
                for j in range(2):
                    t = 2 * g + j
                    ins = pe.matmul(psum[:, 5 + g % 2, 256 * j:256 * j + 256], xT[:, PT * t:PT * t + PT], wT,
                                    start=True, stop=True)
                ins.then_inc(s_sdp, 1)
            for q in range(NQ):
                pe.matmul(psum[:, 1 + q, :], wT[:, PT:2 * PT], xT[:, BANK * q:BANK * q + BANK],
                          start=True, stop=True).then_inc(s_dtp, 1)

            def turn_adj(s):
                pe.wait_ge(s_adj[s % 2], 16 * (s // 2 + 1))
                for q in range(NQ):
                    n = NQ * s + q
                    if n >= 2:
                        pe.wait_ge(s_tpc, n - 1)
                    else:
                        pe.wait_ge(s_dt, 4)
                    for j in range(TPQ):
                        m = TPQ * q + j
                        ins = pe.transpose(psum[:, n % 2, PT * j:PT * j + PT],
                                           adj_in[:, s % 2, PT * m:PT * m + PT], eye)
                    ins.then_inc(s_tp, 1)

            unit = 0
            for s in range(NT + 1):
                if s < NT:
                    turn_adj(s)
                if s == 0:
                    continue
                if s >= 3:
                    pe.wait_ge(s_aggc, s - 2)
                for v in range(UNITS[s - 1]):
                    pe.wait_ge(s_gelu, unit + 1)
                    pe.wait_ge(s_diag, unit + 1)
                    for j in range(UNIT):
                        k = UNIT * v + j
                        ins = pe.matmul(psum[:, 2 + s % 2, 0:PT], gath[:, unit % RING, j, :], diag[:, unit % 2, j, :],
                                        start=k == 0, stop=k == UNIT * UNITS[s - 1] - 1)
                    ins.then_inc(s_unit, 1)
                    unit += 1
            pe.wait_ge(s_ext, NT)
            pe.wait_ge(s_const2, 3)
            pe.matmul(psum[:, 4, 0:NT], prefix_tri, flags[:, :], start=True, stop=True)
            pe.matmul(psum[:, 4, NT:2 * NT], ones_sq, flags[:, :], start=True, stop=True).then_inc(s_flagp, 1)
            pe.wait_ge(s_counts, 1)
            batches = pe.value_load(loop_counts[0:1, NT:NT + 1], min_val=1, max_val=NT)
            pe.wait_ge(s_aggc, NT)
            with pe.Fori(0, batches) as b:
                pairs = pe.value_load(loop_counts[0:1, ds(b, 1)], min_val=1, max_val=PT // 2)
                hold(pe, s_hot, b + 1)
                for t in range(NT):
                    pe.matmul(psum[:, 2, 0:1], pick_hot[:, t, :], rowid[:, t:t + 1], start=t == 0, stop=t == NT - 1)
                for t in range(NT):
                    ins = pe.matmul(psum[:, 3, 0:PT], s_rows[:, t, :], pick_hot[:, t, :], start=t == 0, stop=t == NT - 1)
                ins.then_inc(s_pickp, 1)
                hold(pe, s_asel, 16 * b + 16)
                with pe.Fori(0, pairs) as r:
                    for k in range(2):
                        row = b * PT + r * 2 + k
                        hold(pe, s_sel, row + 1 + b * 2)
                        for h in range(2):
                            hold(pe, s_half, row * 2 + h + 1)
                            for j in range(2):
                                ins = pe.matmul(psum[:, 4 + 2 * h + j, :], diag[:, 0, k, :],
                                                adj_sel[:, 1024 * h + BANK * j:1024 * h + BANK * j + BANK],
                                                start=True, stop=True)
                            ins.then_inc(s_bc, 1)
                hold(pe, s_dsum, b * PT + pairs * 2)
                pe.transpose(psum[:, 2, 0:PT], agg_sel, eye)
                for t in range(NT):
                    ins = pe.transpose(psum[:, 4 + t // TPQ, PT * (t % TPQ):PT * (t % TPQ) + PT], pick_hot[:, t, :], eye)
                ins.then_inc(s_dtr, 1)
                hold(pe, s_dcp, b * 2 + 2)
                for q in range(NQ):
                    ins = pe.matmul(psum[:, 4 + q, :], agg_selr, sel_hot[:, TPQ * q:TPQ * q + TPQ, :],
                                    start=True, stop=True)
                ins.then_inc(s_dout, 1)
            pe.wait_ge(s_dense, 1)
            pe.wait_ge(s_w2, 80)
            pe.transpose(psum[:, 0, 0:PT], updw_in[:, 0:PT], eye)
            pe.transpose(psum[:, 0, PT:2 * PT], updw_in[:, PT:2 * PT], eye).then_inc(s_utp, 1)
            pe.wait_ge(s_ut, 1)
            for q in range(NQ):
                part = slice(BANK * q, BANK * q + BANK)
                pe.matmul(psum[:, 4 + q, :], uT[:, 0:PT], xT[:, part], start=True, stop=False)
                pe.matmul(psum[:, 4 + q, :], uT[:, PT:2 * PT], aggT[:, part], start=False, stop=False)
                pe.matmul(psum[:, 4 + q, :], uT[:, PT:2 * PT], aggD[:, part], start=False, stop=True).then_inc(s_newp, 1)
            for q in range(NQ):
                pe.wait_ge(s_newx, q + 1)
                for j in range(TPQ):
                    t = TPQ * q + j
                    ins = pe.transpose(psum[:, q, PT * j:PT * j + PT], newT[:, PT * t:PT * t + PT], eye)
                ins.then_inc(s_rowp, 1)

            turn = [0]

            def turn_chunk(source):
                n = turn[0]
                if n >= 2:
                    pe.wait_ge(s_tnc, n - 1)
                for j in range(TPQ):
                    ins = pe.transpose(psum[:, 6 + n % 2, PT * j:PT * j + PT], source(j), eye)
                ins.then_inc(s_tnp, 1)
                turn[0] += 1

            def theta_product(k, q):
                for j in range(TPQ):
                    t = TPQ * q + j
                    ins = pe.matmul(psum[:, q, PT * j:PT * j + PT], termT[k][:, PT * t:PT * t + PT], theta_in[:, k, :],
                                    start=k == 0 and j == 0, stop=k == CHEB - 1, skip_group_check=True)
                return ins

            pe.wait_ge(s_x1, 1)
            for q in range(NQ):
                turn_chunk(lambda j: x1_rows[:, TPQ * q + j, :])
            pe.wait_ge(s_ths, 1)
            for q in range(NQ):
                pe.wait_ge(s_tnc, q + 1)
                theta_product(0, q)

            def finish_chunk(k, q):
                pe.wait_ge(s_hopc, NQ * (k - 1) + q + 1)
                if k < CHEB - 1:
                    turn_chunk(lambda j: termT[k][:, PT * (TPQ * q + j):PT * (TPQ * q + j) + PT])
                ins = theta_product(k, q)
                if k == CHEB - 1:
                    ins.then_inc(s_chp, 1)

            for k in range(1, CHEB):
                for q in range(NQ):
                    n = NQ * (k - 1) + q
                    if n >= 2:
                        pe.wait_ge(s_hopc, n - 1)
                    for m in range(NT):
                        if q == 0 and k > 1 and m % TPQ == 0:
                            pe.wait_ge(s_tnc, NQ * (k - 1) + m // TPQ + 1)
                        ins = pe.matmul(psum[:, 4 + n % 2, :], term_rows[k - 1][:, m, :],
                                        adjT[:, m, BANK * q:BANK * q + BANK], start=m == 0, stop=m == NT - 1)
                    ins.then_inc(s_hopp, 1)
                    if q >= 1:
                        finish_chunk(k, q - 1)
                finish_chunk(k, NQ - 1)

            pe.wait_ge(s_gwl, 96)
            pe.wait_ge(s_x2, 1)
            for g in range(7):
                ins = pe.transpose(psum[:, g // TPQ, PT * (g % TPQ):PT * (g % TPQ) + PT], gw_in[:, g, :], eye)
            ins.then_inc(s_gwp, 1)
            for q in range(NQ):
                turn_chunk(lambda j: x2_rows[:, TPQ * q + j, :])

            def hop2(q, ms):
                if ms[0] == 0 and q >= 2:
                    pe.wait_ge(s_agg2, q - 1)
                for m in ms:
                    ins = pe.matmul(psum[:, 4 + q % 2, :], x2_rows[:, m, :], adjT[:, m, BANK * q:BANK * q + BANK],
                                    start=m == 0, stop=m == NT - 1)
                if ms[-1] == NT - 1:
                    ins.then_inc(s_agg2p, 1)

            def message(q):
                if q == 0:
                    pe.wait_ge(s_gwc, 2)
                    pe.wait_ge(s_tnc, turn[0])
                pe.wait_ge(s_agg2, q + 1)
                if q >= 1:
                    pe.wait_ge(s_msg, q)
                pe.matmul(psum[:, 6, :], gwT[:, 0, :], agg_c, start=True, stop=True).then_inc(s_msgp, 1)

            def gates(q):
                part = x2T[:, BANK * q:BANK * q + BANK]
                pe.wait_ge(s_msg, q + 1)
                if q >= 1:
                    pe.wait_ge(s_pre, q)
                for g in range(2):
                    pe.matmul(psum[:, g, :], gwT[:, 1 + g, :], msg_c, start=True, stop=False)
                    pe.matmul(psum[:, g, :], gwT[:, 4 + g, :], part, start=False, stop=True)
                pe.matmul(psum[:, 2, :], gwT[:, 3, :], msg_c, start=True, stop=True)
                pe.matmul(psum[:, 3, :], gwT[:, 6, :], part, start=True, stop=True).then_inc(s_gate, 1)

            def turn_u(q):
                pe.wait_ge(s_cell, q + 1)
                if q >= 1:
                    pe.wait_ge(s_utc, q)
                for j in range(TPQ):
                    ins = pe.transpose(psum[:, 7, PT * j:PT * j + PT], u_c[:, PT * j:PT * j + PT], eye)
                ins.then_inc(s_utn, 1)

            for q in range(NQ + 2):
                if q < NQ:
                    hop2(q, range(0, NT // 2))
                if 1 <= q <= NQ:
                    message(q - 1)
                if q >= 2:
                    turn_u(q - 2)
                if q < NQ:
                    hop2(q, range(NT // 2, NT))
                if 1 <= q <= NQ:
                    gates(q - 1)

            pe.wait_ge(s_x3, 1)
            for q in range(NQ):
                turn_chunk(lambda j: x3_rows[:, TPQ * q + j, :])
            pe.wait_ge(s_rep, 2)
            n = 0
            for i in range(2):
                for h in range(H):
                    for q in range(NQ):
                        if i == 0 and h == 0:
                            pe.wait_ge(s_tnc, turn[0] - NQ + q + 1)
                        if n >= 4:
                            pe.wait_ge(s_lo, n - 3)
                        pe.matmul(psum[:, n % 4, :], w_rep[:, i, h, :], x3T[:, BANK * q:BANK * q + BANK],
                                  start=True, stop=True).then_inc(s_prp, 1)
                        n += 1
            for g in range(NT // 2):
                if g >= 2:
                    pe.wait_ge(s_vc, g - 1)
                for j in range(2):
                    t = 2 * g + j
                    ins = pe.matmul(psum[:, 4 + g % 2, 256 * j:256 * j + 256], x3T[:, PT * t:PT * t + PT],
                                    attw[:, 2 * PT:4 * PT], start=True, stop=True)
                ins.then_inc(s_vp, 1)

            def scores(i):
                t, h = divmod(i, H)
                for a in range(2):
                    if i >= 1:
                        pe.wait_ge(s_mask, 2 * (i - 1) + a + 1)
                    for j in range(2):
                        ins = pe.matmul(psum[:, 2 * a + j, :], qs[:, h, PT * t:PT * t + PT],
                                        ks[:, h, 1024 * a + BANK * j:1024 * a + BANK * j + BANK], start=True, stop=True)
                    ins.then_inc(s_scp, 1)

            def turn_probs(i):
                pe.wait_ge(s_exp, i + 1)
                for q in range(NQ):
                    n = NQ * i + q
                    if n >= 3:
                        before = n - 3
                        f, e = divmod(before, NQ)
                        pe.wait_ge(s_etA if e < 2 else s_etV, 2 * f + e % 2 + 1)
                    for j in range(TPQ):
                        m = TPQ * q + j
                        ins = pe.transpose(psum[:, 4 + n % 3, PT * j:PT * j + PT], masked[:, i % 2, PT * m:PT * m + PT], eye)
                    ins.then_inc(s_etp, 1)

            def values(t):
                pe.wait_ge(s_etA, 2 * H * (t + 1))
                pe.wait_ge(s_etV, 2 * H * (t + 1))
                if t >= 1:
                    pe.wait_ge(s_o, t)
                for m in range(NT):
                    for h in range(H):
                        ins = pe.matmul(psum[C * h:C * h + C, 7, 0:PT], v_rows[:, m, C * h:C * h + C],
                                        turned[(H * t + h) % 8][:, m, :], start=m == 0, stop=m == NT - 1)
                ins.then_inc(s_avp, 1)

            def turn_values(t):
                pe.wait_ge(s_avc, t + 1)
                if t >= 1:
                    pe.wait_ge(s_o, t)
                pe.transpose(psum[:, 7, PT:2 * PT], avT, eye).then_inc(s_avt, 1)

            pe.wait_ge(s_vc, NT // 2)
            pe.wait_ge(s_lo, 32)
            steps = NT * H
            for i in range(steps + 3):
                if i < steps:
                    scores(i)
                if i >= 2 and (i - 2) % H == H - 1:
                    values((i - 2) // H)
                if 1 <= i <= steps:
                    turn_probs(i - 1)
                if i >= 2 and (i - 2) % H == H - 1:
                    turn_values((i - 2) // H)

        @block.vector
        def _(ve):
            tally = Tally(s_dve)

            def settle(ins):
                ve.wait_ge(s_dve, tally.step(ins))

            def layernorm(turn, source, target, ready):
                for t in range(NT):
                    ins = ve.bn_stats(stats[:, t, :], source[:, t, :])
                settle(ins)
                for t in range(NT):
                    ins = ve.bn_aggr(moments[:, t, :], stats[:, t, :])
                settle(ins)
                ve.tensor_scalar(rstd, moments[:, :, 1], LN_EPS, None, ALU.add).then_inc(s_ln, 1)
                ve.wait_ge(s_ln2, turn + 1)
                settle(ve.reciprocal(rstd, rstd))
                for t in range(NT):
                    ins = ve.tensor_scalar(target[:, t, :], source[:, t, :], moments[:, t, 0:1], rstd[:, t:t + 1],
                                           ALU.subtract, ALU.mult)
                if ready is None:
                    settle(ins)
                else:
                    ins.then_inc(ready, 1)
                    ve.wait_ge(ready, 1)

            ve.wait_ge(s_w, 48)
            for g in range(NT // 2):
                ve.wait_ge(s_sdA, g + 1)
                both = psum[:, 5 + g % 2, :].rearrange("p (j c) -> p j c", j=2)
                ve.tensor_tensor(d_stage[:, 2 * g:2 * g + 2, :], both[:, :, PT:2 * PT],
                                 msgb_rows.rearrange("p (o d) -> p o d", o=1).to_broadcast([PT, 2, PT]),
                                 ALU.add).then_inc(s_sdV, 1)

            def count_edges(a):
                scratch = msgs.bitcast(bf16)[:, 0:N]
                settle(ve.tensor_scalar(scratch, a, 0.0, None, ALU.not_equal, ALU.add, accum_out=edge_count[:, 0:1]))

            def extract(s):
                t, a, r = ORDER[s], adj_in[:, s % 2, :], s % 3
                slots = UNIT * UNITS[s]
                ve.wait_ge(s_adj[s % 2], 16 * (s // 2 + 1))
                if s == 0:
                    ve.wait_ge(s_const, 4)
                    ve.wait_ge(s_dtp, 4)
                    ve.wait_ge(s_sdV, NT // 2)
                count_edges(a)
                if slots > 20:
                    source = a
                    for k in range(0, slots, 8):
                        eight = picked[:, k:k + 8]
                        settle(ve.max(eight, source))
                        ve.max_index(column.bitcast(u32)[:, r, k:k + 8], eight, source)
                        if k + 8 < slots:
                            settle(ve.match_replace(msgs, eight, source, -1.0))
                            source = msgs
                    settle(ve.tensor_scalar(scrap[:, 0:slots], picked[:, 0:slots], 0.0, None, ALU.is_gt, ALU.add,
                                            accum_out=edge_count[:, 1:2]))
                    ve.tensor_tensor(flags[:, t:t + 1], edge_count[:, 0:1], edge_count[:, 1:2], ALU.not_equal)
                    settle(ve.tensor_tensor(keep[:, :], edge_count[:, 0:1], edge_count[:, 1:2], ALU.is_equal))
                    ve.tensor_scalar(weight[:, r, 0:slots], picked[:, 0:slots], keep[:, 0:1], None,
                                     ALU.mult).then_inc(s_ext, 1)
                    ve.wait_ge(s_ext, s + 1)
                    return
                for g in range(NSEG):
                    ins = ve.max(cand_val[:, 8 * g:8 * g + 8], a[:, SEG * g:SEG * g + SEG])
                settle(ins)
                for g in range(NSEG):
                    ins = ve.max_index(cand_pos[:, 8 * g:8 * g + 8], cand_val[:, 8 * g:8 * g + 8],
                                       a[:, SEG * g:SEG * g + SEG])
                settle(ins)
                settle(ve.tensor_tensor(cand_left[:, :], cand_pos[:, :], seg_base.rearrange("p g e -> p (g e)"), ALU.add))
                settle(ve.scalar_tensor_tensor(cand_key[:, :], cand_val[:, :], 0.0, cand_left[:, :], ALU.is_gt, ALU.mult))
                source = cand_key
                for k in range(0, slots, 8):
                    eight = picked[:, k:k + 8]
                    settle(ve.max(eight, source[:, :]))
                    if k + 8 < slots:
                        settle(ve.match_replace(cand_left[:, :], eight, source[:, :], 0.0))
                        source = cand_left
                for k in range(slots):
                    ve.scalar_tensor_tensor(msgs[:, CAND * k:CAND * k + CAND], cand_key[:, :], picked[:, k:k + 1],
                                            cand_val[:, :], ALU.is_equal, ALU.mult, accum_out=weight[:, r, k:k + 1])
                settle(ve.tensor_scalar(scrap[:, 0:slots], picked[:, 0:slots], 0.0, None, ALU.is_gt, ALU.add,
                                        accum_out=edge_count[:, 1:2]))
                ve.tensor_tensor(flags[:, t:t + 1], edge_count[:, 0:1], edge_count[:, 1:2], ALU.not_equal)
                settle(ve.tensor_tensor(keep[:, :], edge_count[:, 0:1], edge_count[:, 1:2], ALU.is_equal))
                settle(ve.tensor_scalar(weight[:, r, 0:slots], weight[:, r, 0:slots], keep[:, 0:1], None, ALU.mult))
                ve.tensor_scalar(column[:, r, 0:slots], picked[:, 0:slots], 1.0, 1.0, ALU.max,
                                 ALU.subtract).then_inc(s_ext, 1)

            def feed_unit(u, s, v):
                t = ORDER[s]
                ve.wait_ge(s_gath[u % RING], 16 * UNIT * (u // RING + 1))
                ve.tensor_tensor(gath[:, u % RING, :, :], gath[:, u % RING, :, :],
                                 s_rows[:, t:t + 1, :].to_broadcast([PT, UNIT, PT]), ALU.add).then_inc(s_add, 1)
                if u >= 2:
                    ve.wait_ge(s_unit, u - 1)
                w = weight[:, s % 3, UNIT * v:UNIT * v + UNIT].rearrange("p (k o) -> p k o", o=1)
                ve.tensor_tensor(diag[:, u % 2, :, :], eye.rearrange("p (o q) -> p o q", o=1).to_broadcast([PT, UNIT, PT]),
                                 w.to_broadcast([PT, UNIT, PT]), ALU.mult).then_inc(s_diag, 1)

            unit = 0
            for s in range(NT + 1):
                if s < NT:
                    extract(s)
                if s == 0:
                    ve.wait_ge(s_sdA, NT // 2)
                else:
                    for v in range(UNITS[s - 1]):
                        feed_unit(unit, s - 1, v)
                        unit += 1
            ve.wait_ge(s_flagp, 1)
            settle(ve.tensor_copy(total[:, :], psum[:, 4, 0:2 * NT]))
            cum = loop_f[:, 0:NT]
            settle(ve.tensor_tensor_scan(cum, ones_sq[:, 0:NT], total[:, NT:2 * NT], 0.0, ALU.mult, ALU.add))
            settle(ve.tensor_tensor(pos[:, :], cum, total[:, NT:2 * NT], ALU.subtract))
            settle(ve.tensor_tensor(pos[:, :], pos[:, :], total[:, 0:NT], ALU.add))
            settle(ve.scalar_tensor_tensor(pos[:, :], pos[:, :], 1.0, flags[:, :], ALU.add, ALU.mult))
            settle(ve.tensor_scalar(pos[:, :], pos[:, :], -1.0, None, ALU.add))
            left = loop_f[0:1, NT:2 * NT]
            settle(ve.tensor_scalar(left, rowid[0:1, :], -1.0, loop_f[0:1, NT - 1:NT], ALU.mult, ALU.add))
            settle(ve.tensor_scalar(loop_f[0:1, 2 * NT:3 * NT], left, 0.0, None, ALU.is_gt, ALU.add,
                                    accum_out=edge_count[0:1, 0:1]))
            ve.tensor_scalar(loop_counts[0:1, NT:NT + 1], edge_count[0:1, 0:1], 1.0, None, ALU.max)
            settle(ve.tensor_scalar(left, left, 1.0, 2.0, ALU.add, ALU.max))
            settle(ve.tensor_scalar(loop_counts[0:1, 0:NT], left, PT + 1.0, None, ALU.min))
            ve.tensor_scalar(loop_counts[0:1, 0:NT], loop_counts[0:1, 0:NT], 1, None,
                             ALU.arith_shift_right).then_inc(s_counts, 1)
            ve.memset(aggD[:, 0:N // 2], 0.0).then_inc(s_half, 1)
            ve.memset(aggD[:, N // 2:N], 0.0).then_inc(s_half, 1)
            ve.wait_ge(s_half, 2)
            ve.wait_ge(s_counts, 1)
            ve.wait_ge(s_aggc, NT)
            flat = psum.rearrange("p b n -> p (b n)")
            batches = ve.value_load(loop_counts[0:1, NT:NT + 1], min_val=1, max_val=NT)
            with ve.Fori(0, batches) as b:
                pairs = ve.value_load(loop_counts[0:1, ds(b, 1)], min_val=1, max_val=PT // 2)
                ve.tensor_tensor(pick_hot, pos.rearrange("p (t o) -> p t o", o=1).to_broadcast([PT, NT, PT]),
                                 iota_r.rearrange("p (o r) -> p o r", o=1).to_broadcast([PT, NT, PT]),
                                 ALU.is_equal).then_inc(s_hot, 1)
                ve.memset(agg_sel, 0.0).then_inc(s_zero, 1)
                hold(ve, s_hot, b + 1)
                ve.tensor_scalar(iota_r[:, :], iota_r[:, :], float(PT), None, ALU.add).then_inc(s_iota, 1)
                hold(ve, s_pickp, b + 1)
                ve.tensor_copy(rows_i[:, :], psum[:, 2, 0:1]).then_inc(s_picki, 1)
                ve.tensor_copy(sT_sel, psum[:, 3, 0:PT]).then_inc(s_stsel, 1)
                for k in range(2):
                    ve.tensor_copy(diag[:, 0, k, :], ident[:, k:k + 1].to_broadcast([PT, PT])).then_inc(s_sel, 1)
                hold(ve, s_zero, b + 1)
                with ve.Fori(0, pairs) as r:
                    for k in range(2):
                        row = b * PT + r * 2 + k
                        for h in range(2):
                            half = msgs[:, 1024 * h:1024 * h + 1024]
                            hold(ve, s_mg, row * 2 + h + 1)
                            hold(ve, s_bc, row * 2 + h + 1)
                            ve.tensor_tensor_reduce(half, half, flat[:, 2048 + 1024 * h:2048 + 1024 * h + 1024], 1.0, 0.0,
                                                    ALU.mult, ALU.add, half_sum[:, k, h:h + 1]).then_inc(s_half, 1)
                        hold(ve, s_half, row * 2 + 4)
                        ve.tensor_tensor(agg_sel[:, ds(r * 2 + k, 1)], half_sum[:, k, 0:1], half_sum[:, k, 1:2],
                                         ALU.add).then_inc(s_dsum, 1)
                        ve.tensor_copy(diag[:, 0, k, :],
                                       ident[:, ds(r * 2 + k + 2, 1)].to_broadcast([PT, PT])).then_inc(s_sel, 1)
                hold(ve, s_dtr, b + 1)
                ve.tensor_copy(agg_selr, psum[:, 2, 0:PT]).then_inc(s_dcp, 1)
                ve.tensor_copy(slot(5), flat[:, 2048:4096]).then_inc(s_dcp, 1)
                hold(ve, s_dout, b + 1)
                ve.tensor_tensor(aggD, aggD, flat[:, 2048:4096], ALU.add).then_inc(s_dacc, 1)
                hold(ve, s_dacc, b + 1)
                hold(ve, s_iota, b + 1)
            ve.memset(edge_count[:, :], 0.0).then_inc(s_dense, 1)
            for q in range(NQ):
                part = slice(BANK * q, BANK * q + BANK)
                ve.wait_ge(s_newg, q + 1)
                ve.tensor_tensor(newT[:, part], newT[:, part], xT[:, part], ALU.add).then_inc(s_newx, 1)
            ve.wait_ge(s_hc, NQ)
            layernorm(0, h_rows, h_rows, None)
            ve.wait_ge(s_w2, 80)
            settle(ve.tensor_tensor(h_rows, h_rows, lnw_rows.rearrange("p (o d) -> p o d", o=1).to_broadcast([PT, NT, PT]),
                                    ALU.mult))
            settle(ve.tensor_tensor(h_rows, h_rows, lnb_rows.rearrange("p (o d) -> p o d", o=1).to_broadcast([PT, NT, PT]),
                                    ALU.add))
            settle(ve.tensor_tensor(h_rows, h_rows, x_again, ALU.add))
            layernorm(1, h_rows, x1_rows, s_x1)

            ve.wait_ge(s_th, 16)
            for k in range(CHEB):
                ins = ve.tensor_scalar(theta_in[:, k, :], theta_in[:, k, :], cheb_coeff(k), None, ALU.mult)
            ins.then_inc(s_ths, 1)
            for k in range(1, CHEB):
                for q in range(NQ):
                    n = NQ * (k - 1) + q
                    part = slice(BANK * q, BANK * q + BANK)
                    ve.wait_ge(s_hopp, n + 1)
                    if k == 1:
                        ve.tensor_copy(termT[1][:, part], psum[:, 4 + n % 2, :]).then_inc(s_hopc, 1)
                    else:
                        ve.scalar_tensor_tensor(termT[k][:, part], psum[:, 4 + n % 2, :], 2.0, termT[k - 2][:, part],
                                                ALU.mult, ALU.subtract).then_inc(s_hopc, 1)
            for q in range(NQ):
                ve.wait_ge(s_chp, q + 1)
                ins = ve.tensor_tensor(slot(5)[:, BANK * q:BANK * q + BANK], psum[:, q, :],
                                       slot(6)[:, BANK * q:BANK * q + BANK], ALU.add)
            settle(ins)
            layernorm(2, y_rows, x2_rows, s_x2)

            ve.wait_ge(s_gwl, 96)
            ve.tensor_tensor(brz_cols, bih_cols[:, 0:2], bhh_cols[:, 0:2], ALU.add).then_inc(s_gb, 1)
            for q in range(NQ):
                part = x2T[:, BANK * q:BANK * q + BANK]
                ve.wait_ge(s_gact, 2 * q + 2)
                settle(ve.scalar_tensor_tensor(t_c, psum[:, 3, :], bhh_cols[:, 2:3], r_c, ALU.add, ALU.mult))
                ve.tensor_tensor(t_c, psum[:, 2, :], t_c, ALU.add).then_inc(s_pre, 1)
                ve.wait_ge(s_tanh, q + 1)
                settle(ve.tensor_tensor(t_c, part, n_c, ALU.subtract))
                settle(ve.tensor_tensor(t_c, t_c, z_c, ALU.mult))
                settle(ve.tensor_tensor(t_c, t_c, n_c, ALU.add))
                if q >= 1:
                    ve.wait_ge(s_utn, q)
                ve.tensor_tensor(u_c, t_c, part, ALU.add).then_inc(s_cell, 1)
            ve.wait_ge(s_utc, NQ)
            layernorm(3, u_rows, x3_rows, s_x3)

            ve.wait_ge(s_aw, 16 * 15)
            n = 0
            for i, (stack, lows) in enumerate(((qs, ((64, 64),)), (ks, ((32, 32), (96, 32))))):
                for h in range(H):
                    for q in range(NQ):
                        ve.wait_ge(s_hi, n + 1)
                        for p, k in lows:
                            part = stack[p:p + k, h, BANK * q:BANK * q + BANK]
                            ins = ve.scalar_tensor_tensor(part, psum[p:p + k, n % 4, :], qk_cols[p:p + k, H * i + h:H * i + h + 1],
                                                          part.bitcast(fp32), ALU.add, ALU.subtract)
                        ins.then_inc(s_lo, 1)
                        n += 1
            for g in range(NT // 2):
                ve.wait_ge(s_vp, g + 1)
                both = psum[:, 4 + g % 2, :].rearrange("p (j c) -> p j c", j=2)
                bias = bvs_rows.rearrange("p (a o d) -> p a o d", a=2, o=1)
                ve.tensor_tensor(v_rows[:, 2 * g:2 * g + 2, :], both[:, :, 0:PT], bias[:, 0].to_broadcast([PT, 2, PT]), ALU.add)
                ve.tensor_tensor(xr_rows[:, 2 * g:2 * g + 2, :], both[:, :, PT:2 * PT],
                                 bias[:, 1].to_broadcast([PT, 2, PT]), ALU.add).then_inc(s_vc, 1)
            ve.wait_ge(s_vc, NT // 2)
            ve.tensor_tensor(wb_out, wb_rows[:, 0:PT], wb_rows[:, 2 * PT:3 * PT], ALU.add)
            settle(ve.tensor_tensor(wb_skip, wb_rows[:, PT:2 * PT], wb_rows[:, 2 * PT:3 * PT], ALU.subtract))
            for t in range(NT):
                settle(ve.tensor_tensor_reduce(gate_scrap, xr_rows[:, t, :], wb_skip, 1.0, 0.0, ALU.mult, ALU.add,
                                               skip_dot[:, t:t + 1]))

            def mask_and_max(i):
                t, h = divmod(i, H)
                if h == 0:
                    ve.wait_ge(s_pen, t + 1)
                if i >= 2:
                    ve.wait_ge(s_etp, NQ * (i - 1))
                for a in range(2):
                    ve.wait_ge(s_scp, 2 * i + a + 1)
                    ve.tensor_tensor_reduce(masked[:, i % 2, 1024 * a:1024 * a + 1024], flat[:, 1024 * a:1024 * a + 1024],
                                            adj_again[:, t % 2, 1024 * a:1024 * a + 1024], 1.0, FLOOR, ALU.add, ALU.max,
                                            row_max[:, i % 2, a:a + 1]).then_inc(s_mask, 1)
                ve.wait_ge(s_mask, 2 * i + 2)
                settle(ve.tensor_tensor(row_max[:, i % 2, 2:3], row_max[:, i % 2, 0:1], row_max[:, i % 2, 1:2], ALU.max))
                ve.tensor_scalar(row_max[:, i % 2, 3:4], row_max[:, i % 2, 2:3], -SCALE, None, ALU.mult).then_inc(s_bias, 1)

            def copy_turned(i):
                if i // H >= 2:
                    ve.wait_ge(s_avp, i // H - 1)
                for q in (2, 3):
                    n = NQ * i + q
                    ve.wait_ge(s_etp, n + 1)
                    ve.tensor_copy(turned[i % 8][:, TPQ * q:TPQ * q + TPQ, :], psum[:, 4 + n % 3, :]).then_inc(s_etV, 1)

            def normalise(t):
                ve.wait_ge(s_exp, H * (t + 1))
                settle(ve.scalar_tensor_tensor(rden[:, t % 2, :], den[:, t, :], 0.0, den[:, t, :], ALU.is_equal, ALU.add))
                settle(ve.reciprocal(rden[:, t % 2, :], rden[:, t % 2, :]))
                ve.wait_ge(s_avt, t + 1)
                ve.tensor_tensor(o_rows[:, t, :].rearrange("p (c h) -> p h c", h=H),
                                 psum[:, 7, PT:2 * PT].rearrange("p (h c) -> p h c", h=H),
                                 rden[:, t % 2, :].rearrange("p (h o) -> p h o", o=1).to_broadcast([PT, H, C]),
                                 ALU.mult).then_inc(s_o, 1)
                ve.wait_ge(s_o, t + 1)
                ve.tensor_tensor_reduce(gate_scrap, o_rows[:, t, :], wb_out, 1.0, skip_dot[:, t:t + 1], ALU.mult, ALU.add,
                                        gate[:, t % 2, 0:1]).then_inc(s_gz, 1)

            def mix(t):
                ve.wait_ge(s_ge, t + 1)
                settle(ve.tensor_scalar(gate[:, t % 2, 2:3], gate[:, t % 2, 1:2], 1.0, None, ALU.add))
                ve.reciprocal(gate[:, t % 2, 3:4], gate[:, t % 2, 2:3])
                settle(ve.tensor_tensor(gate_scrap, xr_rows[:, t, :], o_rows[:, t, :], ALU.subtract))
                settle(ve.scalar_tensor_tensor(o_rows[:, t, :], gate_scrap, gate[:, t % 2, 3:4], o_rows[:, t, :],
                                               ALU.mult, ALU.add))
                settle(ve.tensor_tensor(o_rows[:, t, :], o_rows[:, t, :], x3_rows[:, t, :], ALU.add))

            steps = NT * H
            for i in range(steps + 5):
                if i < steps:
                    mask_and_max(i)
                if 1 <= i <= steps:
                    copy_turned(i - 1)
                if i >= 6 and (i - 6) % H == 0 and (i - 6) // H < NT:
                    normalise((i - 6) // H)
                if i >= 8 and (i - 8) % H == 0 and (i - 8) // H < NT:
                    mix((i - 8) // H)
            layernorm(4, o_rows, o_rows, s_fin)

        @block.scalar
        def _(ac):
            def square_root(turn):
                ac.wait_ge(s_ln, turn + 1)
                ac.activation(rstd, rstd, ACT.Sqrt).then_inc(s_ln2, 1)

            ac.wait_ge(s_xtp, 1)
            ac.activation(wT, psum[:, 0, 0:2 * PT], ACT.Copy).then_inc(s_xt, 1)
            for q in range(NQ):
                ac.wait_ge(s_xtp, q + 2)
                ac.activation(xT[:, BANK * q:BANK * q + BANK], psum[:, 1 + q, :], ACT.Copy).then_inc(s_xt, 1)
            for g in range(NT // 2):
                ac.wait_ge(s_sdp, g + 1)
                both = psum[:, 5 + g % 2, :].rearrange("p (j c) -> p j c", j=2)
                ac.activation(s_rows[:, 2 * g:2 * g + 2, :], both[:, :, 0:PT], ACT.Copy).then_inc(s_sdA, 1)
            ac.wait_ge(s_w, 48)
            for q in range(NQ):
                ac.wait_ge(s_dtp, q + 1)
                ac.activation(dT[:, BANK * q:BANK * q + BANK], psum[:, 1 + q, :], ACT.Identity,
                              bias=msgb_col).then_inc(s_dt, 1)
            unit = 0
            for s in range(NT + 1):
                if s < NT:
                    t = ORDER[s]
                    for q in range(NQ):
                        n = NQ * s + q
                        ac.wait_ge(s_tp, n + 1)
                        ac.activation(adjT[:, TPQ * q:TPQ * q + TPQ, PT * t:PT * t + PT], psum[:, n % 2, :],
                                      ACT.Copy).then_inc(s_tpc, 1)
                if s == 0:
                    continue
                for v in range(UNITS[s - 1]):
                    ac.wait_ge(s_add, unit + 1)
                    ac.activation(gath[:, unit % RING, :, :], gath[:, unit % RING, :, :], ACT.Gelu).then_inc(s_gelu, 1)
                    unit += 1
                t = ORDER[s - 1]
                ac.wait_ge(s_unit, unit)
                ac.activation(aggT[:, PT * t:PT * t + PT], psum[:, 2 + s % 2, 0:PT], ACT.Copy).then_inc(s_aggc, 1)
            ac.wait_ge(s_counts, 1)
            batches = ac.value_load(loop_counts[0:1, NT:NT + 1], min_val=1, max_val=NT)
            with ac.Fori(0, batches) as b:
                pairs = ac.value_load(loop_counts[0:1, ds(b, 1)], min_val=1, max_val=PT // 2)
                hold(ac, s_stsel, b + 1)
                with ac.Fori(0, pairs) as r:
                    for k in range(2):
                        row = b * PT + r * 2 + k
                        for h in range(2):
                            hold(ac, s_half, row * 2 + h + 1)
                            ac.activation(msgs[:, 1024 * h:1024 * h + 1024], dT[:, 1024 * h:1024 * h + 1024], ACT.Gelu,
                                          bias=sT_sel[:, ds(r * 2 + k, 1)]).then_inc(s_mg, 1)
            ac.wait_ge(s_utp, 1)
            ac.activation(uT, psum[:, 0, 0:2 * PT], ACT.Copy).then_inc(s_ut, 1)
            for q in range(NQ):
                ac.wait_ge(s_newp, q + 1)
                ac.activation(newT[:, BANK * q:BANK * q + BANK], psum[:, 4 + q, :], ACT.Gelu,
                              bias=updb_col).then_inc(s_newg, 1)
            for q in range(NQ):
                ac.wait_ge(s_rowp, q + 1)
                ac.activation(slot(2)[:, BANK * q:BANK * q + BANK], psum[:, q, :], ACT.Copy).then_inc(s_hc, 1)
            square_root(0)
            square_root(1)

            turn = [0]

            def copy_turned(target):
                n = turn[0]
                ac.wait_ge(s_tnp, n + 1)
                ac.activation(target, psum[:, 6 + n % 2, :], ACT.Copy).then_inc(s_tnc, 1)
                turn[0] += 1

            for q in range(NQ):
                copy_turned(slot(0)[:, BANK * q:BANK * q + BANK])
            for k in range(1, CHEB - 1):
                for q in range(NQ):
                    copy_turned(term_rows[k][:, TPQ * q:TPQ * q + TPQ, :])
            square_root(2)

            ac.wait_ge(s_gwp, 1)
            ac.activation(gwT[:, 0:4, :], psum[:, 0, :], ACT.Copy).then_inc(s_gwc, 1)
            ac.activation(gwT[:, 4:7, :], psum[:, 1, 0:3 * PT], ACT.Copy).then_inc(s_gwc, 1)
            for q in range(NQ):
                copy_turned(slot(0)[:, BANK * q:BANK * q + BANK])
            ac.wait_ge(s_gb, 1)
            for q in range(NQ + 2):
                if 1 <= q <= NQ:
                    ac.wait_ge(s_msgp, q)
                    if q >= 2:
                        ac.wait_ge(s_gate, q - 1)
                    ac.activation(msg_c, psum[:, 6, :], ACT.Relu, bias=bmsg_col).then_inc(s_msg, 1)
                if q >= 2:
                    ac.wait_ge(s_utn, q - 1)
                    ac.activation(slot(4)[:, BANK * (q - 2):BANK * (q - 1)], psum[:, 7, :], ACT.Copy).then_inc(s_utc, 1)
                if q < NQ:
                    ac.wait_ge(s_agg2p, q + 1)
                    if q >= 1:
                        ac.wait_ge(s_msgp, q)
                    ac.activation(agg_c, psum[:, 4 + q % 2, :], ACT.Copy).then_inc(s_agg2, 1)
                if 1 <= q <= NQ:
                    ac.wait_ge(s_gate, q)
                    if q >= 2:
                        ac.wait_ge(s_cell, q - 1)
                    ac.activation(r_c, psum[:, 0, :], ACT.Sigmoid, bias=brz_cols[:, 0:1]).then_inc(s_gact, 1)
                    ac.activation(z_c, psum[:, 1, :], ACT.Sigmoid, bias=brz_cols[:, 1:2]).then_inc(s_gact, 1)
                    ac.wait_ge(s_pre, q)
                    ac.activation(n_c, t_c, ACT.Tanh, bias=bih_cols[:, 2:3]).then_inc(s_tanh, 1)
            square_root(3)

            for q in range(NQ):
                copy_turned(slot(0)[:, BANK * q:BANK * q + BANK])
            ac.wait_ge(s_aw, 16 * 15)
            n = 0
            for i, stack in enumerate((qs, ks)):
                for h in range(H):
                    for q in range(NQ):
                        ac.wait_ge(s_prp, n + 1)
                        ac.activation(stack[:, h, BANK * q:BANK * q + BANK], psum[:, n % 4, :], ACT.Identity,
                                      bias=qk_cols[:, H * i + h:H * i + h + 1]).then_inc(s_hi, 1)
                        n += 1
            steps = NT * H
            for i in range(steps + 4):
                t, h = divmod(i, H)
                if i < steps:
                    ac.wait_ge(s_bias, i + 1)
                    ac.activation(masked[:, i % 2, :], masked[:, i % 2, :], ACT.Exp, scale=SCALE,
                                  bias=row_max[:, i % 2, 3:4], accum_out=den[:, t, h:h + 1]).then_inc(s_exp, 1)
                if i >= 5 and (i - 5) % H == 0 and (i - 5) // H < NT:
                    done = (i - 5) // H
                    ac.wait_ge(s_avp, done + 1)
                    if done >= 1:
                        ac.wait_ge(s_avt, done)
                    ac.activation(avT, psum[:, 7, 0:PT], ACT.Copy).then_inc(s_avc, 1)
                if 1 <= i <= steps:
                    j = i - 1
                    if j // H >= 2:
                        ac.wait_ge(s_avp, j // H - 1)
                    for q in (0, 1):
                        n = NQ * j + q
                        ac.wait_ge(s_etp, n + 1)
                        ac.activation(turned[j % 8][:, TPQ * q:TPQ * q + TPQ, :], psum[:, 4 + n % 3, :],
                                      ACT.Copy).then_inc(s_etA, 1)
                if i >= 7 and (i - 7) % H == 0 and (i - 7) // H < NT:
                    done = (i - 7) // H
                    ac.wait_ge(s_gz, done + 1)
                    ac.activation(gate[:, done % 2, 1:2], gate[:, done % 2, 0:1], ACT.Exp, scale=-1.0).then_inc(s_ge, 1)
            square_root(4)


_INS = ['x', 'adj', 'L0_gnn_msg_w', 'L0_gnn_msg_b', 'L0_gnn_upd_w', 'L0_gnn_upd_b', 'L0_gnn_ln_w', 'L0_gnn_ln_b',
        'L1_gnn_theta', 'L2_gnn_W_msg', 'L2_gnn_b_msg', 'L2_gnn_W_ih', 'L2_gnn_W_hh', 'L2_gnn_b_ih', 'L2_gnn_b_hh',
        'L3_gnn_Wq', 'L3_gnn_bq', 'L3_gnn_Wk', 'L3_gnn_bk', 'L3_gnn_Wv', 'L3_gnn_bv', 'L3_gnn_Ws', 'L3_gnn_bs',
        'L3_gnn_Wb']


def kernel(**inputs):
    import numpy as _np
    import concourse.bacc as _bacc
    from concourse import mybir as _mybir
    from concourse.bass_utils import run_bass_kernel_spmd as _run

    nc = _bacc.Bacc("TRN2", target_bir_lowering=False, num_devices=1)
    arrays, args = {}, []
    for name in _INS:
        a = _np.ascontiguousarray(inputs[name])
        arrays[f"in_{name}_dram"] = a
        args.append(nc.dram_tensor(f"in_{name}_dram", a.shape, _mybir.dt.from_np(a.dtype), kind="ExternalInput").ap())
    args.append(nc.dram_tensor("out_0_dram", (N, D), _mybir.dt.float32, kind="ExternalOutput").ap())
    args.append(nc.dram_tensor("d_rows_dram", (N, D), _mybir.dt.float32).ap())
    graph_network(nc, *args)
    r = _run(nc, [arrays], core_ids=[0])
    return r.results[0]["out_0_dram"]
```

```python
import math
import concourse.bass as bass
from concourse import mybir
from contextlib import ExitStack

N, D, PT, BANK = 2048, 128, 128, 512
NT = N // PT
NQ = N // BANK
TPQ = BANK // PT
H, C = 4, 32
CHEB = 5
TAU = 0.5
LN_EPS = 1e-5
SCALE = 1.0 / math.sqrt(C)
ORDER = [1, 0] + list(range(2, NT))
UNIT = 4
SLOTS = {0: 32, 1: 24, 2: 20, 3: 16, 4: 16, 5: 16}
UNITS = [SLOTS.get(t, 12) // UNIT for t in ORDER]
ALL_UNITS = sum(UNITS)
NSEG = 7
EDGES = [round((k / NSEG) ** 2 * N / 16) * 16 for k in range(NSEG + 1)]
CAND = 8 * NSEG
RING = 4
MASKS = 4
LAG = 2
MASKED = -1.0e30
FLOOR = -1.0e20


def cheb_coeff(k):
    return 2.0 / CHEB * math.exp(-TAU * math.cos(math.pi * (k + 0.5) / CHEB))


class Tally:

    def __init__(self, semaphore):
        self.semaphore, self.count = semaphore, 0

    def step(self, instruction):
        instruction.then_inc(self.semaphore, 1)
        self.count += 1
        return self.count


def graph_network(nc, x, adj, msg_w, msg_b, upd_w, upd_b, ln_w, ln_b, theta, w_msg, b_msg, w_ih, w_hh, b_ih, b_hh,
                  wq, bq, wk, bk, wv, bv, ws, bs, wb, out, d_rows):
    fp32 = mybir.dt.float32
    fp32r = mybir.dt.float32r
    bf16 = mybir.dt.bfloat16
    i32 = mybir.dt.int32
    u32 = mybir.dt.uint32
    ALU = mybir.AluOpType
    ACT = mybir.ActivationFunctionType
    ds = bass.ds

    ctx = ExitStack()
    with ctx:
        def sb(name, shape, dt=fp32):
            return ctx.enter_context(nc.sbuf_tensor(name, shape, dt))

        def sem(name):
            return ctx.enter_context(nc.semaphore(name))

        ident = sb("ident", [PT, PT + 4])
        eye = ident[:, 0:PT]
        psum = ctx.enter_context(nc.psum_tensor("psum", [PT, 8, BANK], fp32))
        cols = sb("cols", [PT, 12])
        msgb_col, updb_col, bmsg_col = cols[:, 0:1], cols[:, 1:2], cols[:, 2:3]
        bih_cols, bhh_cols, brz_cols = cols[:, 3:6], cols[:, 6:9], cols[:, 9:11]
        iota_r = sb("iota_r", [PT, PT])
        rowid = sb("rowid", [PT, NT])
        flags = sb("flags", [PT, NT])
        seg_base = sb("seg_base", [PT, NSEG, 8])
        cand_val = sb("cand_val", [PT, CAND])
        cand_pos = sb("cand_pos", [PT, CAND], u32)
        cand_key = sb("cand_key", [PT, CAND])
        cand_left = sb("cand_left", [PT, CAND])
        picked = sb("picked", [PT, 32])
        scrap = sb("scrap", [PT, 32])
        edge_count = sb("edge_count", [PT, 4])
        keep = sb("keep", [PT, 1])
        weight = sb("weight", [PT, 3, 32])
        column = sb("column", [PT, 3, 32], i32)
        pos = sb("pos", [PT, NT])
        loop_counts = sb("loop_counts", [PT, NT + 1], i32)
        rows_i = sb("rows_i", [PT, 1], i32)
        diag = sb("diag", [PT, 2, UNIT, PT])
        stats = diag[:, 0, 0, 0:6 * NT].rearrange("p (t c) -> p t c", c=6)
        moments = diag[:, 0, 1, 0:2 * NT].rearrange("p (t c) -> p t c", c=2)
        rstd = diag[:, 0, 2, 0:NT]
        pool = sb("pool", [PT, 9, N])
        pool_end = ctx.enter_context(ExitStack())
        adjT = pool_end.enter_context(nc.sbuf_tensor("adjT", [PT, NT, N], fp32))
        pool_end.close()
        qs = sb("q_stack", [PT, H, N], fp32r)
        ks = sb("k_stack", [PT, H, N], fp32r)
        masked = sb("masked_scores", [PT, MASKS, N])
        adj_again = sb("adj_again", [PT, 2, N])
        turned_sb = sb("turned_probs", [PT, 2, N])

        def as_rows(ap):
            return ap.rearrange("p (t d) -> p t d", t=NT)

        def slot(k):
            return pool[:, k, :]

        xT, dT, s_rows, aggT, aggD = slot(0), slot(1), as_rows(slot(2)), slot(3), slot(4)
        x_rows, d_stage = as_rows(slot(3)), as_rows(slot(4))
        adj_in = pool[:, 5:7, :]
        adj_sel, sel_hot, pick_hot = slot(5), as_rows(slot(5)), as_rows(slot(6))
        msgs = slot(7)
        total, loop_f = slot(7)[:, 0:2 * NT], slot(7)[:, 2 * NT:5 * NT]
        msgw_in, wT, msgb_rows = slot(7)[:, 0:256], slot(7)[:, 256:512], slot(7)[:, 512:640]
        prefix_tri, ones_sq = slot(4)[:, 0:128], slot(4)[:, 128:256]
        gath = slot(8).rearrange("p (r k d) -> p r k d", r=RING, k=UNIT)
        agg_sel, half_sum = slot(8)[:, 0:PT], slot(8)[:, PT:PT + 4].rearrange("p (k h) -> p k h", k=2)
        sT_sel, agg_selr = slot(8)[:, 256:384], slot(8)[:, 384:512]
        updw_in, uT = slot(7)[:, 0:256], slot(7)[:, 256:512]
        lnw_rows, lnb_rows = slot(7)[:, 512:640], slot(7)[:, 640:768]
        newT, h_rows, x_again, x1_rows = slot(1), as_rows(slot(2)), as_rows(slot(5)), as_rows(slot(6))
        termT = [slot(0), slot(1), slot(2), slot(0), slot(1)]
        term_rows = [x1_rows, as_rows(slot(3)), as_rows(slot(4)), as_rows(slot(3))]
        theta_in = slot(7)[:, 768:768 + CHEB * PT].rearrange("p (k o) -> p k o", k=CHEB)
        y_rows, x2_rows = as_rows(slot(5)), as_rows(slot(3))
        x2T = slot(0)
        gw_in = slot(8)[:, 0:7 * PT].rearrange("p (g f) -> p g f", g=7)
        gwT = slot(8)[:, 7 * PT:14 * PT].rearrange("p (g f) -> p g f", g=7)
        agg_c, msg_c, r_c, z_c = [slot(1)[:, BANK * i:BANK * i + BANK] for i in range(4)]
        n_c, t_c, u_c, _ = [slot(2)[:, BANK * i:BANK * i + BANK] for i in range(4)]
        u_rows, x3_rows = as_rows(slot(4)), as_rows(slot(5))
        x3T, v_rows, xr_rows, o_rows = slot(0), as_rows(slot(1)), as_rows(slot(2)), as_rows(slot(3))
        w_rep = slot(6)[:, 0:1024].rearrange("p (i h m) -> p i h m", i=2, h=H)
        attw = slot(8)[:, 0:512]
        bvs_rows, wb_rows = slot(8)[:, 512:768], slot(8)[:, 768:1152]
        wb_out, wb_skip = slot(8)[:, 1152:1280], slot(8)[:, 1280:1408]
        turned = [as_rows(turned_sb[:, k, :]) for k in range(2)] + [as_rows(slot(k)) for k in (4, 6, 7, 0)]
        avT, gate_scrap = slot(8)[:, 1408:1536], slot(8)[:, 1536:1664]
        qk_cols = slot(8)[:, 1664:1672]
        row_max = slot(8)[:, 1672:1688].rearrange("p (a b) -> p a b", b=4)
        den = slot(8)[:, 1688:1752].rearrange("p (t h) -> p t h", h=H)
        rden = slot(8)[:, 1752:1760].rearrange("p (a h) -> p a h", h=H)
        skip_dot = slot(8)[:, 1760:1776]
        gate = slot(8)[:, 1776:1792].rearrange("p (a b) -> p a b", b=8)

        s_w, s_x, s_const, s_const2 = sem("message_weights"), sem("x_loaded"), sem("constants"), sem("prefix_consts")
        s_adj = [sem(f"adj_loaded{i}") for i in range(2)]
        s_dve, s_act, s_pool = sem("vector_step"), sem("scalar_step"), sem("gpsimd_step")
        s_xtp, s_xt = sem("x_turned"), sem("x_turned_copied")
        s_sdp, s_sdA, s_sdV, s_dstore = sem("sd_product"), sem("s_copied"), sem("d_copied"), sem("d_rows_stored")
        s_dtp, s_dt = sem("dT_product"), sem("dT_copied")
        s_tp, s_tpc = sem("adj_turned"), sem("adj_turned_copied")
        s_ext, s_count = sem("neighbours_extracted"), sem("nonzeros_counted")
        s_gath = [sem(f"gathered{i}") for i in range(RING)]
        s_add, s_gelu, s_diag, s_unit, s_aggc = sem("s_added"), sem("unit_gelu"), sem("diag_made"), sem("unit_summed"), sem("agg_tile_copied")
        s_flagp, s_counts = sem("flag_prefix"), sem("loop_counts_ready")
        s_hot, s_pickp, s_picki, s_asel = sem("pick_hot"), sem("picked_product"), sem("picked_ready"), sem("adj_rows_gathered")
        s_sel, s_bc, s_mg, s_half = sem("selector"), sem("adj_half_broadcast"), sem("dense_half_gelu"), sem("dense_half_reduced")
        s_dsum, s_dtr, s_dcp, s_dout, s_dacc = sem("dense_sum"), sem("dense_turned"), sem("dense_turned_copied"), sem("dense_scattered"), sem("dense_accumulated")
        s_dense, s_zero, s_iota, s_stsel, s_hc, s_held = sem("dense_done"), sem("sums_cleared"), sem("iota_moved"), sem("picked_s"), sem("h_copied"), sem("waits_held")
        s_w2, s_utp, s_ut = sem("update_weights"), sem("upd_w_turned"), sem("upd_w_copied")
        s_newp, s_newg, s_newx = sem("new_feats_product"), sem("new_feats_gelu"), sem("new_feats_plus_x")
        s_rowp = sem("h_turned")
        s_ln, s_ln2 = sem("layernorm_variance"), sem("layernorm_sqrt")
        s_x1, s_x2, s_x3 = sem("x1_ready"), sem("x2_ready"), sem("x3_ready")
        s_tnp, s_tnc = sem("turned_psum"), sem("turned_copied")
        s_th, s_ths = sem("theta_loaded"), sem("theta_scaled")
        s_hopp, s_hopc, s_chp = sem("hop_product"), sem("hop_copied"), sem("cheb_sum")
        s_gwl, s_gwp, s_gwc, s_gb = sem("gru_weights"), sem("gru_weights_turned"), sem("gru_weights_copied"), sem("gru_bias")
        s_agg2p, s_agg2, s_msgp, s_msg = sem("agg2_product"), sem("agg2_copied"), sem("msg_product"), sem("msg_ready")
        s_gate, s_gact, s_pre, s_tanh, s_cell = sem("gates_product"), sem("gates_ready"), sem("candidate_sum"), sem("candidate_ready"), sem("cell_ready")
        s_utn, s_utc = sem("u_turned"), sem("u_turned_copied")
        s_rep, s_aw, s_prp, s_hi, s_lo = sem("weights_repeated"), sem("att_weights"), sem("projection"), sem("stack_high"), sem("stack_low")
        s_vp, s_vc, s_wbs = sem("value_product"), sem("value_copied"), sem("gate_weights")
        s_adj2 = [sem(f"adj_again{i}") for i in range(2)]
        s_pen, s_scp, s_mask, s_bias, s_exp = sem("penalty"), sem("scores"), sem("masked_half"), sem("exp_bias"), sem("exp_done")
        s_etp, s_etA, s_etV = sem("probs_turned"), sem("turned_by_scalar"), sem("turned_by_vector")
        s_avp, s_avc, s_avt, s_o = sem("av_product"), sem("av_copied"), sem("av_turned"), sem("out_rows")
        s_gz, s_ge, s_gd = sem("gate_dot"), sem("gate_exp"), sem("gated")
        s_fin, s_out = sem("result_ready"), sem("output_written")
        block = ctx.enter_context(nc.Block())

        def hold(engine, semaphore, value):
            engine.wait_ge(semaphore, value)
            engine.sem_inc(s_held, 1)

        def turned_copy(n):
            step, q = divmod(n, NQ)
            share = 2 + step % 2
            if q < share:
                return s_etA, 5 * (step // 2) + 2 * (step % 2) + q + 1
            return s_etV, 3 * (step // 2) + 2 * (step % 2) + q - share + 1

        def turned_free(step):
            return (step - len(turned)) // H

        def all_rows(dram):
            return dram.rearrange("(t p) d -> p t d", p=PT)

        def column_of(dram):
            return dram.rearrange("(p o) -> p o", o=1)

        @block.sync
        def _(sp):
            sp.dma_start(msgw_in, msg_w).then_inc(s_w, 16)
            sp.dma_start(msgb_rows, msg_b.partition_broadcast(PT)).then_inc(s_w, 16)
            sp.dma_start(msgb_col, column_of(msg_b)).then_inc(s_w, 16)
            sp.dma_start(x_rows, all_rows(x)).then_inc(s_x, 16)
            for s in range(NT):
                t = ORDER[s]
                if s >= 2:
                    sp.wait_ge(s_tp, NQ * (s - 1))
                    sp.wait_ge(s_ext, s - 1)
                sp.dma_start(adj_in[:, s % 2, :], adj[t * PT:(t + 1) * PT, :]).then_inc(s_adj[s % 2], 16)
                if s == 1:
                    sp.wait_ge(s_sdV, NT // 2)
                    sp.dma_start(all_rows(d_rows), d_stage).then_inc(s_dstore, 16)
            sp.wait_ge(s_dense, 1)
            sp.dma_start(updw_in, upd_w).then_inc(s_w2, 16)
            sp.dma_start(updb_col, column_of(upd_b)).then_inc(s_w2, 16)
            sp.dma_start(lnw_rows, ln_w.partition_broadcast(PT)).then_inc(s_w2, 16)
            sp.dma_start(lnb_rows, ln_b.partition_broadcast(PT)).then_inc(s_w2, 16)
            sp.dma_start(x_again, all_rows(x)).then_inc(s_w2, 16)
            sp.dma_start(theta_in, theta.rearrange("k i o -> i k o")).then_inc(s_th, 16)
            sp.dma_start(gw_in[:, 0, :], w_msg).then_inc(s_gwl, 16)
            sp.dma_start(gw_in[:, 1:4, :], w_ih.rearrange("(g p) f -> p g f", p=PT)).then_inc(s_gwl, 16)
            sp.dma_start(gw_in[:, 4:7, :], w_hh.rearrange("(g p) f -> p g f", p=PT)).then_inc(s_gwl, 16)
            sp.dma_start(bmsg_col, column_of(b_msg)).then_inc(s_gwl, 16)
            sp.dma_start(bih_cols, b_ih.rearrange("(g p) -> p g", p=PT), allow_slow_non_contiguous=True).then_inc(s_gwl, 16)
            sp.dma_start(bhh_cols, b_hh.rearrange("(g p) -> p g", p=PT), allow_slow_non_contiguous=True).then_inc(s_gwl, 16)
            sp.wait_ge(s_x3, 1)
            for i, w in enumerate((wq, wk, wv, ws)):
                sp.dma_start(attw[:, PT * i:PT * i + PT], w).then_inc(s_aw, 16)
            sp.dma_start(bvs_rows[:, 0:PT], bv.partition_broadcast(PT)).then_inc(s_aw, 16)
            sp.dma_start(bvs_rows[:, PT:2 * PT], bs.partition_broadcast(PT)).then_inc(s_aw, 16)
            sp.dma_start(wb_rows, wb.rearrange("k o -> (k o)").partition_broadcast(PT)).then_inc(s_aw, 16)
            for r in range(4):
                for i, b in enumerate((bq, bk)):
                    sp.dma_start(qk_cols[C * r:C * r + C, H * i:H * i + H], b.rearrange("(h c) -> c h", c=C),
                                 allow_slow_non_contiguous=True).then_inc(s_aw, 16)
            for t in range(NT):
                if t >= 2:
                    sp.wait_ge(s_mask, 2 * H * (t - 1))
                sp.dma_start(adj_again[:, t % 2, :], adj[t * PT:(t + 1) * PT, :]).then_inc(s_adj2[t % 2], 16)
            sp.wait_ge(s_fin, 1)
            sp.dma_start(all_rows(out), o_rows).then_inc(s_out, 16)
            sp.wait_ge(s_out, 16)

        @block.gpsimd
        def _(gp):
            gp.memset(ident[:, :], 0.0).then_inc(s_pool, 1)
            gp.wait_ge(s_pool, 1)
            gp.affine_select(out=ident[:, :], in_=ident[:, :], compare_op=ALU.not_equal, fill=1.0,
                             base=0, pattern=[[-1, PT + 4]], channel_multiplier=1).then_inc(s_const, 1)
            gp.iota(iota_r[:, :], pattern=[[1, PT]], base=0, channel_multiplier=0,
                    allow_small_or_imprecise_dtypes=True).then_inc(s_const, 1)
            gp.iota(rowid[:, :], pattern=[[PT, NT]], base=0, channel_multiplier=1,
                    allow_small_or_imprecise_dtypes=True).then_inc(s_const, 1)
            for g in range(NSEG):
                ins = gp.memset(seg_base[:, g, :], EDGES[g] + 1.0)
            ins.then_inc(s_const, 1)
            gp.wait_ge(s_dstore, 16)
            gp.memset(ones_sq, 1.0).then_inc(s_const2, 1)
            gp.memset(prefix_tri, 1.0).then_inc(s_const2, 1)
            gp.wait_ge(s_const2, 2)
            gp.affine_select(out=prefix_tri, in_=prefix_tri, compare_op=ALU.is_gt, fill=0.0,
                             base=0, pattern=[[1, PT]], channel_multiplier=-1).then_inc(s_const2, 1)
            u = 0
            for s in range(NT):
                gp.wait_ge(s_ext, s + 1)
                for v in range(UNITS[s]):
                    if u >= RING:
                        gp.wait_ge(s_unit, u - RING + 1)
                    for j in range(UNIT):
                        k = UNIT * v + j
                        gp.indirect_dma_start(
                            out=gath[:, u % RING, j, :], out_offset=None, in_=d_rows,
                            in_offset=bass.IndirectOffsetOnAxis(ap=column[:, s % 3, k:k + 1], axis=0)
                        ).then_inc(s_gath[u % RING], 16)
                    u += 1
            gp.wait_ge(s_counts, 1)
            batches = gp.value_load(loop_counts[0:1, NT:NT + 1], min_val=1, max_val=NT)
            with gp.Fori(0, batches) as b:
                hold(gp, s_picki, b + 1)
                gp.indirect_dma_start(out=adj_sel, out_offset=None, in_=adj,
                                      in_offset=bass.IndirectOffsetOnAxis(ap=rows_i[:, 0:1], axis=0)).then_inc(s_asel, 16)
            gp.wait_ge(s_aw, 16 * 15)
            for i in range(2):
                source = attw[:, PT * i:PT * i + PT].rearrange("p (h o c) -> p h o c", h=H, o=1)
                gp.tensor_copy(w_rep[:, i].rearrange("p h (r c) -> p h r c", r=4),
                               source.to_broadcast([PT, H, 4, C])).then_inc(s_rep, 1)
            for t in range(NT):
                gp.wait_ge(s_adj2[t % 2], 16 * (t // 2 + 1))
                gp.tensor_scalar(adj_again[:, t % 2, :], adj_again[:, t % 2, :], 0.0, MASKED,
                                 ALU.is_equal, ALU.mult).then_inc(s_pen, 1)

        @block.tensor
        def _(pe):
            pe.wait_ge(s_const, 1)
            pe.wait_ge(s_w, 48)
            pe.transpose(psum[:, 0, 0:PT], msgw_in[:, 0:PT], eye)
            pe.transpose(psum[:, 0, PT:2 * PT], msgw_in[:, PT:2 * PT], eye).then_inc(s_xtp, 1)
            pe.wait_ge(s_x, 16)
            for q in range(NQ):
                for j in range(TPQ):
                    ins = pe.transpose(psum[:, 1 + q, PT * j:PT * j + PT], x_rows[:, TPQ * q + j, :], eye)
                ins.then_inc(s_xtp, 1)
            for g in range(NT // 2):
                pe.wait_ge(s_xt, 2 + g // 2)
                if g >= 2:
                    pe.wait_ge(s_sdA, g - 1)
                    pe.wait_ge(s_sdV, g - 1)
                for j in range(2):
                    t = 2 * g + j
                    ins = pe.matmul(psum[:, 5 + g % 2, 256 * j:256 * j + 256], xT[:, PT * t:PT * t + PT], wT,
                                    start=True, stop=True)
                ins.then_inc(s_sdp, 1)
            for q in range(NQ):
                pe.matmul(psum[:, 1 + q, :], wT[:, PT:2 * PT], xT[:, BANK * q:BANK * q + BANK],
                          start=True, stop=True).then_inc(s_dtp, 1)

            def turn_adj(s):
                pe.wait_ge(s_adj[s % 2], 16 * (s // 2 + 1))
                for q in range(NQ):
                    n = NQ * s + q
                    if n >= 2:
                        pe.wait_ge(s_tpc, n - 1)
                    else:
                        pe.wait_ge(s_dt, 4)
                    for j in range(TPQ):
                        m = TPQ * q + j
                        ins = pe.transpose(psum[:, n % 2, PT * j:PT * j + PT],
                                           adj_in[:, s % 2, PT * m:PT * m + PT], eye)
                    ins.then_inc(s_tp, 1)

            unit = 0
            for s in range(NT + 1):
                if s < NT:
                    turn_adj(s)
                if s == 0:
                    continue
                if s == NT:
                    pe.wait_ge(s_ext, NT)
                    pe.wait_ge(s_const2, 3)
                    pe.matmul(psum[:, 4, 0:NT], prefix_tri, flags[:, :], start=True, stop=True)
                    pe.matmul(psum[:, 4, NT:2 * NT], ones_sq, flags[:, :], start=True, stop=True).then_inc(s_flagp, 1)
                if s >= 3:
                    pe.wait_ge(s_aggc, s - 2)
                for v in range(UNITS[s - 1]):
                    pe.wait_ge(s_gelu, unit + 1)
                    pe.wait_ge(s_diag, unit + 1)
                    for j in range(UNIT):
                        k = UNIT * v + j
                        ins = pe.matmul(psum[:, 2 + s % 2, 0:PT], gath[:, unit % RING, j, :], diag[:, unit % 2, j, :],
                                        start=k == 0, stop=k == UNIT * UNITS[s - 1] - 1)
                    ins.then_inc(s_unit, 1)
                    unit += 1
            pe.wait_ge(s_counts, 1)
            batches = pe.value_load(loop_counts[0:1, NT:NT + 1], min_val=1, max_val=NT)
            pe.wait_ge(s_aggc, NT)
            with pe.Fori(0, batches) as b:
                pairs = pe.value_load(loop_counts[0:1, ds(b, 1)], min_val=1, max_val=PT // 2)
                hold(pe, s_hot, b + 1)
                for t in range(NT):
                    pe.matmul(psum[:, 2, 0:1], pick_hot[:, t, :], rowid[:, t:t + 1], start=t == 0, stop=t == NT - 1)
                for t in range(NT):
                    ins = pe.matmul(psum[:, 3, 0:PT], s_rows[:, t, :], pick_hot[:, t, :], start=t == 0, stop=t == NT - 1)
                ins.then_inc(s_pickp, 1)
                hold(pe, s_asel, 16 * b + 16)
                with pe.Fori(0, pairs) as r:
                    for k in range(2):
                        row = b * PT + r * 2 + k
                        hold(pe, s_sel, row + 1 + b * 2)
                        for h in range(2):
                            hold(pe, s_half, row * 2 + h + 1)
                            for j in range(2):
                                ins = pe.matmul(psum[:, 4 + 2 * h + j, :], diag[:, 0, k, :],
                                                adj_sel[:, 1024 * h + BANK * j:1024 * h + BANK * j + BANK],
                                                start=True, stop=True)
                            ins.then_inc(s_bc, 1)
                hold(pe, s_dsum, b * PT + pairs * 2)
                pe.transpose(psum[:, 2, 0:PT], agg_sel, eye)
                for t in range(NT):
                    ins = pe.transpose(psum[:, 4 + t // TPQ, PT * (t % TPQ):PT * (t % TPQ) + PT], pick_hot[:, t, :], eye)
                ins.then_inc(s_dtr, 1)
                hold(pe, s_dcp, b * 2 + 2)
                for q in range(NQ):
                    ins = pe.matmul(psum[:, 4 + q, :], agg_selr, sel_hot[:, TPQ * q:TPQ * q + TPQ, :],
                                    start=True, stop=True)
                ins.then_inc(s_dout, 1)
            pe.wait_ge(s_dense, 1)
            pe.wait_ge(s_w2, 80)
            pe.transpose(psum[:, 0, 0:PT], updw_in[:, 0:PT], eye)
            pe.transpose(psum[:, 0, PT:2 * PT], updw_in[:, PT:2 * PT], eye).then_inc(s_utp, 1)
            pe.wait_ge(s_ut, 1)
            for q in range(NQ):
                part = slice(BANK * q, BANK * q + BANK)
                pe.matmul(psum[:, 4 + q, :], uT[:, 0:PT], xT[:, part], start=True, stop=False)
                pe.matmul(psum[:, 4 + q, :], uT[:, PT:2 * PT], aggT[:, part], start=False, stop=False)
                pe.matmul(psum[:, 4 + q, :], uT[:, PT:2 * PT], aggD[:, part], start=False, stop=True).then_inc(s_newp, 1)
            for q in range(NQ):
                pe.wait_ge(s_newx, q + 1)
                for j in range(TPQ):
                    t = TPQ * q + j
                    ins = pe.transpose(psum[:, q, PT * j:PT * j + PT], newT[:, PT * t:PT * t + PT], eye)
                ins.then_inc(s_rowp, 1)

            turn = [0]

            def turn_chunk(source):
                n = turn[0]
                if n >= 2:
                    pe.wait_ge(s_tnc, n - 1)
                for j in range(TPQ):
                    ins = pe.transpose(psum[:, 6 + n % 2, PT * j:PT * j + PT], source(j), eye)
                ins.then_inc(s_tnp, 1)
                turn[0] += 1

            def theta_product(k, q):
                for j in range(TPQ):
                    t = TPQ * q + j
                    ins = pe.matmul(psum[:, q, PT * j:PT * j + PT], termT[k][:, PT * t:PT * t + PT], theta_in[:, k, :],
                                    start=k == 0 and j == 0, stop=k == CHEB - 1, skip_group_check=True)
                return ins

            pe.wait_ge(s_x1, 1)
            for q in range(NQ):
                turn_chunk(lambda j: x1_rows[:, TPQ * q + j, :])
            pe.wait_ge(s_ths, 1)
            for q in range(NQ):
                pe.wait_ge(s_tnc, q + 1)
                theta_product(0, q)

            def finish_chunk(k, q):
                pe.wait_ge(s_hopc, NQ * (k - 1) + q + 1)
                if k < CHEB - 1:
                    turn_chunk(lambda j: termT[k][:, PT * (TPQ * q + j):PT * (TPQ * q + j) + PT])
                ins = theta_product(k, q)
                if k == CHEB - 1:
                    ins.then_inc(s_chp, 1)

            for k in range(1, CHEB):
                for q in range(NQ):
                    n = NQ * (k - 1) + q
                    if n >= 2:
                        pe.wait_ge(s_hopc, n - 1)
                    for m in range(NT):
                        if q == 0 and k > 1 and m % TPQ == 0:
                            pe.wait_ge(s_tnc, NQ * (k - 1) + m // TPQ + 1)
                        ins = pe.matmul(psum[:, 4 + n % 2, :], term_rows[k - 1][:, m, :],
                                        adjT[:, m, BANK * q:BANK * q + BANK], start=m == 0, stop=m == NT - 1)
                    ins.then_inc(s_hopp, 1)
                    if q >= 1:
                        finish_chunk(k, q - 1)
                finish_chunk(k, NQ - 1)

            pe.wait_ge(s_gwl, 96)
            pe.wait_ge(s_x2, 1)
            for g in range(7):
                ins = pe.transpose(psum[:, g // TPQ, PT * (g % TPQ):PT * (g % TPQ) + PT], gw_in[:, g, :], eye)
            ins.then_inc(s_gwp, 1)
            for q in range(NQ):
                turn_chunk(lambda j: x2_rows[:, TPQ * q + j, :])

            def hop2(q, ms):
                if ms[0] == 0 and q >= 2:
                    pe.wait_ge(s_agg2, q - 1)
                for m in ms:
                    ins = pe.matmul(psum[:, 4 + q % 2, :], x2_rows[:, m, :], adjT[:, m, BANK * q:BANK * q + BANK],
                                    start=m == 0, stop=m == NT - 1)
                if ms[-1] == NT - 1:
                    ins.then_inc(s_agg2p, 1)

            def message(q):
                if q == 0:
                    pe.wait_ge(s_gwc, 2)
                    pe.wait_ge(s_tnc, turn[0])
                pe.wait_ge(s_agg2, q + 1)
                if q >= 1:
                    pe.wait_ge(s_msg, q)
                pe.matmul(psum[:, 6, :], gwT[:, 0, :], agg_c, start=True, stop=True).then_inc(s_msgp, 1)

            def gates(q):
                part = x2T[:, BANK * q:BANK * q + BANK]
                pe.wait_ge(s_msg, q + 1)
                if q >= 1:
                    pe.wait_ge(s_pre, q)
                for g in range(2):
                    pe.matmul(psum[:, g, :], gwT[:, 1 + g, :], msg_c, start=True, stop=False)
                    pe.matmul(psum[:, g, :], gwT[:, 4 + g, :], part, start=False, stop=True)
                pe.matmul(psum[:, 2, :], gwT[:, 3, :], msg_c, start=True, stop=True)
                pe.matmul(psum[:, 3, :], gwT[:, 6, :], part, start=True, stop=True).then_inc(s_gate, 1)

            def turn_u(q):
                pe.wait_ge(s_cell, q + 1)
                if q >= 1:
                    pe.wait_ge(s_utc, q)
                for j in range(TPQ):
                    ins = pe.transpose(psum[:, 7, PT * j:PT * j + PT], u_c[:, PT * j:PT * j + PT], eye)
                ins.then_inc(s_utn, 1)

            for q in range(NQ + 2):
                if q < NQ:
                    hop2(q, range(0, NT // 2))
                if 1 <= q <= NQ:
                    message(q - 1)
                if q >= 2:
                    turn_u(q - 2)
                if q < NQ:
                    hop2(q, range(NT // 2, NT))
                if 1 <= q <= NQ:
                    gates(q - 1)

            pe.wait_ge(s_x3, 1)
            for q in range(NQ):
                turn_chunk(lambda j: x3_rows[:, TPQ * q + j, :])
            pe.wait_ge(s_rep, 2)
            n = 0
            for i in range(2):
                for h in range(H):
                    for q in range(NQ):
                        if i == 0 and h == 0:
                            pe.wait_ge(s_tnc, turn[0] - NQ + q + 1)
                        if n >= 4:
                            pe.wait_ge(s_lo, n - 3)
                        pe.matmul(psum[:, n % 4, :], w_rep[:, i, h, :], x3T[:, BANK * q:BANK * q + BANK],
                                  start=True, stop=True).then_inc(s_prp, 1)
                        n += 1
            for g in range(NT // 2):
                if g >= 2:
                    pe.wait_ge(s_vc, g - 1)
                for j in range(2):
                    t = 2 * g + j
                    ins = pe.matmul(psum[:, 4 + g % 2, 256 * j:256 * j + 256], x3T[:, PT * t:PT * t + PT],
                                    attw[:, 2 * PT:4 * PT], start=True, stop=True)
                ins.then_inc(s_vp, 1)

            def scores(i):
                t, h = divmod(i, H)
                for a in range(2):
                    if i >= 1:
                        pe.wait_ge(s_mask, 2 * (i - 1) + a + 1)
                    for j in range(2):
                        ins = pe.matmul(psum[:, 2 * a + j, :], qs[:, h, PT * t:PT * t + PT],
                                        ks[:, h, 1024 * a + BANK * j:1024 * a + BANK * j + BANK], start=True, stop=True)
                    ins.then_inc(s_scp, 1)

            def turn_probs(i):
                pe.wait_ge(s_exp, i + 1)
                for q in range(NQ):
                    n = NQ * i + q
                    if n >= 3:
                        pe.wait_ge(*turned_copy(n - 3))
                    for j in range(TPQ):
                        m = TPQ * q + j
                        ins = pe.transpose(psum[:, 4 + n % 3, PT * j:PT * j + PT], masked[:, i % MASKS, PT * m:PT * m + PT], eye)
                    ins.then_inc(s_etp, 1)

            def values(t):
                pe.wait_ge(s_etA, 5 * H // 2 * (t + 1))
                pe.wait_ge(s_etV, 3 * H // 2 * (t + 1))
                if t >= 1:
                    pe.wait_ge(s_o, t)
                for m in range(NT):
                    for h in range(H):
                        ins = pe.matmul(psum[C * h:C * h + C, 7, 0:PT], v_rows[:, m, C * h:C * h + C],
                                        turned[(H * t + h) % len(turned)][:, m, :], start=m == 0, stop=m == NT - 1)
                ins.then_inc(s_avp, 1)

            def turn_values(t):
                pe.wait_ge(s_avc, t + 1)
                if t >= 1:
                    pe.wait_ge(s_o, t)
                pe.transpose(psum[:, 7, PT:2 * PT], avT, eye).then_inc(s_avt, 1)

            pe.wait_ge(s_vc, NT // 2)
            pe.wait_ge(s_lo, 32)
            steps = NT * H
            for i in range(steps + LAG + 2):
                if i < steps:
                    scores(i)
                ended, h = divmod(i - LAG - 1, H)
                if h == H - 1 and ended >= 0:
                    values(ended)
                if LAG <= i < steps + LAG:
                    turn_probs(i - LAG)
                if h == H - 1 and ended >= 0:
                    turn_values(ended)

        @block.vector
        def _(ve):
            tally = Tally(s_dve)

            def settle(ins):
                ve.wait_ge(s_dve, tally.step(ins))

            def layernorm(turn, source, target, ready):
                for t in range(NT):
                    ins = ve.bn_stats(stats[:, t, :], source[:, t, :])
                settle(ins)
                for t in range(NT):
                    ins = ve.bn_aggr(moments[:, t, :], stats[:, t, :])
                settle(ins)
                ve.tensor_scalar(rstd, moments[:, :, 1], LN_EPS, None, ALU.add).then_inc(s_ln, 1)
                ve.wait_ge(s_ln2, turn + 1)
                settle(ve.reciprocal(rstd, rstd))
                for t in range(NT):
                    ins = ve.tensor_scalar(target[:, t, :], source[:, t, :], moments[:, t, 0:1], rstd[:, t:t + 1],
                                           ALU.subtract, ALU.mult)
                if ready is None:
                    settle(ins)
                else:
                    ins.then_inc(ready, 1)
                    ve.wait_ge(ready, 1)

            def extract(s, feed):
                t, a, r = ORDER[s], adj_in[:, s % 2, :], s % 3
                slots = UNIT * UNITS[s]
                scratch = slot(8) if s == 0 else msgs
                here = edge_count[:, s % 2:s % 2 + 1]
                found = edge_count[:, 2 + s % 2:3 + s % 2]
                ve.wait_ge(s_adj[s % 2], 16 * (s // 2 + 1))
                for g in range(NSEG):
                    ins = ve.max(cand_val[:, 8 * g:8 * g + 8], a[:, EDGES[g]:EDGES[g + 1]])
                settle(ins)
                for g in range(NSEG):
                    ins = ve.max_index(cand_pos[:, 8 * g:8 * g + 8], cand_val[:, 8 * g:8 * g + 8],
                                       a[:, EDGES[g]:EDGES[g + 1]])
                settle(ins)
                feed()
                settle(ve.tensor_tensor(cand_left[:, :], cand_pos[:, :], seg_base.rearrange("p g e -> p (g e)"), ALU.add))
                settle(ve.scalar_tensor_tensor(cand_key[:, :], cand_val[:, :], 0.0, cand_left[:, :], ALU.is_gt, ALU.mult))
                source = cand_key
                for k in range(0, slots, 8):
                    eight = picked[:, k:k + 8]
                    settle(ve.max(eight, source[:, :]))
                    if k + 8 < slots:
                        settle(ve.match_replace(cand_left[:, :], eight, source[:, :], 0.0))
                        source = cand_left
                for k in range(slots):
                    ve.scalar_tensor_tensor(scratch[:, CAND * k:CAND * k + CAND], cand_key[:, :], picked[:, k:k + 1],
                                            cand_val[:, :], ALU.is_equal, ALU.mult, accum_out=weight[:, r, k:k + 1])
                settle(ve.tensor_scalar(scrap[:, 0:slots], picked[:, 0:slots], 0.0, None, ALU.is_gt, ALU.add,
                                        accum_out=found))
                if s:
                    feed()
                ve.wait_ge(s_count, s + 1)
                ve.tensor_tensor(flags[:, t:t + 1], here, found, ALU.not_equal)
                settle(ve.tensor_tensor(keep[:, :], here, found, ALU.is_equal))
                settle(ve.tensor_scalar(weight[:, r, 0:slots], weight[:, r, 0:slots], keep[:, 0:1], None, ALU.mult))
                ve.tensor_scalar(column[:, r, 0:slots], picked[:, 0:slots], 1.0, 1.0, ALU.max,
                                 ALU.subtract).then_inc(s_ext, 1)

            def d_with_bias():
                ve.wait_ge(s_w, 48)
                for g in range(NT // 2):
                    ve.wait_ge(s_sdA, g + 1)
                    both = psum[:, 5 + g % 2, :].rearrange("p (j c) -> p j c", j=2)
                    ve.tensor_tensor(d_stage[:, 2 * g:2 * g + 2, :], both[:, :, PT:2 * PT],
                                     msgb_rows.rearrange("p (o d) -> p o d", o=1).to_broadcast([PT, 2, PT]),
                                     ALU.add).then_inc(s_sdV, 1)

            def feed_unit(u, s):
                t = ORDER[s]
                ve.wait_ge(s_gath[u % RING], 16 * UNIT * (u // RING + 1))
                ve.tensor_tensor(gath[:, u % RING, :, :], gath[:, u % RING, :, :],
                                 s_rows[:, t:t + 1, :].to_broadcast([PT, UNIT, PT]), ALU.add).then_inc(s_add, 1)

            unit = [0]

            def feeder(s):
                def feed():
                    feed_unit(unit[0], s)
                    unit[0] += 1
                return feed

            ve.wait_ge(s_const, 4)
            extract(0, d_with_bias)
            ve.wait_ge(s_dtp, 4)
            for s in range(1, NT):
                extract(s, feeder(s - 1))
                for v in range(UNITS[s - 1] - 2):
                    feeder(s - 1)()
            ve.wait_ge(s_flagp, 1)
            settle(ve.tensor_copy(total[:, :], psum[:, 4, 0:2 * NT]))
            cum = loop_f[:, 0:NT]
            settle(ve.tensor_tensor_scan(cum, ones_sq[:, 0:NT], total[:, NT:2 * NT], 0.0, ALU.mult, ALU.add))
            settle(ve.tensor_tensor(pos[:, :], cum, total[:, NT:2 * NT], ALU.subtract))
            settle(ve.tensor_tensor(pos[:, :], pos[:, :], total[:, 0:NT], ALU.add))
            settle(ve.scalar_tensor_tensor(pos[:, :], pos[:, :], 1.0, flags[:, :], ALU.add, ALU.mult))
            settle(ve.tensor_scalar(pos[:, :], pos[:, :], -1.0, None, ALU.add))
            left = loop_f[0:1, NT:2 * NT]
            settle(ve.tensor_scalar(left, rowid[0:1, :], -1.0, loop_f[0:1, NT - 1:NT], ALU.mult, ALU.add))
            settle(ve.tensor_scalar(loop_f[0:1, 2 * NT:3 * NT], left, 0.0, None, ALU.is_gt, ALU.add,
                                    accum_out=edge_count[0:1, 0:1]))
            ve.tensor_scalar(loop_counts[0:1, NT:NT + 1], edge_count[0:1, 0:1], 1.0, None, ALU.max)
            settle(ve.tensor_scalar(left, left, 1.0, 2.0, ALU.add, ALU.max))
            settle(ve.tensor_scalar(loop_counts[0:1, 0:NT], left, PT + 1.0, None, ALU.min))
            ve.tensor_scalar(loop_counts[0:1, 0:NT], loop_counts[0:1, 0:NT], 1, None,
                             ALU.arith_shift_right).then_inc(s_counts, 1)
            ve.memset(aggD[:, 0:N // 2], 0.0).then_inc(s_half, 1)
            ve.memset(aggD[:, N // 2:N], 0.0).then_inc(s_half, 1)
            ve.wait_ge(s_half, 2)
            ve.wait_ge(s_counts, 1)
            for v in range(UNITS[NT - 1]):
                feeder(NT - 1)()
            ve.wait_ge(s_aggc, NT)
            flat = psum.rearrange("p b n -> p (b n)")
            batches = ve.value_load(loop_counts[0:1, NT:NT + 1], min_val=1, max_val=NT)
            with ve.Fori(0, batches) as b:
                pairs = ve.value_load(loop_counts[0:1, ds(b, 1)], min_val=1, max_val=PT // 2)
                ve.tensor_tensor(pick_hot, pos.rearrange("p (t o) -> p t o", o=1).to_broadcast([PT, NT, PT]),
                                 iota_r.rearrange("p (o r) -> p o r", o=1).to_broadcast([PT, NT, PT]),
                                 ALU.is_equal).then_inc(s_hot, 1)
                ve.memset(agg_sel, 0.0).then_inc(s_zero, 1)
                hold(ve, s_hot, b + 1)
                ve.tensor_scalar(iota_r[:, :], iota_r[:, :], float(PT), None, ALU.add).then_inc(s_iota, 1)
                hold(ve, s_pickp, b + 1)
                ve.tensor_copy(rows_i[:, :], psum[:, 2, 0:1]).then_inc(s_picki, 1)
                ve.tensor_copy(sT_sel, psum[:, 3, 0:PT]).then_inc(s_stsel, 1)
                for k in range(2):
                    ve.tensor_copy(diag[:, 0, k, :], ident[:, k:k + 1].to_broadcast([PT, PT])).then_inc(s_sel, 1)
                hold(ve, s_zero, b + 1)
                with ve.Fori(0, pairs) as r:
                    for k in range(2):
                        row = b * PT + r * 2 + k
                        for h in range(2):
                            half = msgs[:, 1024 * h:1024 * h + 1024]
                            hold(ve, s_mg, row * 2 + h + 1)
                            hold(ve, s_bc, row * 2 + h + 1)
                            ve.tensor_tensor_reduce(half, half, flat[:, 2048 + 1024 * h:2048 + 1024 * h + 1024], 1.0, 0.0,
                                                    ALU.mult, ALU.add, half_sum[:, k, h:h + 1]).then_inc(s_half, 1)
                        hold(ve, s_half, row * 2 + 4)
                        ve.tensor_tensor(agg_sel[:, ds(r * 2 + k, 1)], half_sum[:, k, 0:1], half_sum[:, k, 1:2],
                                         ALU.add).then_inc(s_dsum, 1)
                        ve.tensor_copy(diag[:, 0, k, :],
                                       ident[:, ds(r * 2 + k + 2, 1)].to_broadcast([PT, PT])).then_inc(s_sel, 1)
                hold(ve, s_dtr, b + 1)
                ve.tensor_copy(agg_selr, psum[:, 2, 0:PT]).then_inc(s_dcp, 1)
                ve.tensor_copy(slot(5), flat[:, 2048:4096]).then_inc(s_dcp, 1)
                hold(ve, s_dout, b + 1)
                ve.tensor_tensor(aggD, aggD, flat[:, 2048:4096], ALU.add).then_inc(s_dacc, 1)
                hold(ve, s_dacc, b + 1)
                hold(ve, s_iota, b + 1)
            ve.memset(edge_count[:, :], 0.0).then_inc(s_dense, 1)
            for q in range(NQ):
                part = slice(BANK * q, BANK * q + BANK)
                ve.wait_ge(s_newg, q + 1)
                ve.tensor_tensor(newT[:, part], newT[:, part], xT[:, part], ALU.add).then_inc(s_newx, 1)
            ve.wait_ge(s_hc, NQ)
            layernorm(0, h_rows, h_rows, None)
            ve.wait_ge(s_w2, 80)
            settle(ve.tensor_tensor(h_rows, h_rows, lnw_rows.rearrange("p (o d) -> p o d", o=1).to_broadcast([PT, NT, PT]),
                                    ALU.mult))
            settle(ve.tensor_tensor(h_rows, h_rows, lnb_rows.rearrange("p (o d) -> p o d", o=1).to_broadcast([PT, NT, PT]),
                                    ALU.add))
            settle(ve.tensor_tensor(h_rows, h_rows, x_again, ALU.add))
            layernorm(1, h_rows, x1_rows, s_x1)

            ve.wait_ge(s_th, 16)
            for k in range(CHEB):
                ins = ve.tensor_scalar(theta_in[:, k, :], theta_in[:, k, :], cheb_coeff(k), None, ALU.mult)
            ins.then_inc(s_ths, 1)
            for k in range(1, CHEB):
                for q in range(NQ):
                    n = NQ * (k - 1) + q
                    part = slice(BANK * q, BANK * q + BANK)
                    ve.wait_ge(s_hopp, n + 1)
                    if k == 1:
                        ve.tensor_copy(termT[1][:, part], psum[:, 4 + n % 2, :]).then_inc(s_hopc, 1)
                    else:
                        ve.scalar_tensor_tensor(termT[k][:, part], psum[:, 4 + n % 2, :], 2.0, termT[k - 2][:, part],
                                                ALU.mult, ALU.subtract).then_inc(s_hopc, 1)
            for q in range(NQ):
                ve.wait_ge(s_chp, q + 1)
                ins = ve.tensor_tensor(slot(5)[:, BANK * q:BANK * q + BANK], psum[:, q, :],
                                       slot(6)[:, BANK * q:BANK * q + BANK], ALU.add)
            settle(ins)
            layernorm(2, y_rows, x2_rows, s_x2)

            ve.wait_ge(s_gwl, 96)
            ve.tensor_tensor(brz_cols, bih_cols[:, 0:2], bhh_cols[:, 0:2], ALU.add).then_inc(s_gb, 1)
            for q in range(NQ):
                part = x2T[:, BANK * q:BANK * q + BANK]
                ve.wait_ge(s_gact, 2 * q + 2)
                settle(ve.scalar_tensor_tensor(t_c, psum[:, 3, :], bhh_cols[:, 2:3], r_c, ALU.add, ALU.mult))
                ve.tensor_tensor(t_c, psum[:, 2, :], t_c, ALU.add).then_inc(s_pre, 1)
                ve.wait_ge(s_tanh, q + 1)
                settle(ve.tensor_tensor(t_c, part, n_c, ALU.subtract))
                settle(ve.tensor_tensor(t_c, t_c, z_c, ALU.mult))
                settle(ve.tensor_tensor(t_c, t_c, n_c, ALU.add))
                if q >= 1:
                    ve.wait_ge(s_utn, q)
                ve.tensor_tensor(u_c, t_c, part, ALU.add).then_inc(s_cell, 1)
            ve.wait_ge(s_utc, NQ)
            layernorm(3, u_rows, x3_rows, s_x3)

            ve.wait_ge(s_aw, 16 * 15)
            n = 0
            for i, (stack, lows) in enumerate(((qs, ((64, 64),)), (ks, ((32, 32), (96, 32))))):
                for h in range(H):
                    for q in range(NQ):
                        ve.wait_ge(s_hi, n + 1)
                        for p, k in lows:
                            part = stack[p:p + k, h, BANK * q:BANK * q + BANK]
                            ins = ve.scalar_tensor_tensor(part, psum[p:p + k, n % 4, :], qk_cols[p:p + k, H * i + h:H * i + h + 1],
                                                          part.bitcast(fp32), ALU.add, ALU.subtract)
                        ins.then_inc(s_lo, 1)
                        n += 1
            for g in range(NT // 2):
                ve.wait_ge(s_vp, g + 1)
                both = psum[:, 4 + g % 2, :].rearrange("p (j c) -> p j c", j=2)
                bias = bvs_rows.rearrange("p (a o d) -> p a o d", a=2, o=1)
                ve.tensor_tensor(v_rows[:, 2 * g:2 * g + 2, :], both[:, :, 0:PT], bias[:, 0].to_broadcast([PT, 2, PT]), ALU.add)
                ve.tensor_tensor(xr_rows[:, 2 * g:2 * g + 2, :], both[:, :, PT:2 * PT],
                                 bias[:, 1].to_broadcast([PT, 2, PT]), ALU.add).then_inc(s_vc, 1)
            ve.wait_ge(s_vc, NT // 2)
            ve.tensor_tensor(wb_out, wb_rows[:, 0:PT], wb_rows[:, 2 * PT:3 * PT], ALU.add)
            settle(ve.tensor_tensor(wb_skip, wb_rows[:, PT:2 * PT], wb_rows[:, 2 * PT:3 * PT], ALU.subtract))
            for t in range(NT):
                settle(ve.tensor_tensor_reduce(gate_scrap, xr_rows[:, t, :], wb_skip, 1.0, 0.0, ALU.mult, ALU.add,
                                               skip_dot[:, t:t + 1]))

            def mask_and_max(i):
                t, h = divmod(i, H)
                if h == 0:
                    ve.wait_ge(s_pen, t + 1)
                if i >= MASKS:
                    ve.wait_ge(s_etp, NQ * (i - MASKS + 1))
                for a in range(2):
                    ve.wait_ge(s_scp, 2 * i + a + 1)
                    ve.tensor_tensor_reduce(masked[:, i % MASKS, 1024 * a:1024 * a + 1024], flat[:, 1024 * a:1024 * a + 1024],
                                            adj_again[:, t % 2, 1024 * a:1024 * a + 1024], 1.0,
                                            row_max[:, i % 4, 0:1] if a else FLOOR, ALU.add, ALU.max,
                                            row_max[:, i % 4, a:a + 1]).then_inc(s_mask, 1)
                    ve.wait_ge(s_mask, 2 * i + a + 1)
                ve.tensor_scalar(row_max[:, i % 4, 3:4], row_max[:, i % 4, 1:2], -SCALE, None, ALU.mult).then_inc(s_bias, 1)

            def copy_turned(i):
                if turned_free(i) >= 0:
                    ve.wait_ge(s_avp, turned_free(i) + 1)
                for n in range(NQ * i, NQ * i + NQ):
                    q = n % NQ
                    if turned_copy(n)[0] is s_etV:
                        ve.wait_ge(s_etp, n + 1)
                        ve.tensor_copy(turned[i % len(turned)][:, TPQ * q:TPQ * q + TPQ, :],
                                       psum[:, 4 + n % 3, :]).then_inc(s_etV, 1)

            def normalise(t):
                ve.wait_ge(s_exp, H * (t + 1))
                settle(ve.scalar_tensor_tensor(rden[:, t % 2, :], den[:, t, :], 0.0, den[:, t, :], ALU.is_equal, ALU.add))
                settle(ve.reciprocal(rden[:, t % 2, :], rden[:, t % 2, :]))
                ve.wait_ge(s_avt, t + 1)
                ve.tensor_tensor(o_rows[:, t, :].rearrange("p (c h) -> p h c", h=H),
                                 psum[:, 7, PT:2 * PT].rearrange("p (h c) -> p h c", h=H),
                                 rden[:, t % 2, :].rearrange("p (h o) -> p h o", o=1).to_broadcast([PT, H, C]),
                                 ALU.mult).then_inc(s_o, 1)
                ve.wait_ge(s_o, t + 1)
                ve.tensor_tensor_reduce(gate_scrap, o_rows[:, t, :], wb_out, 1.0, skip_dot[:, t:t + 1], ALU.mult, ALU.add,
                                        gate[:, t % 2, 0:1]).then_inc(s_gz, 1)

            def mix(t):
                ve.wait_ge(s_ge, t + 1)
                settle(ve.tensor_scalar(gate[:, t % 2, 2:3], gate[:, t % 2, 1:2], 1.0, None, ALU.add))
                ve.reciprocal(gate[:, t % 2, 3:4], gate[:, t % 2, 2:3])
                settle(ve.tensor_tensor(gate_scrap, xr_rows[:, t, :], o_rows[:, t, :], ALU.subtract))
                settle(ve.scalar_tensor_tensor(o_rows[:, t, :], gate_scrap, gate[:, t % 2, 3:4], o_rows[:, t, :],
                                               ALU.mult, ALU.add))
                settle(ve.tensor_tensor(o_rows[:, t, :], o_rows[:, t, :], x3_rows[:, t, :], ALU.add))

            steps = NT * H
            for i in range(steps + LAG + 4):
                if i < steps:
                    mask_and_max(i)
                if LAG <= i < steps + LAG:
                    copy_turned(i - LAG)
                ended, h = divmod(i - LAG - 5, H)
                if h == 0 and 0 <= ended < NT:
                    normalise(ended)
                ended, h = divmod(i - LAG - 7, H)
                if h == 0 and 0 <= ended < NT:
                    mix(ended)
            layernorm(4, o_rows, o_rows, s_fin)

        @block.scalar
        def _(ac):
            def square_root(turn):
                ac.wait_ge(s_ln, turn + 1)
                ac.activation(rstd, rstd, ACT.Sqrt).then_inc(s_ln2, 1)

            ac.wait_ge(s_xtp, 1)
            ac.activation(wT, psum[:, 0, 0:2 * PT], ACT.Copy).then_inc(s_xt, 1)
            for q in range(NQ):
                ac.wait_ge(s_xtp, q + 2)
                ac.activation(xT[:, BANK * q:BANK * q + BANK], psum[:, 1 + q, :], ACT.Copy).then_inc(s_xt, 1)
            for g in range(NT // 2):
                ac.wait_ge(s_sdp, g + 1)
                both = psum[:, 5 + g % 2, :].rearrange("p (j c) -> p j c", j=2)
                ac.activation(s_rows[:, 2 * g:2 * g + 2, :], both[:, :, 0:PT], ACT.Copy).then_inc(s_sdA, 1)
            ac.wait_ge(s_w, 48)
            for q in range(NQ):
                ac.wait_ge(s_dtp, q + 1)
                ac.activation(dT[:, BANK * q:BANK * q + BANK], psum[:, 1 + q, :], ACT.Identity,
                              bias=msgb_col).then_inc(s_dt, 1)
            counted = psum[:, 4:8, :]
            unit = 0
            for s in range(NT + 1):
                if s < NT:
                    t = ORDER[s]
                    ac.wait_ge(s_adj[s % 2], 16 * (s // 2 + 1))
                    if s == 0:
                        ac.wait_ge(s_sdV, NT // 2)
                        ac.wait_ge(s_dt, 4)
                    else:
                        ac.wait_ge(s_count, s)
                    ac.activation(counted, adj_in[:, s % 2, :].rearrange("p (b n) -> p b n", b=NQ), ACT.Sign).then_inc(s_act, 1)
                    ac.wait_ge(s_act, s + 1)
                    ac.activation(counted, counted, ACT.Square, accum_out=edge_count[:, s % 2:s % 2 + 1]).then_inc(s_count, 1)
                    for q in range(NQ):
                        n = NQ * s + q
                        ac.wait_ge(s_tp, n + 1)
                        ac.activation(adjT[:, TPQ * q:TPQ * q + TPQ, PT * t:PT * t + PT], psum[:, n % 2, :],
                                      ACT.Copy).then_inc(s_tpc, 1)
                if s == 0:
                    continue
                for v in range(UNITS[s - 1]):
                    if v == 0:
                        ac.wait_ge(s_ext, s)
                    if unit >= 2:
                        ac.wait_ge(s_unit, unit - 1)
                    for j in range(UNIT):
                        k = UNIT * v + j
                        ins = ac.activation(diag[:, unit % 2, j, :], eye, ACT.Copy, scale=weight[:, (s - 1) % 3, k:k + 1])
                    ins.then_inc(s_diag, 1)
                    ac.wait_ge(s_add, unit + 1)
                    ac.activation(gath[:, unit % RING, :, :], gath[:, unit % RING, :, :], ACT.Gelu).then_inc(s_gelu, 1)
                    unit += 1
                t = ORDER[s - 1]
                ac.wait_ge(s_unit, unit)
                ac.activation(aggT[:, PT * t:PT * t + PT], psum[:, 2 + s % 2, 0:PT], ACT.Copy).then_inc(s_aggc, 1)
            ac.wait_ge(s_counts, 1)
            batches = ac.value_load(loop_counts[0:1, NT:NT + 1], min_val=1, max_val=NT)
            with ac.Fori(0, batches) as b:
                pairs = ac.value_load(loop_counts[0:1, ds(b, 1)], min_val=1, max_val=PT // 2)
                hold(ac, s_stsel, b + 1)
                with ac.Fori(0, pairs) as r:
                    for k in range(2):
                        row = b * PT + r * 2 + k
                        for h in range(2):
                            hold(ac, s_half, row * 2 + h + 1)
                            ac.activation(msgs[:, 1024 * h:1024 * h + 1024], dT[:, 1024 * h:1024 * h + 1024], ACT.Gelu,
                                          bias=sT_sel[:, ds(r * 2 + k, 1)]).then_inc(s_mg, 1)
            ac.wait_ge(s_utp, 1)
            ac.activation(uT, psum[:, 0, 0:2 * PT], ACT.Copy).then_inc(s_ut, 1)
            for q in range(NQ):
                ac.wait_ge(s_newp, q + 1)
                ac.activation(newT[:, BANK * q:BANK * q + BANK], psum[:, 4 + q, :], ACT.Gelu,
                              bias=updb_col).then_inc(s_newg, 1)
            for q in range(NQ):
                ac.wait_ge(s_rowp, q + 1)
                ac.activation(slot(2)[:, BANK * q:BANK * q + BANK], psum[:, q, :], ACT.Copy).then_inc(s_hc, 1)
            square_root(0)
            square_root(1)

            turn = [0]

            def copy_turned(target):
                n = turn[0]
                ac.wait_ge(s_tnp, n + 1)
                ac.activation(target, psum[:, 6 + n % 2, :], ACT.Copy).then_inc(s_tnc, 1)
                turn[0] += 1

            for q in range(NQ):
                copy_turned(slot(0)[:, BANK * q:BANK * q + BANK])
            for k in range(1, CHEB - 1):
                for q in range(NQ):
                    copy_turned(term_rows[k][:, TPQ * q:TPQ * q + TPQ, :])
            square_root(2)

            ac.wait_ge(s_gwp, 1)
            ac.activation(gwT[:, 0:4, :], psum[:, 0, :], ACT.Copy).then_inc(s_gwc, 1)
            ac.activation(gwT[:, 4:7, :], psum[:, 1, 0:3 * PT], ACT.Copy).then_inc(s_gwc, 1)
            for q in range(NQ):
                copy_turned(slot(0)[:, BANK * q:BANK * q + BANK])
            ac.wait_ge(s_gb, 1)
            for q in range(NQ + 2):
                if 1 <= q <= NQ:
                    ac.wait_ge(s_msgp, q)
                    if q >= 2:
                        ac.wait_ge(s_gate, q - 1)
                    ac.activation(msg_c, psum[:, 6, :], ACT.Relu, bias=bmsg_col).then_inc(s_msg, 1)
                if q >= 2:
                    ac.wait_ge(s_utn, q - 1)
                    ac.activation(slot(4)[:, BANK * (q - 2):BANK * (q - 1)], psum[:, 7, :], ACT.Copy).then_inc(s_utc, 1)
                if q < NQ:
                    ac.wait_ge(s_agg2p, q + 1)
                    if q >= 1:
                        ac.wait_ge(s_msgp, q)
                    ac.activation(agg_c, psum[:, 4 + q % 2, :], ACT.Copy).then_inc(s_agg2, 1)
                if 1 <= q <= NQ:
                    ac.wait_ge(s_gate, q)
                    if q >= 2:
                        ac.wait_ge(s_cell, q - 1)
                    ac.activation(r_c, psum[:, 0, :], ACT.Sigmoid, bias=brz_cols[:, 0:1]).then_inc(s_gact, 1)
                    ac.activation(z_c, psum[:, 1, :], ACT.Sigmoid, bias=brz_cols[:, 1:2]).then_inc(s_gact, 1)
                    ac.wait_ge(s_pre, q)
                    ac.activation(n_c, t_c, ACT.Tanh, bias=bih_cols[:, 2:3]).then_inc(s_tanh, 1)
            square_root(3)

            for q in range(NQ):
                copy_turned(slot(0)[:, BANK * q:BANK * q + BANK])
            ac.wait_ge(s_aw, 16 * 15)
            n = 0
            for i, stack in enumerate((qs, ks)):
                for h in range(H):
                    for q in range(NQ):
                        ac.wait_ge(s_prp, n + 1)
                        ac.activation(stack[:, h, BANK * q:BANK * q + BANK], psum[:, n % 4, :], ACT.Identity,
                                      bias=qk_cols[:, H * i + h:H * i + h + 1]).then_inc(s_hi, 1)
                        n += 1
            steps = NT * H
            for i in range(steps + LAG + 4):
                t, h = divmod(i, H)
                ended, part = divmod(i - LAG - 4, H)
                if part == 0 and 0 <= ended < NT:
                    ac.wait_ge(s_avp, ended + 1)
                    if ended >= 1:
                        ac.wait_ge(s_avt, ended)
                    ac.activation(avT, psum[:, 7, 0:PT], ACT.Copy).then_inc(s_avc, 1)
                if LAG <= i < steps + LAG:
                    j = i - LAG
                    if turned_free(j) >= 0:
                        ac.wait_ge(s_avp, turned_free(j) + 1)
                    for n in range(NQ * j, NQ * j + NQ):
                        q = n % NQ
                        if turned_copy(n)[0] is s_etA:
                            ac.wait_ge(s_etp, n + 1)
                            ac.activation(turned[j % len(turned)][:, TPQ * q:TPQ * q + TPQ, :], psum[:, 4 + n % 3, :],
                                          ACT.Copy).then_inc(s_etA, 1)
                if i < steps:
                    ac.wait_ge(s_bias, i + 1)
                    ac.activation(masked[:, i % MASKS, :], masked[:, i % MASKS, :], ACT.Exp, scale=SCALE,
                                  bias=row_max[:, i % 4, 3:4], accum_out=den[:, t, h:h + 1]).then_inc(s_exp, 1)
                ended, part = divmod(i - LAG - 6, H)
                if part == 0 and 0 <= ended < NT:
                    ac.wait_ge(s_gz, ended + 1)
                    ac.activation(gate[:, ended % 2, 1:2], gate[:, ended % 2, 0:1], ACT.Exp, scale=-1.0).then_inc(s_ge, 1)
            square_root(4)


_INS = ['x', 'adj', 'L0_gnn_msg_w', 'L0_gnn_msg_b', 'L0_gnn_upd_w', 'L0_gnn_upd_b', 'L0_gnn_ln_w', 'L0_gnn_ln_b',
        'L1_gnn_theta', 'L2_gnn_W_msg', 'L2_gnn_b_msg', 'L2_gnn_W_ih', 'L2_gnn_W_hh', 'L2_gnn_b_ih', 'L2_gnn_b_hh',
        'L3_gnn_Wq', 'L3_gnn_bq', 'L3_gnn_Wk', 'L3_gnn_bk', 'L3_gnn_Wv', 'L3_gnn_bv', 'L3_gnn_Ws', 'L3_gnn_bs',
        'L3_gnn_Wb']


def kernel(**inputs):
    import numpy as _np
    import concourse.bacc as _bacc
    from concourse import mybir as _mybir
    from concourse.bass_utils import run_bass_kernel_spmd as _run

    nc = _bacc.Bacc("TRN2", target_bir_lowering=False, num_devices=1)
    arrays, args = {}, []
    for name in _INS:
        a = _np.ascontiguousarray(inputs[name])
        arrays[f"in_{name}_dram"] = a
        args.append(nc.dram_tensor(f"in_{name}_dram", a.shape, _mybir.dt.from_np(a.dtype), kind="ExternalInput").ap())
    args.append(nc.dram_tensor("out_0_dram", (N, D), _mybir.dt.float32, kind="ExternalOutput").ap())
    args.append(nc.dram_tensor("d_rows_dram", (N, D), _mybir.dt.float32).ap())
    graph_network(nc, *args)
    r = _run(nc, [arrays], core_ids=[0])
    return r.results[0]["out_0_dram"]
```

```python
import math
import concourse.bass as bass
from concourse import mybir
from contextlib import ExitStack

N, D, PT, BANK = 2048, 128, 128, 512
NT = N // PT
NQ = N // BANK
TPQ = BANK // PT
H, C = 4, 32
CHEB = 5
TAU = 0.5
LN_EPS = 1e-5
SCALE = 1.0 / math.sqrt(C)

ORDER = [7, 1, 0, 2, 3, 4, 5, 6] + list(range(8, NT))
UNIT = 4
SLOTS = {0: 32, 1: 23, 2: 21, 3: 16, 4: 16, 5: 14, 6: 13, 9: 13, 10: 13, 13: 9, 14: 11}
UNITS = [[min(UNIT, SLOTS.get(t, 12) - first) for first in range(0, SLOTS.get(t, 12), UNIT)] for t in ORDER]
SIZES = [size for tile in UNITS for size in tile]
RING = 4
NSEG = 7
EDGES = [round((k / NSEG) ** 2 * N / 16) * 16 for k in range(NSEG + 1)]
CAND = 8 * NSEG
RB = 64
NB = N // RB
STEP = 4
SD_BANKS = (5, 6, 7, 0)

MASKS = 4
LAG = 2
MASKED = 1.0e30
CEILING = 1.0e20


def cheb_coeff(k):
    return 2.0 / CHEB * math.exp(-TAU * math.cos(math.pi * (k + 0.5) / CHEB))


class Tally:

    def __init__(self, semaphore):
        self.semaphore, self.count = semaphore, 0

    def step(self, instruction):
        instruction.then_inc(self.semaphore, 1)
        self.count += 1
        return self.count


def graph_network(nc, x, adj, msg_w, msg_b, upd_w, upd_b, ln_w, ln_b, theta, w_msg, b_msg, w_ih, w_hh, b_ih, b_hh,
                  wq, bq, wk, bk, wv, bv, ws, bs, wb, out, d_rows):
    fp32 = mybir.dt.float32
    fp32r = mybir.dt.float32r
    i32 = mybir.dt.int32
    u32 = mybir.dt.uint32
    ALU = mybir.AluOpType
    ACT = mybir.ActivationFunctionType
    ds = bass.ds

    ctx = ExitStack()
    with ctx:
        def sb(name, shape, dt=fp32):
            return ctx.enter_context(nc.sbuf_tensor(name, shape, dt))

        def sem(name):
            return ctx.enter_context(nc.semaphore(name))

        ident = sb("ident", [PT, PT + 4])
        eye = ident[:, 0:PT]
        psum = ctx.enter_context(nc.psum_tensor("psum", [PT, 8, BANK], fp32))
        cols = sb("cols", [PT, 12])
        msgb_col, updb_col, bmsg_col = cols[:, 0:1], cols[:, 1:2], cols[:, 2:3]
        bih_cols, bhh_cols, brz_cols = cols[:, 3:6], cols[:, 6:9], cols[:, 9:11]
        iota_r = sb("iota_r", [PT, PT])
        rowid = sb("rowid", [PT, NT])
        flags = sb("flags", [PT, NT])
        seg_base = sb("seg_base", [PT, NSEG, 8])
        cand = sb("candidates", [PT, 3 * CAND])
        cand_val, cand_key, cand_left = cand[:, 0:CAND], cand[:, CAND:2 * CAND], cand[:, 2 * CAND:3 * CAND]
        sT_sel = cand[:, 0:PT]
        cand_pos = sb("cand_pos", [PT, CAND], u32)
        picked = sb("picked", [PT, 32])
        scrap = sb("scrap", [PT, 32])
        edge_count = sb("edge_count", [PT, 4])
        keep = sb("keep", [PT, 1])
        weight = sb("weight", [PT, 3, 32])
        column = sb("column", [PT, 3, 32], i32)
        pos = sb("pos", [PT, NT])
        loop_counts = sb("loop_counts", [PT, NB + 1], i32)
        rows_i = sb("rows_i", [PT, 1], i32)
        diag = sb("diag", [PT, 2, UNIT, PT])
        stats = [diag[:, i, 0, 0:6 * NT].rearrange("p (t c) -> p t c", c=6) for i in range(2)]
        moments = [diag[:, i, 1, 0:2 * NT].rearrange("p (t c) -> p t c", c=2) for i in range(2)]
        rstd = [diag[:, i, 2, 0:NT] for i in range(2)]
        shift = [diag[:, i, 3, 0:NT] for i in range(2)]
        pool_low = sb("pool_low", [PT, 5, N])
        place = ctx.enter_context(ExitStack())
        place.enter_context(nc.sbuf_tensor("before_selectors", [PT, 1024], fp32))
        selector = place.enter_context(nc.sbuf_tensor("selector", [PT, 2, PT], fp32r))
        place.enter_context(nc.sbuf_tensor("after_selectors", [PT, N - 1024 - 2 * PT], fp32))
        adj_parts = place.enter_context(nc.sbuf_tensor("adj_parts", [PT, N], fp32r))
        place.close()
        pool_high = sb("pool_high", [PT, 4, N])
        pool_end = ctx.enter_context(ExitStack())
        adjT = pool_end.enter_context(nc.sbuf_tensor("adjT", [PT, NT, N], fp32))
        pool_end.close()
        qs = sb("q_stack", [PT, H, N], fp32r)
        ks = sb("k_stack", [PT, H, N], fp32r)
        early = ctx.enter_context(ExitStack())
        qk_parts = early.enter_context(nc.sbuf_tensor("qk_parts", [PT, 4, N], fp32r))
        early.enter_context(nc.sbuf_tensor("adj_again_place", [PT, 2, N], fp32))
        spread_to = early.enter_context(nc.sbuf_tensor("spread_to", [PT, 4 * H * PT], fp32r))
        early.close()
        masked = sb("masked_scores", [PT, MASKS, N])
        adj_again = sb("adj_again", [PT, 2, N])
        turned_sb = sb("turned_probs", [PT, 2, N])

        def as_rows(ap):
            return ap.rearrange("p (t d) -> p t d", t=NT)

        def slot(k):
            return pool_low[:, k, :] if k < 5 else pool_high[:, (k - 4) % 4, :]

        xT, dT, s_rows, aggT = slot(0), slot(1), as_rows(slot(2)), slot(3)
        x_rows, d_stage = as_rows(slot(3)), as_rows(slot(4))
        adj_in = pool_high[:, 1:3, :]
        adj_raw, sel_hot, pick_hot = slot(4), as_rows(slot(5)), as_rows(slot(6))
        msgs = slot(7)
        dense_msgs = [slot(7), slot(4)]
        total, cum = slot(7)[:, 0:2 * NT], slot(7)[:, 2 * NT:3 * NT]
        left, more = slot(7)[0:1, 3 * NT:3 * NT + NB], slot(7)[0:1, 3 * NT + NB:3 * NT + 2 * NB]
        msgw_in, wT, msgb_rows = slot(7)[:, 0:256], slot(7)[:, 256:512], slot(7)[:, 512:640]
        prefix_tri, ones_sq, batch_start = slot(4)[:, 0:128], slot(4)[:, 128:256], slot(4)[:, 256:256 + NB]
        gath = slot(8).rearrange("p (r k d) -> p r k d", r=RING, k=UNIT)
        agg_sel, row_sum, twin = slot(8)[:, 0:PT], slot(8)[:, PT:PT + STEP], slot(8)[:, 512:512 + RB + 2]
        agg_selr = slot(8)[:, 384:512]
        updw_in, uT = slot(8)[:, 1280:1536], slot(8)[:, 1536:1792]
        lnw_rows, lnb_rows = slot(8)[:, 1792:1920], slot(8)[:, 1920:2048]
        newT, h_rows, x_again, x1_rows = slot(1), as_rows(slot(2)), as_rows(slot(5)), as_rows(slot(6))
        termT = [slot(0), slot(1), slot(2), slot(0), slot(1)]
        term_rows = [x1_rows, as_rows(slot(3)), as_rows(slot(4)), as_rows(slot(3))]
        theta_in = slot(7)[:, 768:768 + CHEB * PT].rearrange("p (k o) -> p k o", k=CHEB)
        y_rows, x2_rows = as_rows(slot(5)), as_rows(slot(4))
        x2T = slot(0)
        gw_in = slot(8)[:, 0:7 * PT].rearrange("p (g f) -> p g f", g=7)
        gwT = slot(8)[:, 7 * PT:14 * PT].rearrange("p (g f) -> p g f", g=7)
        agg_c, msg_c, r_c, z_c = [slot(1)[:, BANK * i:BANK * i + BANK] for i in range(4)]
        n_c, t_c, u_c, _ = [slot(2)[:, BANK * i:BANK * i + BANK] for i in range(4)]
        u_rows, x3_rows = as_rows(slot(3)), as_rows(slot(5))
        x3T, v_rows, xr_rows, o_rows = slot(0), as_rows(slot(1)), as_rows(slot(2)), as_rows(slot(3))
        attw = slot(8)[:, 0:512]
        bvs_rows, wb_rows = slot(8)[:, 512:768], slot(7)[:, 1408:1792]
        wb_out, wb_skip = slot(8)[:, 1152:1280], slot(8)[:, 1280:1408]
        turned = [as_rows(turned_sb[:, k, :]) for k in range(2)] + [as_rows(slot(k)) for k in (4, 6, 7, 0)]
        avT, gate_scrap = slot(8)[:, 1408:1536], slot(8)[:, 1536:1664]
        qk_cols = slot(8)[:, 1792:1794]
        row_min = slot(8)[:, 1672:1688].rearrange("p (a b) -> p a b", b=4)
        den = slot(8)[:, 1688:1752].rearrange("p (t h) -> p t h", h=H)
        rden = slot(8)[:, 1752:1760].rearrange("p (a h) -> p a h", h=H)
        skip_dot = slot(8)[:, 1760:1776]
        gate = slot(8)[:, 1776:1792].rearrange("p (a b) -> p a b", b=8)

        s_w, s_x, s_const, s_const2 = sem("message_weights"), sem("x_loaded"), sem("constants"), sem("prefix_consts")
        s_adj = [sem(f"adj_loaded{i}") for i in range(2)]
        s_dve, s_act, s_pool = sem("vector_step"), sem("scalar_step"), sem("gpsimd_step")
        s_xtp, s_xt = sem("x_turned"), sem("x_turned_copied")
        s_sdp, s_sdA, s_sdV, s_dstore = sem("sd_product"), sem("s_copied"), sem("d_copied"), sem("d_rows_stored")
        s_dtp, s_dt = sem("dT_product"), sem("dT_copied")
        s_tp, s_tpc = sem("adj_turned"), sem("adj_turned_copied")
        s_ext, s_count = sem("neighbours_extracted"), sem("nonzeros_counted")
        s_gath = [sem(f"gathered{i}") for i in range(RING)]
        s_add, s_gelu, s_diag, s_unit, s_aggc = sem("s_added"), sem("unit_gelu"), sem("diag_made"), sem("unit_summed"), sem("agg_tile_copied")
        s_flagp, s_counts = sem("flag_prefix"), sem("loop_counts_ready")
        s_hot, s_pickp, s_picki, s_asel = sem("pick_hot"), sem("picked_product"), sem("picked_ready"), sem("adj_rows_gathered")
        s_twin, s_spick, s_ahi, s_alo = sem("twin_identity"), sem("picked_s_product"), sem("adj_rows_high"), sem("adj_rows_low")
        s_sel, s_bc, s_mg, s_red = sem("selector_made"), sem("adj_row_broadcast"), sem("dense_row_gelu"), sem("dense_row_reduced")
        s_dsum, s_dtr, s_dcA, s_dcp, s_dout, s_dacc = sem("dense_sum"), sem("dense_turned"), sem("dense_turned_by_scalar"), sem("dense_turned_copied"), sem("dense_scattered"), sem("dense_accumulated")
        s_dense, s_iota, s_hc, s_held = sem("dense_done"), sem("iota_moved"), sem("h_copied"), sem("waits_held")
        s_w2, s_xb, s_utp, s_ut = sem("update_weights"), sem("x_with_bias"), sem("upd_w_turned"), sem("upd_w_copied")
        s_newp, s_newg, s_newx = sem("new_feats_product"), sem("new_feats_gelu"), sem("new_feats_plus_x")
        s_rowp = sem("h_turned")
        s_ln, s_ln2, s_lnr, s_lnn = sem("layernorm_variance"), sem("layernorm_sqrt"), sem("layernorm_factors"), sem("layernorm_first")
        s_x1, s_x2, s_x3, s_x3A = sem("x1_quarter"), sem("x2_quarter"), sem("x3_by_vector"), sem("x3_by_scalar")
        s_xa = sem("x_loaded_again")
        s_tnp, s_tnc = sem("turned_psum"), sem("turned_copied")
        s_th, s_ths = sem("theta_loaded"), sem("theta_scaled")
        s_hopp, s_hopc, s_chp = sem("hop_product"), sem("hop_copied"), sem("cheb_sum")
        s_gwl, s_gwp, s_gwc, s_gb = sem("gru_weights"), sem("gru_weights_turned"), sem("gru_weights_copied"), sem("gru_bias")
        s_agg2p, s_agg2, s_msgp, s_msg = sem("agg2_product"), sem("agg2_copied"), sem("msg_product"), sem("msg_ready")
        s_reset, s_gate, s_gact, s_pre, s_tanh, s_cell = sem("reset_gate_product"), sem("gates_product"), sem("gates_ready"), sem("candidate_sum"), sem("candidate_ready"), sem("cell_ready")
        s_utn, s_utc = sem("u_turned"), sem("u_turned_copied")
        s_wqs, s_spread, s_stackA, s_stackV = sem("wq_scaled"), sem("qk_spread"), sem("stack_by_scalar"), sem("stack_by_vector")
        s_rep, s_aw, s_prp, s_hi, s_lo = sem("spreading_matrices"), sem("att_weights"), sem("projection"), sem("stack_high"), sem("stack_low")
        s_vp, s_vc = sem("value_product"), sem("value_copied")
        s_adj2 = [sem(f"adj_again{i}") for i in range(2)]
        s_bias, s_pen, s_scp, s_mask, s_exp = sem("attention_biases"), sem("penalty"), sem("scores"), sem("masked_half"), sem("exp_done")
        s_etp, s_etA, s_etV = sem("probs_turned"), sem("turned_by_scalar"), sem("turned_by_vector")
        s_avp, s_avc, s_avt, s_o = sem("av_product"), sem("av_copied"), sem("av_turned"), sem("out_rows")
        s_gz, s_ge = sem("gate_dot"), sem("gate_exp")
        s_fin, s_finA, s_out = sem("result_by_vector"), sem("result_by_scalar"), sem("output_written")
        block = ctx.enter_context(nc.Block())

        def hold(engine, semaphore, value):
            engine.wait_ge(semaphore, value)
            engine.sem_inc(s_held, 1)

        def turned_copy(n):
            step, q = divmod(n, NQ)
            return (s_etV, step + 1) if q == NQ - 1 else (s_etA, 3 * step + q + 1)

        def turned_free(step):
            return (step - len(turned)) // H

        def steps_of(engine, b):
            here = loop_counts[0:1, b:b + 1] if isinstance(b, int) else loop_counts[0:1, ds(b, 1)]
            return engine.value_load(here, min_val=1, max_val=RB // STEP)

        def tiles_of(q):
            return range(TPQ * q, TPQ * q + TPQ)

        def all_rows(dram):
            return dram.rearrange("(t p) d -> p t d", p=PT)

        def column_of(dram):
            return dram.rearrange("(p o) -> p o", o=1)

        @block.sync
        def _(sp):
            sp.dma_start(msgw_in, msg_w).then_inc(s_w, 16)
            sp.dma_start(msgb_rows, msg_b.partition_broadcast(PT)).then_inc(s_w, 16)
            sp.dma_start(msgb_col, column_of(msg_b)).then_inc(s_w, 16)
            sp.dma_start(x_rows, all_rows(x)).then_inc(s_x, 16)
            for s in range(NT):
                t = ORDER[s]
                if s >= 2:
                    sp.wait_ge(s_tp, NQ * (s - 1))
                    sp.wait_ge(s_ext, s - 1)
                sp.dma_start(adj_in[:, s % 2, :], adj[t * PT:(t + 1) * PT, :]).then_inc(s_adj[s % 2], 16)
                if s == 1:
                    sp.wait_ge(s_sdV, NT // 2)
                    sp.dma_start(all_rows(d_rows), d_stage).then_inc(s_dstore, 16)
            sp.wait_ge(s_aggc, NT)
            sp.dma_start(updw_in, upd_w).then_inc(s_w2, 16)
            sp.dma_start(updb_col, column_of(upd_b)).then_inc(s_w2, 16)
            sp.dma_start(lnw_rows, ln_w.partition_broadcast(PT)).then_inc(s_w2, 16)
            sp.dma_start(lnb_rows, ln_b.partition_broadcast(PT)).then_inc(s_w2, 16)
            sp.wait_ge(s_dense, 2)
            sp.dma_start(x_again, all_rows(x)).then_inc(s_xa, 16)
            sp.dma_start(theta_in, theta.rearrange("k i o -> i k o")).then_inc(s_th, 16)
            sp.dma_start(gw_in[:, 0, :], w_msg).then_inc(s_gwl, 16)
            sp.dma_start(gw_in[:, 1:4, :], w_ih.rearrange("(g p) f -> p g f", p=PT)).then_inc(s_gwl, 16)
            sp.dma_start(gw_in[:, 4:7, :], w_hh.rearrange("(g p) f -> p g f", p=PT)).then_inc(s_gwl, 16)
            sp.dma_start(bmsg_col, column_of(b_msg)).then_inc(s_gwl, 16)
            sp.dma_start(bih_cols, b_ih.rearrange("(g p) -> p g", p=PT), allow_slow_non_contiguous=True).then_inc(s_gwl, 16)
            sp.dma_start(bhh_cols, b_hh.rearrange("(g p) -> p g", p=PT), allow_slow_non_contiguous=True).then_inc(s_gwl, 16)
            sp.wait_ge(s_gwp, 1)
            for i, w in enumerate((wq, wk, wv, ws)):
                sp.dma_start(attw[:, PT * i:PT * i + PT], w).then_inc(s_aw, 16)
            sp.dma_start(bvs_rows[:, 0:PT], bv.partition_broadcast(PT)).then_inc(s_aw, 16)
            sp.dma_start(bvs_rows[:, PT:2 * PT], bs.partition_broadcast(PT)).then_inc(s_aw, 16)
            sp.dma_start(wb_rows, wb.rearrange("k o -> (k o)").partition_broadcast(PT)).then_inc(s_aw, 16)
            for i, b in enumerate((bq, bk)):
                sp.dma_start(qk_cols[:, i:i + 1], column_of(b)).then_inc(s_aw, 16)
            for t in range(NT):
                if t == 0:
                    sp.wait_ge(s_agg2p, NQ)
                if t >= 2:
                    sp.wait_ge(s_mask, 2 * H * (t - 1))
                sp.dma_start(adj_again[:, t % 2, :], adj[t * PT:(t + 1) * PT, :]).then_inc(s_adj2[t % 2], 16)
            for q in range(NQ):
                sp.wait_ge(s_finA if q % 2 else s_fin, q // 2 + 1)
                sp.dma_start(all_rows(out)[:, TPQ * q:TPQ * q + TPQ, :], o_rows[:, TPQ * q:TPQ * q + TPQ, :]).then_inc(s_out, 16)
            sp.wait_ge(s_out, 16 * NQ)

        @block.gpsimd
        def _(gp):
            gp.memset(ident[:, :], 0.0).then_inc(s_pool, 1)
            gp.wait_ge(s_pool, 1)
            gp.affine_select(out=ident[:, :], in_=ident[:, :], compare_op=ALU.not_equal, fill=1.0,
                             base=0, pattern=[[-1, PT + 4]], channel_multiplier=1).then_inc(s_const, 1)
            gp.iota(iota_r[:, :], pattern=[[0, PT // RB], [1, RB]], base=0, channel_multiplier=0,
                    allow_small_or_imprecise_dtypes=True).then_inc(s_const, 1)
            gp.iota(rowid[:, :], pattern=[[PT, NT]], base=0, channel_multiplier=1,
                    allow_small_or_imprecise_dtypes=True).then_inc(s_const, 1)
            for g in range(NSEG):
                ins = gp.memset(seg_base[:, g, :], EDGES[g] + 1.0)
            ins.then_inc(s_const, 1)
            gp.wait_ge(s_dstore, 16)
            u = 0
            for s in range(NT):
                gp.wait_ge(s_ext, s + 1)
                for v, size in enumerate(UNITS[s]):
                    if u >= RING:
                        gp.wait_ge(s_unit, u - RING + 1)
                    for j in range(size):
                        k = UNIT * v + j
                        gp.indirect_dma_start(
                            out=gath[:, u % RING, j, :], out_offset=None, in_=d_rows,
                            in_offset=bass.IndirectOffsetOnAxis(ap=column[:, s % 3, k:k + 1], axis=0)
                        ).then_inc(s_gath[u % RING], 16)
                    u += 1
                if s == 0:
                    gp.memset(ones_sq, 1.0).then_inc(s_const2, 1)
                    gp.memset(prefix_tri, 1.0).then_inc(s_const2, 1)
                    gp.wait_ge(s_const2, 2)
                    gp.affine_select(out=prefix_tri, in_=prefix_tri, compare_op=ALU.is_gt, fill=0.0,
                                     base=0, pattern=[[1, PT]], channel_multiplier=-1).then_inc(s_const2, 1)
                    gp.iota(batch_start, pattern=[[RB, NB]], base=0, channel_multiplier=0,
                            allow_small_or_imprecise_dtypes=True).then_inc(s_const2, 1)
            gp.wait_ge(s_counts, 1)
            batches = gp.value_load(loop_counts[0:1, NB:NB + 1], min_val=1, max_val=NB)

            def dense_batch(b):
                steps = steps_of(gp, b)
                hold(gp, s_picki, b + 1)
                gp.indirect_dma_start(out=adj_raw, out_offset=None, in_=adj,
                                      in_offset=bass.IndirectOffsetOnAxis(ap=rows_i[:, 0:1], axis=0)).then_inc(s_asel, 16)
                hold(gp, s_twin, b + 1)
                for k in range(2):
                    gp.tensor_copy(selector[:, k, :], twin[:, k:k + 1].to_broadcast([PT, PT])).then_inc(s_sel, 1)
                with gp.Fori(0, steps) as r:
                    for j in range(STEP):
                        row, k = b * RB + r * STEP + j, j % 2
                        hold(gp, s_bc, row + 1)
                        gp.tensor_copy(selector[:, k, :],
                                       twin[:, ds(r * STEP + j + 2, 1)].to_broadcast([PT, PT])).then_inc(s_sel, 1)
                        hold(gp, s_red, row + 3)
                        gp.tensor_copy(agg_sel[:, ds(r * STEP + j, 1)], row_sum[:, j:j + 1]).then_inc(s_dsum, 1)
                hold(gp, s_sel, b * (RB + 2) + steps * STEP + 2)

            dense_batch(0)
            with gp.If(batches != 1):
                with gp.Fori(1, batches) as b:
                    dense_batch(b)
            gp.memset(keep[:, :], 0.0).then_inc(s_dense, 1)
            gp.wait_ge(s_w2, 64)
            gp.wait_ge(s_xa, 16)
            for q in range(NQ):
                part = x_again[:, TPQ * q:TPQ * q + TPQ, :]
                gp.tensor_tensor(part, part, lnb_rows.rearrange("p (o d) -> p o d", o=1).to_broadcast([PT, TPQ, PT]),
                                 ALU.add).then_inc(s_xb, 1)
            gp.wait_ge(s_aw, 16 * 9)
            gp.tensor_scalar(attw[:, 0:PT], attw[:, 0:PT], -SCALE, None, ALU.mult).then_inc(s_wqs, 1)
            gp.wait_ge(s_agg2p, NQ)
            heads = eye.rearrange("p (h c) -> p h c", h=H)
            for part, blocks in enumerate(((1, 1, 0, 0), (0, 0, 1, 1), (1, 0, 1, 0), (0, 1, 0, 1))):
                target = spread_to[:, H * PT * part:H * PT * (part + 1)].rearrange("p (h r c) -> p h r c", h=H, r=4)
                for block, there in enumerate(blocks):
                    gp.tensor_scalar(target[:, :, block, :], heads, float(there), None, ALU.mult).then_inc(s_rep, 1)
            for t in range(NT):
                gp.wait_ge(s_adj2[t % 2], 16 * (t // 2 + 1))
                gp.tensor_scalar(adj_again[:, t % 2, :], adj_again[:, t % 2, :], 0.0, MASKED,
                                 ALU.is_equal, ALU.mult).then_inc(s_pen, 1)

        @block.tensor
        def _(pe):
            pe.wait_ge(s_const, 1)
            pe.wait_ge(s_w, 48)
            pe.transpose(psum[:, 0, 0:PT], msgw_in[:, 0:PT], eye)
            pe.transpose(psum[:, 0, PT:2 * PT], msgw_in[:, PT:2 * PT], eye).then_inc(s_xtp, 1)
            pe.wait_ge(s_x, 16)
            for q in range(NQ):
                for j in range(TPQ):
                    ins = pe.transpose(psum[:, 1 + q, PT * j:PT * j + PT], x_rows[:, TPQ * q + j, :], eye)
                ins.then_inc(s_xtp, 1)
            for g in range(NT // 2):
                pe.wait_ge(s_xt, 2 + g // 2)
                if g >= 4:
                    pe.wait_ge(s_sdA, g - 3)
                    pe.wait_ge(s_sdV, g - 3)
                for j in range(2):
                    t = 2 * g + j
                    ins = pe.matmul(psum[:, SD_BANKS[g % 4], 256 * j:256 * j + 256], xT[:, PT * t:PT * t + PT], wT,
                                    start=True, stop=True)
                ins.then_inc(s_sdp, 1)
            for q in range(NQ):
                pe.matmul(psum[:, 1 + q, :], wT[:, PT:2 * PT], xT[:, BANK * q:BANK * q + BANK],
                          start=True, stop=True).then_inc(s_dtp, 1)

            def turn_adj(s):
                pe.wait_ge(s_adj[s % 2], 16 * (s // 2 + 1))
                for q in range(NQ):
                    n = NQ * s + q
                    if n >= 2:
                        pe.wait_ge(s_tpc, n - 1)
                    else:
                        pe.wait_ge(s_dt, 4)
                        pe.wait_ge(s_sdA, NT // 2)
                        pe.wait_ge(s_sdV, NT // 2)
                    for j in range(TPQ):
                        m = TPQ * q + j
                        ins = pe.transpose(psum[:, n % 2, PT * j:PT * j + PT],
                                           adj_in[:, s % 2, PT * m:PT * m + PT], eye)
                    ins.then_inc(s_tp, 1)

            def pick_nodes(b):
                hold(pe, s_hot, b + 1)
                for t in range(NT):
                    ins = pe.matmul(psum[:, 6, 0:1], pick_hot[:, t, :], rowid[:, t:t + 1], start=t == 0, stop=t == NT - 1)
                ins.then_inc(s_pickp, 1)

            def pick_s(b):
                for t in range(NT):
                    ins = pe.matmul(psum[:, 7, 0:PT], s_rows[:, t, :], pick_hot[:, t, :], start=t == 0, stop=t == NT - 1)
                ins.then_inc(s_spick, 1)

            def dense_batch(b):
                steps = steps_of(pe, b)
                hold(pe, s_alo, b + 1)
                with pe.Fori(0, steps) as r:
                    for j in range(STEP):
                        row, k = b * RB + r * STEP + j, j % 2
                        hold(pe, s_sel, row + 1 + b * 2)
                        hold(pe, s_red, row + 1)
                        for q in range(NQ):
                            ins = pe.matmul(psum[:, NQ * k + q, :], selector[:, k, :],
                                            adj_parts[:, BANK * q:BANK * q + BANK], start=True, stop=True)
                        ins.then_inc(s_bc, 1)
                hold(pe, s_dsum, b * RB + steps * STEP)
                pe.transpose(psum[:, 2, 0:PT], agg_sel, eye).then_inc(s_dtr, 1)
                for q in range(NQ):
                    for j in range(TPQ):
                        ins = pe.transpose(psum[:, 4 + q, PT * j:PT * j + PT], pick_hot[:, TPQ * q + j, :], eye)
                    ins.then_inc(s_dtr, 1)
                hold(pe, s_dcp, b * 3 + 1)
                for q in range(NQ):
                    if q < 2:
                        hold(pe, s_dcA, b * 2 + q + 1)
                    else:
                        hold(pe, s_dcp, b * 3 + q)
                    pe.matmul(psum[:, q, :], agg_selr, sel_hot[:, TPQ * q:TPQ * q + TPQ, :],
                              start=True, stop=True).then_inc(s_dout, 1)

            unit = 0
            for s in range(NT + 1):
                if s < NT:
                    turn_adj(s)
                if s == 0:
                    continue
                if s == NT:
                    pe.wait_ge(s_counts, 1)
                    batches = pe.value_load(loop_counts[0:1, NB:NB + 1], min_val=1, max_val=NB)
                    pick_nodes(0)
                if s >= 3:
                    pe.wait_ge(s_aggc, s - 2)
                for v, size in enumerate(UNITS[s - 1]):
                    if s == NT - 1 and v == len(UNITS[s - 1]) - 1:
                        pe.wait_ge(s_ext, NT)
                        pe.wait_ge(s_const2, 4)
                        pe.matmul(psum[:, 4, 0:NT], prefix_tri, flags[:, :], start=True, stop=True)
                        pe.matmul(psum[:, 4, NT:2 * NT], ones_sq, flags[:, :], start=True, stop=True).then_inc(s_flagp, 1)
                    pe.wait_ge(s_gelu, unit + 1)
                    pe.wait_ge(s_diag, unit + 1)
                    for j in range(size):
                        k = UNIT * v + j
                        ins = pe.matmul(psum[:, 2 + s % 2, 0:PT], gath[:, unit % RING, j, :], diag[:, unit % 2, j, :],
                                        start=k == 0, stop=k == sum(UNITS[s - 1]) - 1)
                    ins.then_inc(s_unit, 1)
                    unit += 1
            pick_s(0)
            pe.wait_ge(s_aggc, NT)
            pe.wait_ge(s_w2, 64)
            pe.transpose(psum[:, 0, 0:PT], updw_in[:, 0:PT], eye)
            pe.transpose(psum[:, 0, PT:2 * PT], updw_in[:, PT:2 * PT], eye).then_inc(s_utp, 1)
            dense_batch(0)
            with pe.If(batches != 1):
                with pe.Fori(1, batches) as b:
                    pick_nodes(b)
                    pick_s(b)
                    dense_batch(b)
            pe.wait_ge(s_ut, 1)
            for q in range(NQ):
                pe.matmul(psum[:, 4 + q, :], uT[:, 0:PT], xT[:, BANK * q:BANK * q + BANK], start=True, stop=False)
            pe.wait_ge(s_dense, 2)
            for q in range(NQ + 1):
                if q < NQ:
                    part = slice(BANK * q, BANK * q + BANK)
                    pe.matmul(psum[:, 4 + q, :], uT[:, PT:2 * PT], aggT[:, part], start=False, stop=True).then_inc(s_newp, 1)
                if q >= 1:
                    pe.wait_ge(s_newx, q)
                    for j in range(TPQ):
                        t = TPQ * (q - 1) + j
                        ins = pe.transpose(psum[:, q - 1, PT * j:PT * j + PT], newT[:, PT * t:PT * t + PT], eye)
                    ins.then_inc(s_rowp, 1)

            turn = [0]

            def turn_chunk(source):
                n = turn[0]
                if n >= 2:
                    pe.wait_ge(s_tnc, n - 1)
                for j in range(TPQ):
                    ins = pe.transpose(psum[:, 6 + n % 2, PT * j:PT * j + PT], source(j), eye)
                ins.then_inc(s_tnp, 1)
                turn[0] += 1

            def theta_product(k, q):
                for j in range(TPQ):
                    t = TPQ * q + j
                    ins = pe.matmul(psum[:, q, PT * j:PT * j + PT], termT[k][:, PT * t:PT * t + PT], theta_in[:, k, :],
                                    start=k == 0 and j == 0, stop=k == CHEB - 1, skip_group_check=True)
                return ins

            for g in range(NQ):
                pe.wait_ge(s_x1, g + 1)
                turn_chunk(lambda j: x1_rows[:, TPQ * g + j, :])
                for m in range(TPQ * g, TPQ * g + TPQ):
                    ins = pe.matmul(psum[:, 4, :], x1_rows[:, m, :], adjT[:, m, 0:BANK], start=m == 0, stop=m == NT - 1)
            ins.then_inc(s_hopp, 1)
            pe.wait_ge(s_ths, 1)
            for q in range(NQ):
                pe.wait_ge(s_tnc, q + 1)
                theta_product(0, q)

            def finish_chunk(k, q):
                pe.wait_ge(s_hopc, NQ * (k - 1) + q + 1)
                if k < CHEB - 1:
                    turn_chunk(lambda j: termT[k][:, PT * (TPQ * q + j):PT * (TPQ * q + j) + PT])
                ins = theta_product(k, q)
                if k == CHEB - 1:
                    ins.then_inc(s_chp, 1)

            for k in range(1, CHEB):
                for q in range(NQ):
                    n = NQ * (k - 1) + q
                    if n == 0:
                        continue
                    if n >= 2:
                        pe.wait_ge(s_hopc, n - 1)
                    for m in range(NT):
                        if q == 0 and k > 1 and m % TPQ == 0:
                            pe.wait_ge(s_tnc, NQ * (k - 1) + m // TPQ + 1)
                        ins = pe.matmul(psum[:, 4 + n % 2, :], term_rows[k - 1][:, m, :],
                                        adjT[:, m, BANK * q:BANK * q + BANK], start=m == 0, stop=m == NT - 1)
                    ins.then_inc(s_hopp, 1)
                    if q >= 1:
                        finish_chunk(k, q - 1)
                finish_chunk(k, NQ - 1)

            def hop2(q, ms):
                if ms[0] == 0 and q >= 2:
                    pe.wait_ge(s_agg2, q - 1)
                for m in ms:
                    if q == 0 and m % TPQ == 0:
                        pe.wait_ge(s_x2, m // TPQ + 1)
                    ins = pe.matmul(psum[:, 4 + q % 2, :], x2_rows[:, m, :], adjT[:, m, BANK * q:BANK * q + BANK],
                                    start=m == 0, stop=m == NT - 1)
                if ms[-1] == NT - 1:
                    ins.then_inc(s_agg2p, 1)

            def message(q):
                if q == 0:
                    pe.wait_ge(s_gwc, 2)
                    pe.wait_ge(s_tnc, turn[0])
                pe.wait_ge(s_agg2, q + 1)
                if q >= 1:
                    pe.wait_ge(s_msg, q)
                pe.matmul(psum[:, 6, :], gwT[:, 0, :], agg_c, start=True, stop=True).then_inc(s_msgp, 1)

            def gates(q):
                part = x2T[:, BANK * q:BANK * q + BANK]
                if q >= 1:
                    pe.wait_ge(s_pre, q)
                    pe.wait_ge(s_gact, 2 * q)
                for g in range(2):
                    pe.matmul(psum[:, g, :], gwT[:, 4 + g, :], part, start=True, stop=False)
                pe.matmul(psum[:, 3, :], gwT[:, 6, :], part, start=True, stop=True)
                pe.wait_ge(s_msg, q + 1)
                pe.matmul(psum[:, 0, :], gwT[:, 1, :], msg_c, start=False, stop=True).then_inc(s_reset, 1)
                pe.matmul(psum[:, 2, :], gwT[:, 3, :], msg_c, start=True, stop=True)
                pe.matmul(psum[:, 1, :], gwT[:, 2, :], msg_c, start=False, stop=True).then_inc(s_gate, 1)

            def turn_u(q):
                pe.wait_ge(s_cell, q + 1)
                if q >= 1:
                    pe.wait_ge(s_utc, q)
                for j in range(TPQ):
                    ins = pe.transpose(psum[:, 7, PT * j:PT * j + PT], u_c[:, PT * j:PT * j + PT], eye)
                ins.then_inc(s_utn, 1)

            pe.wait_ge(s_hopc, NQ * (CHEB - 1))
            hop2(0, range(0, NT))
            for q in range(NQ):
                turn_chunk(lambda j: x2_rows[:, TPQ * q + j, :])
            pe.wait_ge(s_gwl, 96)
            for g in range(7):
                ins = pe.transpose(psum[:, g // TPQ, PT * (g % TPQ):PT * (g % TPQ) + PT], gw_in[:, g, :], eye)
            ins.then_inc(s_gwp, 1)
            for q in range(1, NQ + 2):
                if q < NQ:
                    hop2(q, range(0, NT // 2))
                if 1 <= q <= NQ:
                    message(q - 1)
                if q < NQ:
                    hop2(q, range(NT // 2, NT))
                if 1 <= q <= NQ:
                    gates(q - 1)
                if q >= 2:
                    turn_u(q - 2)

            for q in range(NQ):
                pe.wait_ge(s_x3A if q % 2 else s_x3, q // 2 + 1)
                turn_chunk(lambda j: x3_rows[:, TPQ * q + j, :])
            pe.wait_ge(s_wqs, 1)
            for i in range(2):
                for q in range(NQ):
                    if i == 0:
                        pe.wait_ge(s_tnc, turn[0] - NQ + q + 1)
                    else:
                        pe.wait_ge(s_lo, q + 1)
                    pe.matmul(psum[:, q, :], attw[:, PT * i:PT * i + PT], x3T[:, BANK * q:BANK * q + BANK],
                              start=True, stop=True).then_inc(s_prp, 1)

            def value_products(g):
                if g >= 2:
                    pe.wait_ge(s_vc, g - 1)
                for j in range(2):
                    t = 2 * g + j
                    ins = pe.matmul(psum[:, 4 + g % 2, 256 * j:256 * j + 256], x3T[:, PT * t:PT * t + PT],
                                    attw[:, 2 * PT:4 * PT], start=True, stop=True)
                ins.then_inc(s_vp, 1)

            value_products(0)
            value_products(1)
            pe.wait_ge(s_rep, 16)
            pe.wait_ge(s_lo, 2 * NQ)
            n = 0
            for i in range(2):
                for h in range(H):
                    for q in range(NQ):
                        if n >= 4:
                            if q == NQ - 1:
                                pe.wait_ge(s_stackV, n // 4)
                            else:
                                pe.wait_ge(s_stackA, 3 * (n // 4 - 1) + q + 1)
                        for low in range(2):
                            part = 2 * i + low
                            at = (H * part + h) * PT
                            ins = pe.matmul(psum[:, q, :], spread_to[:, at:at + PT],
                                            qk_parts[:, part, BANK * q:BANK * q + BANK], start=low == 0, stop=low == 1)
                        ins.then_inc(s_spread, 1)
                        n += 1
                    g = n // 4 + 1
                    if g < NT // 2:
                        value_products(g)

            def scores(i):
                t, h = divmod(i, H)
                for a in range(2):
                    if i >= 1:
                        pe.wait_ge(s_mask, 2 * (i - 1) + a + 1)
                    for j in range(2):
                        ins = pe.matmul(psum[:, 2 * a + j, :], qs[:, h, PT * t:PT * t + PT],
                                        ks[:, h, 1024 * a + BANK * j:1024 * a + BANK * j + BANK], start=True, stop=True)
                    ins.then_inc(s_scp, 1)

            def turn_probs(i):
                pe.wait_ge(s_exp, i + 1)
                for q in range(NQ):
                    n = NQ * i + q
                    if n >= 3:
                        pe.wait_ge(*turned_copy(n - 3))
                    for j in range(TPQ):
                        m = TPQ * q + j
                        ins = pe.transpose(psum[:, 4 + n % 3, PT * j:PT * j + PT], masked[:, i % MASKS, PT * m:PT * m + PT], eye)
                    ins.then_inc(s_etp, 1)

            def values(t, part):
                if part == 0:
                    pe.wait_ge(s_etA, 3 * H * (t + 1))
                    pe.wait_ge(s_etV, H * (t + 1))
                    if t >= 1:
                        pe.wait_ge(s_o, t)
                for m in range(NT * part // 3, NT * (part + 1) // 3):
                    for h in range(H):
                        ins = pe.matmul(psum[C * h:C * h + C, 7, 0:PT], v_rows[:, m, C * h:C * h + C],
                                        turned[(H * t + h) % len(turned)][:, m, :], start=m == 0, stop=m == NT - 1)
                if part == 2:
                    ins.then_inc(s_avp, 1)

            def turn_values(t):
                pe.wait_ge(s_avc, t + 1)
                pe.transpose(psum[:, 7, PT:2 * PT], avT, eye).then_inc(s_avt, 1)

            pe.wait_ge(s_vc, NT // 2)
            pe.wait_ge(s_stackA, 2 * H * (NQ - 1))
            pe.wait_ge(s_stackV, 2 * H)
            steps = NT * H
            for i in range(steps + LAG + 3):
                if i < steps:
                    scores(i)
                ended, part = divmod(i - LAG - H, H)
                if part < 3 and ended >= 0:
                    values(ended, part)
                if LAG <= i < steps + LAG:
                    turn_probs(i - LAG)
                if part == 2 and ended >= 0:
                    turn_values(ended)

        @block.vector
        def _(ve):
            tally = Tally(s_dve)

            def settle(ins):
                ve.wait_ge(s_dve, tally.step(ins))

            def spread(i, source, tiles, ready):
                for t in tiles:
                    ins = ve.bn_stats(stats[i][:, t, :], source[:, t, :])
                settle(ins)
                for t in tiles:
                    ins = ve.bn_aggr(moments[i][:, t, :], stats[i][:, t, :])
                settle(ins)
                if ready:
                    root_of(i, tiles)

            def root_of(i, tiles):
                a, b = tiles[0], tiles[-1] + 1
                ve.tensor_scalar(rstd[i][:, a:b], moments[i][:, a:b, 1], LN_EPS, None, ALU.add).then_inc(s_ln, 1)

            turn = [0]

            def factors(i, tiles):
                a, b = tiles[0], tiles[-1] + 1
                turn[0] += 1
                ve.wait_ge(s_ln2, turn[0])
                settle(ve.reciprocal(rstd[i][:, a:b], rstd[i][:, a:b]))
                ve.scalar_tensor_tensor(shift[i][:, a:b], moments[i][:, a:b, 0], -1.0, rstd[i][:, a:b], ALU.mult,
                                        ALU.mult).then_inc(s_lnr, 1)

            def normalise_rows(i, source, target, tiles, ready):
                for t in tiles:
                    ins = ve.tensor_scalar(target[:, t, :], source[:, t, :], moments[i][:, t, 0:1], rstd[i][:, t:t + 1],
                                           ALU.subtract, ALU.mult)
                ins.then_inc(ready, 1)

            def extract(s, feed):
                t, a, r = ORDER[s], adj_in[:, s % 2, :], s % 3
                slots = sum(UNITS[s])
                scratch = slot(8) if s == 0 else msgs
                here = edge_count[:, s % 2:s % 2 + 1]
                found = edge_count[:, 2 + s % 2:3 + s % 2]
                ve.wait_ge(s_adj[s % 2], 16 * (s // 2 + 1))
                for g in range(NSEG):
                    ins = ve.max(cand_val[:, 8 * g:8 * g + 8], a[:, EDGES[g]:EDGES[g + 1]])
                settle(ins)
                for g in range(NSEG):
                    ins = ve.max_index(cand_pos[:, 8 * g:8 * g + 8], cand_val[:, 8 * g:8 * g + 8],
                                       a[:, EDGES[g]:EDGES[g + 1]])
                settle(ins)
                feed()
                settle(ve.tensor_tensor(cand_left, cand_pos[:, :], seg_base.rearrange("p g e -> p (g e)"), ALU.add))
                settle(ve.scalar_tensor_tensor(cand_key, cand_val, 0.0, cand_left, ALU.is_gt, ALU.mult))
                source = cand_key
                for k in range(0, slots, 8):
                    eight = picked[:, k:k + 8]
                    settle(ve.max(eight, source))
                    if k + 8 < slots:
                        settle(ve.match_replace(cand_left, eight, source, 0.0))
                        source = cand_left
                for k in range(slots):
                    ve.scalar_tensor_tensor(scratch[:, CAND * k:CAND * k + CAND], cand_key, picked[:, k:k + 1],
                                            cand_val, ALU.is_equal, ALU.mult, accum_out=weight[:, r, k:k + 1])
                settle(ve.tensor_scalar(scrap[:, 0:slots], picked[:, 0:slots], 0.0, None, ALU.is_gt, ALU.add,
                                        accum_out=found))
                if s:
                    feed()
                ve.wait_ge(s_count, s + 1)
                ve.tensor_tensor(flags[:, t:t + 1], here, found, ALU.not_equal)
                settle(ve.tensor_tensor(keep[:, :], here, found, ALU.is_equal))
                settle(ve.tensor_scalar(weight[:, r, 0:slots], weight[:, r, 0:slots], keep[:, 0:1], None, ALU.mult))
                ve.tensor_scalar(column[:, r, 0:slots], picked[:, 0:slots], 1.0, 1.0, ALU.max,
                                 ALU.subtract).then_inc(s_ext, 1)

            def d_with_bias():
                ve.wait_ge(s_w, 48)
                for g in range(NT // 2):
                    ve.wait_ge(s_sdA, g + 1)
                    both = psum[:, SD_BANKS[g % 4], :].rearrange("p (j c) -> p j c", j=2)
                    ve.tensor_tensor(d_stage[:, 2 * g:2 * g + 2, :], both[:, :, PT:2 * PT],
                                     msgb_rows.rearrange("p (o d) -> p o d", o=1).to_broadcast([PT, 2, PT]),
                                     ALU.add).then_inc(s_sdV, 1)

            def feed_unit(u, s):
                t = ORDER[s]
                ve.wait_ge(s_gath[u % RING], 16 * sum(SIZES[u % RING:u + 1:RING]))
                rows = gath[:, u % RING, 0:SIZES[u], :]
                ve.tensor_tensor(rows, rows, s_rows[:, t:t + 1, :].to_broadcast([PT, SIZES[u], PT]),
                                 ALU.add).then_inc(s_add, 1)

            unit = [0]

            def feeder(s):
                def feed():
                    feed_unit(unit[0], s)
                    unit[0] += 1
                return feed

            ve.wait_ge(s_const, 4)
            extract(0, d_with_bias)
            ve.wait_ge(s_dtp, 4)
            for s in range(1, NT):
                extract(s, feeder(s - 1))
                for v in range(len(UNITS[s - 1]) - 2):
                    feeder(s - 1)()
            ve.wait_ge(s_flagp, 1)
            settle(ve.tensor_copy(total[:, :], psum[:, 4, 0:2 * NT]))
            settle(ve.tensor_tensor_scan(cum, ones_sq[:, 0:NT], total[:, NT:2 * NT], 0.0, ALU.mult, ALU.add))
            settle(ve.tensor_tensor(pos[:, :], cum, total[:, NT:2 * NT], ALU.subtract))
            settle(ve.tensor_tensor(pos[:, :], pos[:, :], total[:, 0:NT], ALU.add))
            settle(ve.scalar_tensor_tensor(pos[:, :], pos[:, :], 1.0, flags[:, :], ALU.add, ALU.mult))
            settle(ve.tensor_scalar(pos[:, :], pos[:, :], -1.0, None, ALU.add))
            settle(ve.tensor_scalar(left, batch_start[0:1, :], -1.0, cum[0:1, NT - 1:NT], ALU.mult, ALU.add))
            settle(ve.tensor_scalar(more, left, 0.0, None, ALU.is_gt, ALU.add, accum_out=edge_count[0:1, 0:1]))
            ve.tensor_scalar(loop_counts[0:1, NB:NB + 1], edge_count[0:1, 0:1], 1.0, None, ALU.max)
            settle(ve.tensor_scalar(left, left, STEP - 1.0, float(STEP), ALU.add, ALU.max))
            settle(ve.tensor_scalar(loop_counts[0:1, 0:NB], left, RB + STEP - 1.0, None, ALU.min))
            ve.tensor_scalar(loop_counts[0:1, 0:NB], loop_counts[0:1, 0:NB], STEP.bit_length() - 1, None,
                             ALU.arith_shift_right).then_inc(s_counts, 1)
            ve.sem_inc(s_red, 2)
            ve.wait_ge(s_counts, 1)
            flat = psum.rearrange("p b n -> p (b n)")
            batches = ve.value_load(loop_counts[0:1, NB:NB + 1], min_val=1, max_val=NB)

            def pick_rows(b):
                ve.tensor_tensor(pick_hot, pos.rearrange("p (t o) -> p t o", o=1).to_broadcast([PT, NT, PT]),
                                 iota_r.rearrange("p (o r) -> p o r", o=1).to_broadcast([PT, NT, PT]),
                                 ALU.is_equal).then_inc(s_hot, 1)
                hold(ve, s_hot, b + 1)
                ve.tensor_scalar(iota_r[:, :], iota_r[:, :], float(RB), None, ALU.add).then_inc(s_iota, 1)
                hold(ve, s_pickp, b + 1)
                ve.tensor_copy(rows_i[:, :], psum[:, 6, 0:1]).then_inc(s_picki, 1)

            def dense_batch(b):
                steps = steps_of(ve, b)
                hold(ve, s_spick, b + 1)
                ve.tensor_copy(sT_sel, psum[:, 7, 0:PT])
                ve.memset(agg_sel, 0.0)
                ve.tensor_tensor(twin, ident[:, 0:RB + 2], ident[:, RB:2 * RB + 2], ALU.add).then_inc(s_twin, 1)
                hold(ve, s_ahi, b + 1)
                ve.tensor_tensor(adj_parts[RB:PT, :], adj_raw[RB:PT, :], adj_parts[RB:PT, :].bitcast(fp32),
                                 ALU.subtract).then_inc(s_alo, 1)
                with ve.Fori(0, steps) as r:
                    for j in range(STEP):
                        row, k = b * RB + r * STEP + j, j % 2
                        hold(ve, s_mg, row + 1)
                        hold(ve, s_bc, row + 1)
                        ve.tensor_tensor_reduce(dense_msgs[k], dense_msgs[k], flat[:, N * k:N * k + N], 1.0, 0.0,
                                                ALU.mult, ALU.add, row_sum[:, j:j + 1]).then_inc(s_red, 1)
                hold(ve, s_dtr, b * 5 + 1)
                ve.tensor_copy(agg_selr, psum[:, 2, 0:PT]).then_inc(s_dcp, 1)
                for q in range(2, NQ):
                    hold(ve, s_dtr, b * 5 + q + 2)
                    ve.tensor_copy(sel_hot[:, TPQ * q:TPQ * q + TPQ, :], psum[:, 4 + q, :]).then_inc(s_dcp, 1)
                for q in range(NQ):
                    hold(ve, s_dout, b * 4 + q + 1)
                    part = aggT[:, BANK * q:BANK * q + BANK]
                    ve.tensor_tensor(part, part, psum[:, q, :], ALU.add).then_inc(s_dacc, 1)
                hold(ve, s_dacc, b * 4 + 4)
                hold(ve, s_iota, b + 1)

            ve.wait_ge(s_tp, NQ * NT)
            pick_rows(0)
            for v in range(len(UNITS[NT - 1])):
                feeder(NT - 1)()
            ve.wait_ge(s_aggc, NT)
            dense_batch(0)
            with ve.If(batches != 1):
                with ve.Fori(1, batches) as b:
                    pick_rows(b)
                    dense_batch(b)
            ve.memset(edge_count[:, :], 0.0).then_inc(s_dense, 1)
            def add_x(q):
                part = slice(BANK * q, BANK * q + BANK)
                ve.wait_ge(s_newg, q + 1)
                ve.tensor_tensor(newT[:, part], newT[:, part], xT[:, part], ALU.add).then_inc(s_newx, 1)

            def weigh(q):
                part = h_rows[:, TPQ * q:TPQ * q + TPQ, :]
                ve.wait_ge(s_lnn, q + 1)
                settle(ve.tensor_tensor(part, part, lnw_rows.rearrange("p (o d) -> p o d", o=1).to_broadcast([PT, TPQ, PT]),
                                        ALU.mult))
                ve.wait_ge(s_xb, q + 1)
                settle(ve.tensor_tensor(part, part, x_again[:, TPQ * q:TPQ * q + TPQ, :], ALU.add))

            add_x(0)
            add_x(1)
            for q in range(NQ + 1):
                if q < NQ:
                    ve.wait_ge(s_hc, q + 1)
                    spread(0, h_rows, tiles_of(q), True)
                if q + 2 < NQ:
                    add_x(q + 2)
                if q >= 1:
                    weigh(q - 1)
                    spread(1, h_rows, tiles_of(q - 1), True)
                if q < NQ:
                    factors(0, tiles_of(q))
                if q >= 1:
                    factors(1, tiles_of(q - 1))

            ve.wait_ge(s_th, 16)
            for k in range(CHEB):
                ins = ve.tensor_scalar(theta_in[:, k, :], theta_in[:, k, :], cheb_coeff(k), None, ALU.mult)
            ins.then_inc(s_ths, 1)
            for k in range(1, CHEB):
                for q in range(NQ):
                    n = NQ * (k - 1) + q
                    part = slice(BANK * q, BANK * q + BANK)
                    ve.wait_ge(s_hopp, n + 1)
                    if k == 1:
                        ve.tensor_copy(termT[1][:, part], psum[:, 4 + n % 2, :]).then_inc(s_hopc, 1)
                    else:
                        ve.scalar_tensor_tensor(termT[k][:, part], psum[:, 4 + n % 2, :], 2.0, termT[k - 2][:, part],
                                                ALU.mult, ALU.subtract).then_inc(s_hopc, 1)
            for q in range(NQ):
                ve.wait_ge(s_chp, q + 1)
                settle(ve.tensor_tensor(slot(5)[:, BANK * q:BANK * q + BANK], psum[:, q, :],
                                        slot(6)[:, BANK * q:BANK * q + BANK], ALU.add))
                spread(0, y_rows, tiles_of(q), True)
                factors(0, tiles_of(q))

            ve.wait_ge(s_gwl, 96)
            ve.tensor_tensor(brz_cols, bih_cols[:, 0:2], bhh_cols[:, 0:2], ALU.add).then_inc(s_gb, 1)
            for q in range(NQ):
                part = x2T[:, BANK * q:BANK * q + BANK]
                if q >= 2:
                    ve.wait_ge(s_utc, q - 1)
                    spread(1, u_rows, tiles_of(q - 2), False)
                ve.wait_ge(s_gact, 2 * q + 1)
                settle(ve.scalar_tensor_tensor(t_c, psum[:, 3, :], bhh_cols[:, 2:3], r_c, ALU.add, ALU.mult))
                ve.wait_ge(s_gate, q + 1)
                ve.tensor_tensor(t_c, psum[:, 2, :], t_c, ALU.add).then_inc(s_pre, 1)
                ve.wait_ge(s_tanh, q + 1)
                settle(ve.tensor_tensor(t_c, part, n_c, ALU.subtract))
                settle(ve.tensor_tensor(t_c, t_c, z_c, ALU.mult))
                settle(ve.tensor_tensor(t_c, t_c, n_c, ALU.add))
                if q >= 1:
                    ve.wait_ge(s_utn, q)
                ve.tensor_tensor(u_c, t_c, part, ALU.add).then_inc(s_cell, 1)
            for q in range(NQ - 2, NQ):
                ve.wait_ge(s_utc, q + 1)
                spread(1, u_rows, tiles_of(q), False)
            root_of(1, range(NT))
            factors(1, range(NT))
            for q in range(0, NQ, 2):
                normalise_rows(1, u_rows, x3_rows, tiles_of(q), s_x3)

            ve.wait_ge(s_aw, 16 * 9)
            ve.tensor_scalar(qk_cols[:, 0:1], qk_cols[:, 0:1], -SCALE, None, ALU.mult).then_inc(s_bias, 1)
            ve.wait_ge(s_bias, 1)
            for i in range(2):
                for q in range(NQ):
                    ve.wait_ge(s_hi, NQ * i + q + 1)
                    part = slice(BANK * q, BANK * q + BANK)
                    ve.scalar_tensor_tensor(qk_parts[:, 2 * i + 1, part], psum[:, q, :], qk_cols[:, i:i + 1],
                                            qk_parts[:, 2 * i, part].bitcast(fp32), ALU.add, ALU.subtract).then_inc(s_lo, 1)

            def copy_values(g):
                ve.wait_ge(s_vp, g + 1)
                both = psum[:, 4 + g % 2, :].rearrange("p (j c) -> p j c", j=2)
                bias = bvs_rows.rearrange("p (a o d) -> p a o d", a=2, o=1)
                ve.tensor_tensor(v_rows[:, 2 * g:2 * g + 2, :], both[:, :, 0:PT], bias[:, 0].to_broadcast([PT, 2, PT]), ALU.add)
                ve.tensor_tensor(xr_rows[:, 2 * g:2 * g + 2, :], both[:, :, PT:2 * PT],
                                 bias[:, 1].to_broadcast([PT, 2, PT]), ALU.add).then_inc(s_vc, 1)

            copy_values(0)
            copy_values(1)
            for n in range(2 * H):
                i, h = divmod(n, H)
                ve.wait_ge(s_spread, NQ * n + NQ)
                ve.tensor_copy((ks if i else qs)[:, h, BANK * (NQ - 1):BANK * NQ], psum[:, NQ - 1, :]).then_inc(s_stackV, 1)
                if n + 2 < NT // 2:
                    copy_values(n + 2)
            ve.wait_ge(s_vc, NT // 2)
            ve.tensor_tensor(wb_out, wb_rows[:, 0:PT], wb_rows[:, 2 * PT:3 * PT], ALU.add)
            settle(ve.tensor_tensor(wb_skip, wb_rows[:, PT:2 * PT], wb_rows[:, 2 * PT:3 * PT], ALU.subtract))

            def mask_and_min(i):
                t, h = divmod(i, H)
                if h == 0:
                    ve.wait_ge(s_pen, t + 1)
                if i >= MASKS:
                    ve.wait_ge(s_etp, NQ * (i - MASKS + 1))
                for a in range(2):
                    ve.wait_ge(s_scp, 2 * i + a + 1)
                    ve.tensor_tensor_reduce(masked[:, i % MASKS, 1024 * a:1024 * a + 1024], flat[:, 1024 * a:1024 * a + 1024],
                                            adj_again[:, t % 2, 1024 * a:1024 * a + 1024], 1.0,
                                            row_min[:, i % 4, 0:1] if a else CEILING, ALU.add, ALU.min,
                                            row_min[:, i % 4, a:a + 1]).then_inc(s_mask, 1)
                    if a == 0:
                        ve.wait_ge(s_mask, 2 * i + 1)

            def copy_turned(i):
                if turned_free(i) >= 0:
                    ve.wait_ge(s_avp, turned_free(i) + 1)
                for n in range(NQ * i, NQ * i + NQ):
                    q = n % NQ
                    if turned_copy(n)[0] is s_etV:
                        ve.wait_ge(s_etp, n + 1)
                        ve.tensor_copy(turned[i % len(turned)][:, TPQ * q:TPQ * q + TPQ, :],
                                       psum[:, 4 + n % 3, :]).then_inc(s_etV, 1)

            def prepare_gate(t):
                ve.wait_ge(s_exp, H * (t + 1))
                settle(ve.scalar_tensor_tensor(rden[:, t % 2, :], den[:, t, :], 0.0, den[:, t, :], ALU.is_equal, ALU.add))
                ve.reciprocal(rden[:, t % 2, :], rden[:, t % 2, :])
                settle(ve.tensor_tensor_reduce(o_rows[:, t, :], xr_rows[:, t, :], wb_skip, 1.0, 0.0, ALU.mult, ALU.add,
                                               skip_dot[:, t:t + 1]))

            def normalise(t):
                ve.wait_ge(s_avt, t + 1)
                ve.tensor_tensor(o_rows[:, t, :].rearrange("p (c h) -> p h c", h=H),
                                 psum[:, 7, PT:2 * PT].rearrange("p (h c) -> p h c", h=H),
                                 rden[:, t % 2, :].rearrange("p (h o) -> p h o", o=1).to_broadcast([PT, H, C]),
                                 ALU.mult).then_inc(s_o, 1)

            def gate_dot(t):
                ve.wait_ge(s_o, t + 1)
                ve.tensor_tensor_reduce(gate_scrap, o_rows[:, t, :], wb_out, 1.0, skip_dot[:, t:t + 1], ALU.mult, ALU.add,
                                        gate[:, t % 2, 0:1]).then_inc(s_gz, 1)

            def mix(t):
                ve.wait_ge(s_ge, t + 1)
                settle(ve.tensor_scalar(gate[:, t % 2, 2:3], gate[:, t % 2, 1:2], 1.0, None, ALU.add))
                ve.reciprocal(gate[:, t % 2, 3:4], gate[:, t % 2, 2:3])
                settle(ve.tensor_tensor(gate_scrap, xr_rows[:, t, :], o_rows[:, t, :], ALU.subtract))
                settle(ve.scalar_tensor_tensor(o_rows[:, t, :], gate_scrap, gate[:, t % 2, 3:4], o_rows[:, t, :],
                                               ALU.mult, ALU.add))
                settle(ve.tensor_tensor(o_rows[:, t, :], o_rows[:, t, :], x3_rows[:, t, :], ALU.add))
                spread(0, o_rows, [t], False)

            steps = NT * H
            for i in range(steps + LAG + 6):
                for late, step in ((7, normalise), (8, gate_dot)):
                    ended, h = divmod(i - LAG - late, H)
                    if h == 0 and 0 <= ended < NT:
                        step(ended)
                if i < steps:
                    mask_and_min(i)
                if LAG <= i < steps + LAG:
                    copy_turned(i - LAG)
                for late, step in ((6, prepare_gate), (9, mix)):
                    ended, h = divmod(i - LAG - late, H)
                    if h == 0 and 0 <= ended < NT:
                        step(ended)
            root_of(0, range(NT))
            factors(0, range(NT))
            for q in range(0, NQ, 2):
                normalise_rows(0, o_rows, o_rows, tiles_of(q), s_fin)

        @block.scalar
        def _(ac):
            roots, shifts = [0], [0]

            def square_root(i, tiles):
                a, b = tiles[0], tiles[-1] + 1
                roots[0] += 1
                ac.wait_ge(s_ln, roots[0])
                ac.activation(rstd[i][:, a:b], rstd[i][:, a:b], ACT.Sqrt).then_inc(s_ln2, 1)

            def wait_factors():
                shifts[0] += 1
                ac.wait_ge(s_lnr, shifts[0])

            def normalise_rows(i, source, target, tiles, ready):
                for t in tiles:
                    ins = ac.activation(target[:, t, :], source[:, t, :], ACT.Identity, bias=shift[i][:, t:t + 1],
                                        scale=rstd[i][:, t:t + 1])
                ins.then_inc(ready, 1)

            ac.wait_ge(s_xtp, 1)
            ac.activation(wT, psum[:, 0, 0:2 * PT], ACT.Copy).then_inc(s_xt, 1)
            for q in range(NQ):
                ac.wait_ge(s_xtp, q + 2)
                ac.activation(xT[:, BANK * q:BANK * q + BANK], psum[:, 1 + q, :], ACT.Copy).then_inc(s_xt, 1)
            for g in range(NT // 2):
                ac.wait_ge(s_sdp, g + 1)
                both = psum[:, SD_BANKS[g % 4], :].rearrange("p (j c) -> p j c", j=2)
                ac.activation(s_rows[:, 2 * g:2 * g + 2, :], both[:, :, 0:PT], ACT.Copy).then_inc(s_sdA, 1)

            counted = adjT[:, :, PT * ORDER[NT - 1]:PT * ORDER[NT - 1] + PT]

            def count_nonzeros(s):
                ac.wait_ge(s_adj[s % 2], 16 * (s // 2 + 1))
                if s:
                    ac.wait_ge(s_count, s)
                ac.activation(counted, as_rows(adj_in[:, s % 2, :]), ACT.Sign).then_inc(s_act, 1)
                ac.wait_ge(s_act, s + 1)
                ac.activation(counted, counted, ACT.Square, accum_out=edge_count[:, s % 2:s % 2 + 1]).then_inc(s_count, 1)

            count_nonzeros(0)
            ac.wait_ge(s_w, 48)
            for q in range(NQ):
                ac.wait_ge(s_dtp, q + 1)
                ac.activation(dT[:, BANK * q:BANK * q + BANK], psum[:, 1 + q, :], ACT.Identity,
                              bias=msgb_col).then_inc(s_dt, 1)
            unit = 0
            for s in range(NT + 1):
                if s < NT:
                    t = ORDER[s]
                    if s:
                        count_nonzeros(s)
                    for q in range(NQ):
                        n = NQ * s + q
                        if s == NT - 1:
                            ac.wait_ge(s_count, NT)
                        ac.wait_ge(s_tp, n + 1)
                        ac.activation(adjT[:, TPQ * q:TPQ * q + TPQ, PT * t:PT * t + PT], psum[:, n % 2, :],
                                      ACT.Copy).then_inc(s_tpc, 1)
                if s == 0:
                    continue
                for v, size in enumerate(UNITS[s - 1]):
                    if v == 0:
                        ac.wait_ge(s_ext, s)
                    if unit >= 2:
                        ac.wait_ge(s_unit, unit - 1)
                    for j in range(size):
                        k = UNIT * v + j
                        ins = ac.activation(diag[:, unit % 2, j, :], eye, ACT.Copy, scale=weight[:, (s - 1) % 3, k:k + 1])
                    ins.then_inc(s_diag, 1)
                    ac.wait_ge(s_add, unit + 1)
                    ac.activation(gath[:, unit % RING, 0:size, :], gath[:, unit % RING, 0:size, :],
                                  ACT.Gelu).then_inc(s_gelu, 1)
                    unit += 1
                t = ORDER[s - 1]
                ac.wait_ge(s_unit, unit)
                ac.activation(aggT[:, PT * t:PT * t + PT], psum[:, 2 + s % 2, 0:PT], ACT.Copy).then_inc(s_aggc, 1)
            ac.wait_ge(s_counts, 1)
            batches = ac.value_load(loop_counts[0:1, NB:NB + 1], min_val=1, max_val=NB)

            ac.wait_ge(s_utp, 1)
            ac.activation(uT, psum[:, 0, 0:2 * PT], ACT.Copy).then_inc(s_ut, 1)

            def dense_batch(b):
                steps = steps_of(ac, b)
                hold(ac, s_asel, b * 16 + 16)
                ac.activation(adj_parts[:, :], adj_raw, ACT.Copy).then_inc(s_ahi, 1)
                hold(ac, s_alo, b + 1)
                with ac.Fori(0, steps) as r:
                    for j in range(STEP):
                        row, k = b * RB + r * STEP + j, j % 2
                        hold(ac, s_red, row + 1)
                        ac.activation(dense_msgs[k], dT, ACT.Gelu, bias=sT_sel[:, ds(r * STEP + j, 1)]).then_inc(s_mg, 1)
                for q in range(2):
                    hold(ac, s_dtr, b * 5 + q + 2)
                    ac.activation(sel_hot[:, TPQ * q:TPQ * q + TPQ, :], psum[:, 4 + q, :], ACT.Copy).then_inc(s_dcA, 1)

            dense_batch(0)
            with ac.If(batches != 1):
                with ac.Fori(1, batches) as b:
                    dense_batch(b)
            turn = [0]

            def copy_turned(target):
                n = turn[0]
                ac.wait_ge(s_tnp, n + 1)
                ac.activation(target, psum[:, 6 + n % 2, :], ACT.Copy).then_inc(s_tnc, 1)
                turn[0] += 1

            def copy_h(q):
                ac.wait_ge(s_rowp, q + 1)
                ac.activation(slot(2)[:, BANK * q:BANK * q + BANK], psum[:, q, :], ACT.Copy).then_inc(s_hc, 1)

            for q in range(NQ):
                ac.wait_ge(s_newp, q + 1)
                ac.activation(newT[:, BANK * q:BANK * q + BANK], psum[:, 4 + q, :], ACT.Gelu,
                              bias=updb_col).then_inc(s_newg, 1)
                if q >= 2:
                    copy_h(q - 2)
            for q in range(NQ + 1):
                if q < NQ:
                    square_root(0, tiles_of(q))
                if q + 2 < NQ:
                    copy_h(q + 2)
                if q >= 1:
                    square_root(1, tiles_of(q - 1))
                if q < NQ:
                    wait_factors()
                    normalise_rows(0, h_rows, h_rows, tiles_of(q), s_lnn)
                if q >= 1:
                    wait_factors()
                    normalise_rows(1, h_rows, x1_rows, tiles_of(q - 1), s_x1)
                if q >= 2:
                    copy_turned(slot(0)[:, BANK * (q - 2):BANK * (q - 1)])
            copy_turned(slot(0)[:, BANK * (NQ - 1):BANK * NQ])

            for k in range(1, CHEB - 1):
                for q in range(NQ):
                    copy_turned(term_rows[k][:, TPQ * q:TPQ * q + TPQ, :])
            for q in range(NQ):
                square_root(0, tiles_of(q))
                wait_factors()
                normalise_rows(0, y_rows, x2_rows, tiles_of(q), s_x2)

            for q in range(NQ):
                copy_turned(slot(0)[:, BANK * q:BANK * q + BANK])
            ac.wait_ge(s_gwp, 1)
            ac.activation(gwT[:, 0:4, :], psum[:, 0, :], ACT.Copy).then_inc(s_gwc, 1)
            ac.activation(gwT[:, 4:7, :], psum[:, 1, 0:3 * PT], ACT.Copy).then_inc(s_gwc, 1)
            ac.wait_ge(s_gb, 1)
            for q in range(NQ + 2):
                if 1 <= q <= NQ:
                    ac.wait_ge(s_msgp, q)
                    if q >= 2:
                        ac.wait_ge(s_gate, q - 1)
                    ac.activation(msg_c, psum[:, 6, :], ACT.Relu, bias=bmsg_col).then_inc(s_msg, 1)
                if q >= 2:
                    ac.wait_ge(s_utn, q - 1)
                    ac.activation(slot(3)[:, BANK * (q - 2):BANK * (q - 1)], psum[:, 7, :], ACT.Copy).then_inc(s_utc, 1)
                if q < NQ:
                    ac.wait_ge(s_agg2p, q + 1)
                    if q >= 1:
                        ac.wait_ge(s_msgp, q)
                    ac.activation(agg_c, psum[:, 4 + q % 2, :], ACT.Copy).then_inc(s_agg2, 1)
                if 1 <= q <= NQ:
                    ac.wait_ge(s_reset, q)
                    if q >= 2:
                        ac.wait_ge(s_cell, q - 1)
                    ac.activation(r_c, psum[:, 0, :], ACT.Sigmoid, bias=brz_cols[:, 0:1]).then_inc(s_gact, 1)
                    ac.wait_ge(s_gate, q)
                    ac.activation(z_c, psum[:, 1, :], ACT.Sigmoid, bias=brz_cols[:, 1:2]).then_inc(s_gact, 1)
                    ac.wait_ge(s_pre, q)
                    ac.activation(n_c, t_c, ACT.Tanh, bias=bih_cols[:, 2:3]).then_inc(s_tanh, 1)
            square_root(1, range(NT))
            wait_factors()
            for q in range(1, NQ, 2):
                normalise_rows(1, u_rows, x3_rows, tiles_of(q), s_x3A)

            for q in range(NQ):
                copy_turned(slot(0)[:, BANK * q:BANK * q + BANK])
            ac.wait_ge(s_bias, 1)
            for i in range(2):
                for q in range(NQ):
                    ac.wait_ge(s_prp, NQ * i + q + 1)
                    ac.activation(qk_parts[:, 2 * i, BANK * q:BANK * q + BANK], psum[:, q, :], ACT.Identity,
                                  bias=qk_cols[:, i:i + 1]).then_inc(s_hi, 1)
            for n in range(2 * H):
                i, h = divmod(n, H)
                for q in range(NQ - 1):
                    ac.wait_ge(s_spread, NQ * n + q + 1)
                    ac.activation((ks if i else qs)[:, h, BANK * q:BANK * q + BANK], psum[:, q, :], ACT.Copy).then_inc(s_stackA, 1)
            steps = NT * H
            for i in range(steps + LAG + 6):
                t, h = divmod(i, H)
                ended, part = divmod(i - LAG - 6, H)
                if part == 0 and 0 <= ended < NT:
                    ac.wait_ge(s_avp, ended + 1)
                    if ended >= 1:
                        ac.wait_ge(s_avt, ended)
                    ac.activation(avT, psum[:, 7, 0:PT], ACT.Copy).then_inc(s_avc, 1)
                if LAG <= i < steps + LAG:
                    j = i - LAG
                    if turned_free(j) >= 0:
                        ac.wait_ge(s_avp, turned_free(j) + 1)
                    for n in range(NQ * j, NQ * j + NQ):
                        q = n % NQ
                        if turned_copy(n)[0] is s_etA:
                            ac.wait_ge(s_etp, n + 1)
                            ac.activation(turned[j % len(turned)][:, TPQ * q:TPQ * q + TPQ, :], psum[:, 4 + n % 3, :],
                                          ACT.Copy).then_inc(s_etA, 1)
                if i < steps:
                    ac.wait_ge(s_mask, 2 * i + 2)
                    ac.activation(masked[:, i % MASKS, :], masked[:, i % MASKS, :], ACT.Exp, scale=-1.0,
                                  bias=row_min[:, i % 4, 1:2], accum_out=den[:, t, h:h + 1]).then_inc(s_exp, 1)
                ended, part = divmod(i - LAG - 8, H)
                if part == 0 and 0 <= ended < NT:
                    ac.wait_ge(s_gz, ended + 1)
                    ac.activation(gate[:, ended % 2, 1:2], gate[:, ended % 2, 0:1], ACT.Exp, scale=-1.0).then_inc(s_ge, 1)
            square_root(0, range(NT))
            wait_factors()
            for q in range(1, NQ, 2):
                normalise_rows(0, o_rows, o_rows, tiles_of(q), s_finA)


_INS = ['x', 'adj', 'L0_gnn_msg_w', 'L0_gnn_msg_b', 'L0_gnn_upd_w', 'L0_gnn_upd_b', 'L0_gnn_ln_w', 'L0_gnn_ln_b',
        'L1_gnn_theta', 'L2_gnn_W_msg', 'L2_gnn_b_msg', 'L2_gnn_W_ih', 'L2_gnn_W_hh', 'L2_gnn_b_ih', 'L2_gnn_b_hh',
        'L3_gnn_Wq', 'L3_gnn_bq', 'L3_gnn_Wk', 'L3_gnn_bk', 'L3_gnn_Wv', 'L3_gnn_bv', 'L3_gnn_Ws', 'L3_gnn_bs',
        'L3_gnn_Wb']


def kernel(**inputs):
    import numpy as _np
    import concourse.bacc as _bacc
    from concourse import mybir as _mybir
    from concourse.bass_utils import run_bass_kernel_spmd as _run

    nc = _bacc.Bacc("TRN2", target_bir_lowering=False, num_devices=1)
    arrays, args = {}, []
    for name in _INS:
        a = _np.ascontiguousarray(inputs[name])
        arrays[f"in_{name}_dram"] = a
        args.append(nc.dram_tensor(f"in_{name}_dram", a.shape, _mybir.dt.from_np(a.dtype), kind="ExternalInput").ap())
    args.append(nc.dram_tensor("out_0_dram", (N, D), _mybir.dt.float32, kind="ExternalOutput").ap())
    args.append(nc.dram_tensor("d_rows_dram", (N, D), _mybir.dt.float32).ap())
    graph_network(nc, *args)
    r = _run(nc, [arrays], core_ids=[0])
    return r.results[0]["out_0_dram"]
```
